# Optimizing a Trainium2 kernel written in Bass

```python
import numpy as np
import jax
import jax.numpy as jnp

def _softmax(x, axis=-1):
    return jax.nn.softmax(x, axis=axis)

def _gelu(x):
    return jax.nn.gelu(x, approximate=True)

def _silu(x):
    return jax.nn.silu(x)

def _sigmoid(x):
    return jax.nn.sigmoid(x)

def _layernorm(x, axis=-1, eps=1e-05):
    m = jnp.mean(x, axis=axis, keepdims=True)
    v = jnp.var(x, axis=axis, keepdims=True)
    return (x - m) / jnp.sqrt(v + eps)

def _scatter_add(tgt, idx, src, axis=0):
    return tgt.at[idx].add(src)

def _segment_sum(src, seg, n):
    return jax.ops.segment_sum(src, seg, n)
kernel_name = 'mk_gps_d2_gnn_r8_0347dc'

def setup_inputs(seed: int=0):
    np.random.seed(seed)
    _w = jnp.asarray

    def _rec_inputs():
        import jax
        import jax.numpy as jnp
        _gk = jax.random.key(seed)
        x = -0.0003019 + 1 * jax.random.normal(jax.random.fold_in(_gk, 1), (1250, 512), jnp.float32)
        _s = jax.random.randint(jax.random.fold_in(_gk, 2), (20000,), 0, 1250, jnp.int32)
        _d = jax.random.randint(jax.random.fold_in(_gk, 3), (20000,), 0, 1250, jnp.int32)
        _loop = jnp.arange(1250, dtype=jnp.int32)
        src = jnp.concatenate([_s, _d, _loop])
        dst = jnp.concatenate([_d, _s, _loop])
        _o = jnp.argsort(dst, stable=True)
        src = src[_o]
        dst = dst[_o]
        edge_attr_512 = -8.513e-05 + 0.999844 * jax.random.normal(jax.random.fold_in(_gk, 11), (41250, 512), jnp.float32)
        return (x, src, dst, edge_attr_512)
    x, src, dst, edge_attr_512 = _rec_inputs()

    def _L0_gnn_setup():
        import jax, jax.numpy as jnp
        import numpy as np
        N_NODES = 5000
        N_EDGES = 80000
        DIM_H = 512
        N_HEADS = 8
        D_HEAD = DIM_H // N_HEADS

        def _exphormer_attn(x, edge_index, Wq, Wk, Wv):
            N, D = x.shape
            H, d = (N_HEADS, D_HEAD)
            Q = (x @ Wq).reshape(N, H, d)
            K = (x @ Wk).reshape(N, H, d)
            V = (x @ Wv).reshape(N, H, d)
            src, dst = (edge_index[0], edge_index[1])
            scale = np.float32(1.0 / np.sqrt(d))
            score = jnp.einsum('ehd,ehd->eh', K[src], Q[dst]) * scale
            score = jnp.exp(jnp.clip(score, -5.0, 5.0))[..., None]
            msg = V[src] * score
            wV = jax.ops.segment_sum(msg, dst, num_segments=N)
            Z = jax.ops.segment_sum(score, dst, num_segments=N)
            return (wV / (Z + 1e-06)).reshape(N, D)
        key = jax.random.key(seed)
        ks = jax.random.split(key, 8)
        x = jax.random.normal(ks[0], (N_NODES, DIM_H), dtype=jnp.float32)
        edge_index = jax.random.randint(ks[1], (2, N_EDGES), 0, N_NODES, dtype=jnp.int32)
        virt_h = jax.random.normal(ks[2], (1, DIM_H), dtype=jnp.float32)
        virt_edge_index = jnp.zeros((2, 1), dtype=jnp.int32)
        s = 1.0 / np.sqrt(DIM_H)
        Wq = jax.random.normal(ks[3], (DIM_H, DIM_H), dtype=jnp.float32) * s
        Wk = jax.random.normal(ks[4], (DIM_H, DIM_H), dtype=jnp.float32) * s
        Wv = jax.random.normal(ks[5], (DIM_H, DIM_H), dtype=jnp.float32) * s
        bn_gamma = jnp.ones((DIM_H,), dtype=jnp.float32)
        bn_beta = jnp.zeros((DIM_H,), dtype=jnp.float32)
        return {'x': x, 'edge_index': edge_index, 'virt_h': virt_h, 'virt_edge_index': virt_edge_index, 'Wq': Wq, 'Wk': Wk, 'Wv': Wv, 'bn_gamma': bn_gamma, 'bn_beta': bn_beta}
    _L0_gnn_all = _L0_gnn_setup()
    _L0_gnn_in = {k: v for k, v in _L0_gnn_all.items() if k in ('virt_h', 'virt_edge_index', 'Wq', 'Wk', 'Wv', 'bn_gamma', 'bn_beta')}
    del _L0_gnn_all

    def _L0_mix_setup():
        import jax, jax.numpy as jnp
        import numpy as np
        DIM = 512
        HEADS = 8
        DIM_HEAD = 64
        INNER = HEADS * DIM_HEAD
        key = jax.random.key(seed)
        k1, k2, k3, k4 = jax.random.split(key, 4)
        x = jax.random.normal(k1, (4, 1024, DIM), dtype=jnp.float32)
        w_qkv = jax.random.normal(k2, (DIM, 3 * INNER), dtype=jnp.float32) / np.sqrt(DIM)
        w_out = jax.random.normal(k3, (INNER, DIM), dtype=jnp.float32) / np.sqrt(INNER)
        b_out = jax.random.normal(k4, (DIM,), dtype=jnp.float32) * 0.01
        return {'x': x, 'w_qkv': w_qkv, 'w_out': w_out, 'b_out': b_out}
    _L0_mix_all = _L0_mix_setup()
    _L0_mix_in = {k: v for k, v in _L0_mix_all.items() if k in ('w_qkv', 'w_out', 'b_out')}
    del _L0_mix_all

    def _L0_ffn_setup():
        import jax, jax.numpy as jnp
        import numpy as np
        B, S, H, E, K, DF, SH = (8, 512, 512, 8, 2, 128, 512)
        key = jax.random.key(seed)
        ks = jax.random.split(key, 10)
        n = lambda i, shape, sc: jax.random.normal(ks[i], shape, jnp.float32) * sc
        return {'hidden_states': n(0, (B, S, H), 1.0), 'gate_w': n(1, (E, H), 0.05), 'w1': n(2, (E, H, DF), 0.05), 'b1': n(3, (E, DF), 0.01), 'w2': n(4, (E, DF, H), 0.05), 'b2': n(5, (E, H), 0.01), 'sw1': n(6, (H, SH), 0.05), 'sb1': n(7, (SH,), 0.01), 'sw2': n(8, (SH, H), 0.05), 'sb2': n(9, (H,), 0.01)}
    _L0_ffn_all = _L0_ffn_setup()
    _L0_ffn_in = {k: v for k, v in _L0_ffn_all.items() if k in ('gate_w', 'w1', 'b1', 'w2', 'b2', 'sw1', 'sb1', 'sw2', 'sb2')}
    del _L0_ffn_all

    def _L1_gnn_setup():
        import jax, jax.numpy as jnp
        import numpy as np
        N = 1250
        E = 20000
        D = 512
        key = jax.random.key(seed)
        k1, k2, k3, k4, k5 = jax.random.split(key, 5)
        node_tokens = jax.random.normal(k1, (N, D), dtype=jnp.float32)
        relation_tokens = jax.random.normal(k2, (E, D), dtype=jnp.float32)
        edge_index = jax.random.randint(k3, (2, E), 0, N, dtype=jnp.int64)
        lim_m = float(np.sqrt(6.0 / (D + D)))
        Wm = jax.random.uniform(k4, (D, D), minval=-lim_m, maxval=lim_m, dtype=jnp.float32)
        bm = jnp.zeros((D,), dtype=jnp.float32)
        lim_u = float(np.sqrt(6.0 / (2 * D + D)))
        Wu = jax.random.uniform(k5, (D, 2 * D), minval=-lim_u, maxval=lim_u, dtype=jnp.float32)
        bu = jnp.zeros((D,), dtype=jnp.float32)
        gamma = jnp.ones((D,), dtype=jnp.float32)
        beta = jnp.zeros((D,), dtype=jnp.float32)
        return {'node_tokens': node_tokens, 'relation_tokens': relation_tokens, 'edge_index': edge_index, 'num_nodes': N, 'Wm': Wm, 'bm': bm, 'Wu': Wu, 'bu': bu, 'gamma': gamma, 'beta': beta}
    _L1_gnn_all = _L1_gnn_setup()
    _L1_gnn_in = {k: v for k, v in _L1_gnn_all.items() if k in ('Wm', 'bm', 'Wu', 'bu', 'gamma', 'beta')}
    del _L1_gnn_all

    def _L1_mix_setup():
        import jax, jax.numpy as jnp
        import numpy as np
        HEADS = 8
        EPS_LN = 1e-05
        EPS_NORM = 1e-08
        key = jax.random.key(seed)
        ks = jax.random.split(key, 3)
        B, N, C = (4, 1024, 512)
        x = jax.random.normal(ks[0], (B, N, C), dtype=jnp.float32)
        qkv_w = jax.random.normal(ks[1], (3 * C, C), dtype=jnp.float32) / np.sqrt(C)
        qkv_b = jnp.zeros((3 * C,), dtype=jnp.float32)
        out_w = jax.random.normal(ks[2], (C, C), dtype=jnp.float32) / np.sqrt(C)
        out_b = jnp.zeros((C,), dtype=jnp.float32)
        ln_gamma = jnp.ones((C,), dtype=jnp.float32)
        ln_beta = jnp.zeros((C,), dtype=jnp.float32)
        return {'x': x, 'qkv_w': qkv_w, 'qkv_b': qkv_b, 'out_w': out_w, 'out_b': out_b, 'ln_gamma': ln_gamma, 'ln_beta': ln_beta}
    _L1_mix_all = _L1_mix_setup()
    _L1_mix_in = {k: v for k, v in _L1_mix_all.items() if k in ('qkv_w', 'qkv_b', 'out_w', 'out_b', 'ln_gamma', 'ln_beta')}
    del _L1_mix_all

    def _L1_ffn_setup():
        import jax, jax.numpy as jnp
        import numpy as np
        B, S, D = (32, 512, 512)
        E, H, O, K = (8, 256, 512, 2)
        key = jax.random.key(seed)
        ks = jax.random.split(key, 5)
        sc = lambda k, shape, scale: jax.random.normal(k, shape, jnp.float32) * scale
        return {'x': sc(ks[0], (B, S, D), 1.0), 'attn_w': sc(ks[1], (D, 1), 0.05), 'attn_b': jnp.zeros((1,), jnp.float32), 'gate_w': sc(ks[2], (D, E), 0.05), 'gate_b': jnp.zeros((E,), jnp.float32), 'w1': sc(ks[3], (E, D, H), 0.02), 'b1': jnp.zeros((E, H), jnp.float32), 'w2': sc(ks[4], (E, H, O), 0.02), 'b2': jnp.zeros((E, O), jnp.float32)}
    _L1_ffn_all = _L1_ffn_setup()
    _L1_ffn_in = {k: v for k, v in _L1_ffn_all.items() if k in ('attn_w', 'attn_b', 'gate_w', 'gate_b', 'w1', 'b1', 'w2', 'b2')}
    del _L1_ffn_all
    return {'x': x, 'src': src, 'dst': dst, 'edge_attr_512': edge_attr_512, 'L0_gnn_virt_h': _L0_gnn_in['virt_h'], 'L0_gnn_virt_edge_index': _L0_gnn_in['virt_edge_index'], 'L0_gnn_Wq': _L0_gnn_in['Wq'], 'L0_gnn_Wk': _L0_gnn_in['Wk'], 'L0_gnn_Wv': _L0_gnn_in['Wv'], 'L0_gnn_bn_gamma': _L0_gnn_in['bn_gamma'], 'L0_gnn_bn_beta': _L0_gnn_in['bn_beta'], 'L0_mix_w_qkv': _L0_mix_in['w_qkv'], 'L0_mix_w_out': _L0_mix_in['w_out'], 'L0_mix_b_out': _L0_mix_in['b_out'], 'L0_ffn_gate_w': _L0_ffn_in['gate_w'], 'L0_ffn_w1': _L0_ffn_in['w1'], 'L0_ffn_b1': _L0_ffn_in['b1'], 'L0_ffn_w2': _L0_ffn_in['w2'], 'L0_ffn_b2': _L0_ffn_in['b2'], 'L0_ffn_sw1': _L0_ffn_in['sw1'], 'L0_ffn_sb1': _L0_ffn_in['sb1'], 'L0_ffn_sw2': _L0_ffn_in['sw2'], 'L0_ffn_sb2': _L0_ffn_in['sb2'], 'L1_gnn_Wm': _L1_gnn_in['Wm'], 'L1_gnn_bm': _L1_gnn_in['bm'], 'L1_gnn_Wu': _L1_gnn_in['Wu'], 'L1_gnn_bu': _L1_gnn_in['bu'], 'L1_gnn_gamma': _L1_gnn_in['gamma'], 'L1_gnn_beta': _L1_gnn_in['beta'], 'L1_mix_qkv_w': _L1_mix_in['qkv_w'], 'L1_mix_qkv_b': _L1_mix_in['qkv_b'], 'L1_mix_out_w': _L1_mix_in['out_w'], 'L1_mix_out_b': _L1_mix_in['out_b'], 'L1_mix_ln_gamma': _L1_mix_in['ln_gamma'], 'L1_mix_ln_beta': _L1_mix_in['ln_beta'], 'L1_ffn_attn_w': _L1_ffn_in['attn_w'], 'L1_ffn_attn_b': _L1_ffn_in['attn_b'], 'L1_ffn_gate_w': _L1_ffn_in['gate_w'], 'L1_ffn_gate_b': _L1_ffn_in['gate_b'], 'L1_ffn_w1': _L1_ffn_in['w1'], 'L1_ffn_b1': _L1_ffn_in['b1'], 'L1_ffn_w2': _L1_ffn_in['w2'], 'L1_ffn_b2': _L1_ffn_in['b2']}

def reference(x, src, dst, edge_attr_512, L0_gnn_virt_h, L0_gnn_virt_edge_index, L0_gnn_Wq, L0_gnn_Wk, L0_gnn_Wv, L0_gnn_bn_gamma, L0_gnn_bn_beta, L0_mix_w_qkv, L0_mix_w_out, L0_mix_b_out, L0_ffn_gate_w, L0_ffn_w1, L0_ffn_b1, L0_ffn_w2, L0_ffn_b2, L0_ffn_sw1, L0_ffn_sb1, L0_ffn_sw2, L0_ffn_sb2, L1_gnn_Wm, L1_gnn_bm, L1_gnn_Wu, L1_gnn_bu, L1_gnn_gamma, L1_gnn_beta, L1_mix_qkv_w, L1_mix_qkv_b, L1_mix_out_w, L1_mix_out_b, L1_mix_ln_gamma, L1_mix_ln_beta, L1_ffn_attn_w, L1_ffn_attn_b, L1_ffn_gate_w, L1_ffn_gate_b, L1_ffn_w1, L1_ffn_b1, L1_ffn_w2, L1_ffn_b2):
    import jax
    import jax.numpy as jnp

    def _L0_gnn_ref(x, edge_index, virt_h, virt_edge_index, Wq, Wk, Wv, bn_gamma, bn_beta):
        import jax, jax.numpy as jnp
        import numpy as np
        N_NODES = 5000
        N_EDGES = 80000
        DIM_H = 512
        N_HEADS = 8
        D_HEAD = DIM_H // N_HEADS

        def _exphormer_attn(x, edge_index, Wq, Wk, Wv):
            N, D = x.shape
            H, d = (N_HEADS, D_HEAD)
            Q = (x @ Wq).reshape(N, H, d)
            K = (x @ Wk).reshape(N, H, d)
            V = (x @ Wv).reshape(N, H, d)
            src, dst = (edge_index[0], edge_index[1])
            scale = np.float32(1.0 / np.sqrt(d))
            score = jnp.einsum('ehd,ehd->eh', K[src], Q[dst]) * scale
            score = jnp.exp(jnp.clip(score, -5.0, 5.0))[..., None]
            msg = V[src] * score
            wV = jax.ops.segment_sum(msg, dst, num_segments=N)
            Z = jax.ops.segment_sum(score, dst, num_segments=N)
            return (wV / (Z + 1e-06)).reshape(N, D)
        h_attn = _exphormer_attn(x, edge_index, Wq, Wk, Wv)
        h = x + h_attn
        mean = jnp.mean(h, axis=0)
        var = jnp.mean(jnp.square(h - mean), axis=0)
        return (h - mean) * jax.lax.rsqrt(var + 1e-05) * bn_gamma + bn_beta

    def _L0_mix_ref(x, w_qkv, w_out, b_out):
        import jax, jax.numpy as jnp
        import numpy as np
        DIM = 512
        HEADS = 8
        DIM_HEAD = 64
        INNER = HEADS * DIM_HEAD
        b, n, d = x.shape
        qkv = x @ w_qkv
        q, k, v = jnp.split(qkv, 3, axis=-1)

        def to_heads(t):
            return t.reshape(b, n, HEADS, DIM_HEAD).transpose(0, 2, 1, 3)
        q, k, v = map(to_heads, (q, k, v))
        q = jax.nn.elu(q) + 1.0
        k = jax.nn.elu(k) + 1.0
        kv = jnp.einsum('bhnd,bhnm->bhdm', k, v)
        z = 1.0 / (jnp.einsum('bhnd,bhd->bhn', q, k.sum(axis=2)) + 1e-06)
        out = jnp.einsum('bhnd,bhdm->bhnm', q, kv) * z[..., None]
        out = out.transpose(0, 2, 1, 3).reshape(b, n, INNER)
        return out @ w_out + b_out

    def _L0_ffn_ref(hidden_states, gate_w, w1, b1, w2, b2, sw1, sb1, sw2, sb2):
        import jax, jax.numpy as jnp
        import numpy as np
        B, S, H, E, K, DF, SH = (8, 512, 512, 8, 2, 128, 512)
        x = hidden_states
        xf = x.reshape(-1, x.shape[-1])
        T = xf.shape[0]
        scores = jax.nn.softmax(xf @ gate_w.T, axis=-1)
        topk_w, topk_i = jax.lax.top_k(scores, K)
        topk_w = topk_w / (topk_w.sum(-1, keepdims=True) + 1e-20)
        combine = jnp.zeros((T, E), xf.dtype).at[jnp.arange(T)[:, None], topk_i].add(topk_w)
        h1 = jax.nn.relu(jnp.einsum('th,ehf->tef', xf, w1) + b1)
        eo = jnp.einsum('tef,efh->teh', h1, w2) + b2
        y = jnp.einsum('te,teh->th', combine, eo)
        shared = jax.nn.relu(xf @ sw1 + sb1) @ sw2 + sb2
        return (y + shared).reshape(x.shape)

    def _L1_gnn_ref(node_tokens, relation_tokens, edge_index, num_nodes, Wm, bm, Wu, bu, gamma, beta):
        import jax, jax.numpy as jnp
        import numpy as np
        N = 1250
        E = 20000
        D = 512
        head = edge_index[0]
        tail = edge_index[1]
        msg = node_tokens[head] + relation_tokens
        msg = msg @ Wm.T + bm
        agg = jax.ops.segment_sum(msg, tail, num_segments=num_nodes)
        deg = jax.ops.segment_sum(jnp.ones((msg.shape[0],), dtype=msg.dtype), tail, num_segments=num_nodes)
        agg = agg / jnp.maximum(deg, 1.0)[:, None]
        update_in = jnp.concatenate((node_tokens, agg), axis=-1)
        update = update_in @ Wu.T + bu
        out = node_tokens + jax.nn.gelu(update, approximate=False)
        mean = jnp.mean(out, axis=-1, keepdims=True)
        var = jnp.var(out, axis=-1, keepdims=True)
        return (out - mean) / jnp.sqrt(var + 1e-05) * gamma + beta

    def _L1_mix_ref(x, qkv_w, qkv_b, out_w, out_b, ln_gamma, ln_beta):
        import jax, jax.numpy as jnp
        import numpy as np
        HEADS = 8
        EPS_LN = 1e-05
        EPS_NORM = 1e-08
        B, N, C = x.shape
        h = HEADS
        d = C // h
        residual = x
        mu = jnp.mean(x, axis=-1, keepdims=True)
        var = jnp.var(x, axis=-1, keepdims=True)
        xn = (x - mu) / jnp.sqrt(var + EPS_LN) * ln_gamma + ln_beta
        qkv = xn @ qkv_w.T + qkv_b
        qkv = qkv.reshape(B, N, 3, h, d).transpose(2, 0, 3, 1, 4)
        q, k, v = (qkv[0], qkv[1], qkv[2])
        q = jax.nn.elu(q) + 1.0
        k = jax.nn.elu(k) + 1.0
        kv = jnp.einsum('bhnd,bhne->bhde', k, v)
        k_sum = jnp.sum(k, axis=2)
        out = jnp.einsum('bhnd,bhde->bhne', q, kv)
        normalizer = jnp.einsum('bhnd,bhd->bhn', q, k_sum)
        out = out / (normalizer[..., None] + EPS_NORM)
        out = out.transpose(0, 2, 1, 3).reshape(B, N, C)
        out = out @ out_w.T + out_b
        return out + residual

    def _L1_ffn_ref(x, attn_w, attn_b, gate_w, gate_b, w1, b1, w2, b2):
        import jax, jax.numpy as jnp
        import numpy as np
        B, S, D = (32, 512, 512)
        E, H, O, K = (8, 256, 512, 2)
        scores = x @ attn_w + attn_b
        aw = jax.nn.softmax(scores, axis=1)
        pooled = jnp.sum(x * aw, axis=1)
        gates = jax.nn.softmax(pooled @ gate_w + gate_b, axis=-1)
        _, idx = jax.lax.top_k(gates, K)
        mask = jnp.sum(jax.nn.one_hot(idx, E, dtype=gates.dtype), axis=-2)
        g = gates * mask
        g = g / (jnp.sum(g, axis=-1, keepdims=True) + 1e-09)
        h = jax.nn.gelu(jnp.einsum('bsd,edh->ebsh', x, w1) + b1[:, None, None, :], approximate=False)
        eo = jax.nn.gelu(jnp.einsum('ebsh,eho->ebso', h, w2) + b2[:, None, None, :], approximate=False)
        return jnp.einsum('ebso,be->bso', eo, g)
    edge_index = jnp.stack([src, dst])
    xn = _layernorm(x, axis=-1)
    x = x + _L0_gnn_ref(xn, edge_index, L0_gnn_virt_h, L0_gnn_virt_edge_index, L0_gnn_Wq, L0_gnn_Wk, L0_gnn_Wv, L0_gnn_bn_gamma, L0_gnn_bn_beta) + _L0_mix_ref(xn[None], L0_mix_w_qkv, L0_mix_w_out, L0_mix_b_out)[0]
    x = x + _L0_ffn_ref(_layernorm(x, axis=-1)[None], L0_ffn_gate_w, L0_ffn_w1, L0_ffn_b1, L0_ffn_w2, L0_ffn_b2, L0_ffn_sw1, L0_ffn_sb1, L0_ffn_sw2, L0_ffn_sb2)[0]
    xn = _layernorm(x, axis=-1)
    x = x + _L1_gnn_ref(xn, edge_attr_512, edge_index, 1250, L1_gnn_Wm, L1_gnn_bm, L1_gnn_Wu, L1_gnn_bu, L1_gnn_gamma, L1_gnn_beta) + _L1_mix_ref(xn[None], L1_mix_qkv_w, L1_mix_qkv_b, L1_mix_out_w, L1_mix_out_b, L1_mix_ln_gamma, L1_mix_ln_beta)[0]
    x = x + _L1_ffn_ref(_layernorm(x, axis=-1)[None], L1_ffn_attn_w, L1_ffn_attn_b, L1_ffn_gate_w, L1_ffn_gate_b, L1_ffn_w1, L1_ffn_b1, L1_ffn_w2, L1_ffn_b2)[0]
    return x

_drawn_inputs = setup_inputs


def setup_inputs(seed=0):
    import zlib

    import numpy as np

    out = dict(_drawn_inputs(seed))
    spreads = {'L0_gnn_bn_gamma': (1.0, 0.2),
     'L0_gnn_bn_beta': (0.0, 0.1),
     'L1_gnn_bm': (0.0, 0.631),
     'L1_gnn_bu': (0.0, 0.519),
     'L1_gnn_gamma': (1.0, 0.2),
     'L1_gnn_beta': (0.0, 0.319),
     'L1_mix_qkv_b': (0.0, 0.353),
     'L1_mix_out_b': (0.0, 0.341),
     'L1_mix_ln_gamma': (1.0, 0.6),
     'L1_mix_ln_beta': (0.0, 0.349),
     'L1_ffn_gate_b': (0.0, 0.8),
     'L1_ffn_b1': (0.0, 0.8),
     'L1_ffn_b2': (0.0, 0.8)}
    factors = {'L0_mix_w_qkv': 3.141,
     'L0_mix_w_out': 2.98,
     'L0_mix_b_out': 6.863,
     'L0_ffn_b1': 40.758,
     'L0_ffn_b2': 8.0,
     'L0_ffn_sb1': 8.0,
     'L0_ffn_sb2': 8.0,
     'L1_ffn_attn_w': 4.915,
     'L1_ffn_gate_w': 4.736,
     'L1_ffn_w1': 8.0,
     'L1_ffn_w2': 7.638,
     'edge_attr_512': 2.845}
    for name, (base, spread) in spreads.items():
        noise = np.random.default_rng([zlib.crc32(name.encode()), seed]).standard_normal(out[name].shape)
        drawn = base * np.exp(spread * noise) if base else spread * noise
        out[name] = jnp.asarray(drawn.astype(out[name].dtype))
    for name, factor in factors.items():
        out[name] = (out[name] * factor).astype(out[name].dtype)
    return out
```

```python
import concourse.bass as bass
from concourse import mybir
from contextlib import ExitStack

import numpy as np

F32 = mybir.dt.float32
F32R = mybir.dt.float32r
BF16 = mybir.dt.bfloat16
FP16 = mybir.dt.float16
I32 = mybir.dt.int32
U32 = mybir.dt.uint32
U16 = mybir.dt.uint16
ALU = mybir.AluOpType
ACT = mybir.ActivationFunctionType
AX = mybir.AxisListType
ds = bass.ds

N = 1250
D = 512
E = 41250
H = 8
DH = D // H
P = 125
NT = N // P
NP = NT // 2
KT = D // 128
EC = 128
GC = 6
GE = GC * EC
G = -(-E // GE)
STAGE = 2 * D
POOL_LO = (1, 3, 5)
EPS = 1e-5


class Kernel:

    def __init__(self, nc, ctx):
        self.nc, self.ctx = nc, ctx
        self.banks = ctx.enter_context(nc.psum_tensor("banks", [128, 8, 512], F32))
        self.sems = []

    def sem(self, name):
        self.sems.append(self.nc.alloc_semaphore(name=name))
        return self.sems[-1]

    def clear(self):
        self.nc.clear_and_free_semaphores(self.sems)
        self.nc.all_engine_barrier()
        self.sems = []

    def keep(self, name, shape, dt):
        return self.ctx.enter_context(self.nc.sbuf_tensor(name, shape, dt))


def edge_phase(k, src, dst, edge_attr, counts, esum, ident):
    nc = k.nc
    ctx = ExitStack()
    with ctx:
        def sb(name, shape, dt):
            return ctx.enter_context(nc.sbuf_tensor(name, shape, dt))

        SW = 418
        idx_i = sb("idx_i", [128, 2, G * GC], I32)
        dst_f = sb("dst_f", [128, G * GC], F32)
        src_f = sb("src_f", [128, G * GC], F32)
        gext = sb("gext", [128, 2, G], F32)
        gall = sb("gall", [128, 2, G], F32)
        tcol = sb("tcol", [1, 2, NT, G], F32)
        gnum = sb("gnum", [1, 2, NT, G], F32)
        tmask = sb("tmask", [1, 3, NT, G], F32)
        tlim = sb("tlim", [1, 6, NT], F32)
        tab = sb("tab", [1, 3, NT], I32)
        iota_s = sb("iota_s", [128, 3 * SW], FP16)
        iota_t = sb("iota_t", [128, NT, P + 1], FP16)
        raw = sb("raw", [128, GC, D], F32)
        e_hi = sb("e_hi", [128, GC, D], F32R)
        e_lo = sb("e_lo", [128, GC, D], F32R)
        oh_s = sb("oh_s", [128, GC, 3 * SW], BF16)
        oh_d = sb("oh_d", [128, GC, P + 1], F32R)
        oh_db = sb("oh_db", [128, GC, P + 1], BF16)
        zero_b = sb("zero_b", [128, D], BF16)
        ct = sb("ct", [128, 3 * SW], F32)

        s_idx = k.sem("s_idx")
        s_iota = k.sem("s_iota")
        s_prep = k.sem("s_prep")
        s_all = k.sem("s_all")
        s_tab = k.sem("s_tab")
        s_raw = [k.sem(f"s_raw{c}") for c in range(GC)]
        s_hi = [k.sem(f"s_hi{c}") for c in range(GC)]
        s_lo = [k.sem(f"s_lo{c}") for c in range(GC)]
        s_oh = [k.sem(f"s_oh{c}") for c in range(GC)]
        s_use = [k.sem(f"s_use{c}") for c in range(GC)]
        s_fin = k.sem("s_fin")
        s_ct = k.sem("s_ct")
        s_es = k.sem("s_es")
        s_tr = k.sem("s_tr")
        s_tre = k.sem("s_tre")

        banks = k.banks
        block = ctx.enter_context(nc.Block())
        edge_h = edge_attr.rearrange("(c p) f -> c p f", p=EC)

        def visits(eng, t):
            v0 = eng.value_load(tab[0:1, 0, ds(t, 1)], min_val=0, max_val=NT * G)
            v1 = eng.value_load(tab[0:1, 1, ds(t, 1)], min_val=1, max_val=NT * G)
            return v0, v1

        @block.sync
        def _(sp):
            sp.dma_start(idx_i[:, 0, :], src).then_inc(s_idx, 16)
            sp.dma_start(idx_i[:, 1, :], dst).then_inc(s_idx, 16)
            sp.wait_ge(s_tab, 1)
            with sp.Fori(0, NT) as t:
                v0, v1 = visits(sp, t)
                shift = sp.value_load(tab[0:1, 2, ds(t, 1)], min_val=0, max_val=2 * NT * G)
                with sp.Fori(v0, v1) as v:
                    g = sp.snap(nc.s_assert_within(v + shift - NT * G, 0, G - 1))
                    for c in range(GC):
                        sp.wait_ge(s_lo[c], v + 1)
                        sp.dma_start(raw[:, c, :], edge_h[ds(GC * g + c, 1), :, :].rearrange("a p f -> (a p) f"))\
                          .then_inc(s_raw[c], 16)

        @block.gpsimd
        def _(pool):
            pool.iota(iota_s[:, :], [[1, 3 * SW]], base=0, channel_multiplier=0,
                      allow_small_or_imprecise_dtypes=True)
            pool.iota(iota_t[:, :, :], [[P, NT], [1, P + 1]], base=0, channel_multiplier=0,
                      allow_small_or_imprecise_dtypes=True)
            pool.iota(tcol[:, 0, :, :], [[P, NT], [0, G]], base=0, channel_multiplier=0,
                      allow_small_or_imprecise_dtypes=True)
            pool.iota(tcol[:, 1, :, :], [[P, NT], [0, G]], base=P, channel_multiplier=0,
                      allow_small_or_imprecise_dtypes=True)
            pool.iota(gnum[:, 0, :, :], [[0, NT], [1, G]], base=1, channel_multiplier=0,
                      allow_small_or_imprecise_dtypes=True)
            pool.iota(gnum[:, 1, :, :], [[0, NT], [-1, G]], base=G, channel_multiplier=0,
                      allow_small_or_imprecise_dtypes=True).then_inc(s_iota, 1)
            pool.wait_ge(s_prep, 5)
            pool.partition_all_reduce(gall[:, :, :].rearrange("p a g -> p (a g)"),
                                      gext[:, :, :].rearrange("p a g -> p (a g)"), 128,
                                      bass.bass_isa.ReduceOp.max).then_inc(s_all, 1)
            for c in POOL_LO:
                pool.sem_inc(s_lo[c], 1)
            pool.wait_ge(s_tab, 1)
            with pool.Fori(0, NT) as t:
                v0, v1 = visits(pool, t)
                with pool.Fori(v0, v1) as v:
                    for c in POOL_LO:
                        pool.wait_ge(s_hi[c], v + 1)
                        pool.wait_ge(s_use[c], v + 1)
                        pool.tensor_tensor(e_lo[:, c, :], raw[:, c, :], e_hi[:, c, :].bitcast(F32),
                                           ALU.subtract).then_inc(s_lo[c], 1)

        @block.scalar
        def _(act):
            act.sem_inc(s_ct, 1)
            act.sem_inc(s_tre, 1)
            act.wait_ge(s_tab, 1)
            with act.Fori(0, NT) as t:
                v0, v1 = visits(act, t)
                with act.Fori(v0, v1) as v:
                    for c in range(GC):
                        act.wait_ge(s_raw[c], v * 16 + 16)
                        act.wait_ge(s_use[c], v + 1)
                        act.copy(e_hi[:, c, :], raw[:, c, :]).then_inc(s_hi[c], 1)
                act.wait_ge(s_fin, t + 1)
                act.wait_ge(s_tr, t + 1)
                act.copy(ct[:P, :].rearrange("p (b f) -> p b f", b=3), banks[:P, 0:3, 0:SW]).then_inc(s_ct, 1)
                act.wait_ge(s_tr, t + 2)
                act.copy(counts[:, ds(t, 1), 0:8, :].rearrange("p t (b a) f -> p (t b) (a f)", b=2),
                               banks[:P, 4:6, 0:4 * P])
                act.copy(counts[:, ds(t, 1), 8:NT, :].rearrange("p t a f -> p (t a f)"),
                               banks[:P, 6, 0:2 * P]).then_inc(s_tre, 1)

        @block.vector
        def _(dve):
            dve.wait_ge(s_idx, 32)
            dve.tensor_copy(src_f[:, :], idx_i[:, 0, :]).then_inc(s_prep, 1)
            dve.tensor_copy(dst_f[:, :], idx_i[:, 1, :]).then_inc(s_prep, 1)
            dve.memset(zero_b[:, :], 0.0).then_inc(s_prep, 1)
            dve.wait_ge(s_prep, 3)
            dg = dst_f[:, :].rearrange("p (g c) -> p g c", c=GC)
            dve.tensor_reduce(gext[:, 0, :], dg, AX.X, ALU.max).then_inc(s_prep, 1)
            dve.tensor_reduce(gext[:, 1, :], dg, AX.X, ALU.min, negate=True).then_inc(s_prep, 1)
            dve.wait_ge(s_all, 1)
            dve.wait_ge(s_iota, 1)
            step = [5]

            def link(ins):
                step[0] += 1
                ins.then_inc(s_prep, 1)
                dve.wait_ge(s_prep, step[0])

            gmax = gall[0:1, 0:1, :].to_broadcast([1, NT, G])
            gmin = gall[0:1, 1:2, :].to_broadcast([1, NT, G])
            link(dve.tensor_tensor(tmask[:, 0], gmax, tcol[:, 0], ALU.is_ge))
            link(dve.scalar_tensor_tensor(tmask[:, 1], gmin, -1.0, tcol[:, 1], ALU.mult, ALU.is_lt))
            link(dve.tensor_tensor(tmask[:, 2], tmask[:, 0], tmask[:, 1], ALU.mult))
            link(dve.tensor_tensor(tmask[:, 0], tmask[:, 2], gnum[:, 0], ALU.mult))
            link(dve.tensor_tensor(tmask[:, 1], tmask[:, 2], gnum[:, 1], ALU.mult))
            hi, lo, cnt, one, v1, v0 = (tlim[:, i, :] for i in range(6))
            link(dve.tensor_reduce(hi, tmask[:, 0], AX.X, ALU.max))
            link(dve.tensor_reduce(lo, tmask[:, 1], AX.X, ALU.max))
            link(dve.tensor_scalar(lo, lo, -1.0, float(G), ALU.mult, ALU.add))
            link(dve.tensor_scalar(lo, lo, float(G - 1), None, ALU.min))
            link(dve.tensor_tensor(cnt, hi, lo, ALU.subtract))
            link(dve.tensor_scalar(cnt, cnt, 1.0, None, ALU.max))
            link(dve.memset(one, 1.0))
            link(dve.tensor_tensor_scan(v1, one, cnt, 0.0, ALU.mult, ALU.add))
            link(dve.tensor_tensor(v0, v1, cnt, ALU.subtract))
            link(dve.tensor_tensor(lo, lo, v0, ALU.subtract))
            link(dve.tensor_copy(tab[:, 0, :], v0))
            link(dve.tensor_copy(tab[:, 1, :], v1))
            link(dve.tensor_scalar(tab[:, 2, :], lo, float(NT * G), None, ALU.add))
            for c in range(GC):
                if c not in POOL_LO:
                    dve.sem_inc(s_lo[c], 1)
            dve.sem_inc(s_es, 1)
            dve.sem_inc(s_tab, 1)
            with dve.Fori(0, NT) as t:
                v0, v1 = visits(dve, t)
                shift = dve.value_load(tab[0:1, 2, ds(t, 1)], min_val=0, max_val=2 * NT * G)
                with dve.Fori(v0, v1) as v:
                    g = dve.snap(nc.s_assert_within(v + shift - NT * G, 0, G - 1))
                    for c in range(GC):
                        chunk = ds(g * GC + c, 1)
                        dve.wait_ge(s_use[c], v + 1)
                        dve.tensor_scalar(oh_s[:, c, :], iota_s[:, :], src_f[:, chunk], None, ALU.is_equal)
                        tile_nodes = iota_t[:, ds(t, 1), :].rearrange("p a f -> p (a f)")
                        dve.tensor_scalar(oh_d[:, c, :], tile_nodes, dst_f[:, chunk], None, ALU.is_equal)
                        dve.tensor_scalar(oh_db[:, c, :], tile_nodes, dst_f[:, chunk], None,
                                          ALU.is_equal).then_inc(s_oh[c], 1)
                        if c not in POOL_LO:
                            dve.wait_ge(s_hi[c], v + 1)
                            dve.tensor_tensor(e_lo[:, c, :], raw[:, c, :], e_hi[:, c, :].bitcast(F32),
                                              ALU.subtract).then_inc(s_lo[c], 1)
                dve.wait_ge(s_fin, t + 1)
                dve.tensor_copy(esum[:, ds(t, 1), :].rearrange("p a f -> p (a f)"), banks[:P, 3, :]).then_inc(s_es, 1)

        @block.tensor
        def _(pe):
            for c in range(GC):
                pe.sem_inc(s_use[c], 1)
            pe.sem_inc(s_tr, 1)
            pe.wait_ge(s_tab, 1)
            with pe.Fori(0, NT) as t:
                v0, v1 = visits(pe, t)
                pe.wait_ge(s_ct, t + 1)
                pe.wait_ge(s_es, t + 1)
                for b in range(3):
                    pe.matmul(banks[:P, b, 0:SW], zero_b[:, 0:P], zero_b[:, 0:SW], start=True, stop=False)
                pe.matmul(banks[:P, 3, :], zero_b[:, 0:P], zero_b[:, :], start=True, stop=False)
                with pe.Fori(v0, v1) as v:
                    for c in range(GC):
                        pe.wait_ge(s_oh[c], v + 1)
                        for b in range(3):
                            pe.matmul(banks[:P, b, 0:SW], oh_db[:, c, 0:P], oh_s[:, c, b * SW:(b + 1) * SW],
                                      start=False, stop=False)
                        pe.wait_ge(s_hi[c], v + 1)
                        pe.matmul(banks[:P, 3, :], oh_d[:, c, 0:P], e_hi[:, c, :], start=False, stop=False)
                        pe.wait_ge(s_lo[c], v + 2)
                        pe.matmul(banks[:P, 3, :], oh_d[:, c, 0:P], e_lo[:, c, :], start=False,
                                  stop=False).then_inc(s_use[c], 1)
                for b in range(3):
                    pe.matmul(banks[:P, b, 0:SW], zero_b[:, 0:P], zero_b[:, 0:SW], start=False, stop=True)
                pe.matmul(banks[:P, 3, :], zero_b[:, 0:P], zero_b[:, :], start=False, stop=True).then_inc(s_fin, 1)
                pe.wait_ge(s_ct, t + 2)
                pe.wait_ge(s_tre, t + 1)
                for a in range(NT):
                    last = pe.transpose(banks[:P, 4 + a // 4, a % 4 * P:(a % 4 + 1) * P], ct[:P, a * P:(a + 1) * P],
                                        ident[:P, :P])
                last.then_inc(s_tr, 1)


class Weights:

    def __init__(self, k, sb, name, pieces):
        self.pieces = []
        for dram, hi, lo in pieces:
            rows = min(max(1, STAGE // hi.shape[-1]), hi.shape[1])
            self.pieces += [((dram, r, rows), hi[:, r:r + rows], lo[:, r:r + rows])
                            for r in range(0, hi.shape[1], rows)] if len(hi.shape) == 3 else [((dram, 0, 0), hi, lo)]
        self.stage = sb(f"{name}_stage", [128, 2, STAGE], F32)
        self.s_in = [k.sem(f"s_{name}_w_in{b}") for b in range(2)]
        self.s_hi = k.sem(f"s_{name}_w_hi")
        self.s_lo = k.sem(f"s_{name}_w_lo")

    def view(self, n):
        hi = self.pieces[n][1]
        rows, size = hi.shape[0], hi.free_size()
        flat = self.stage[:rows, n % 2, 0:size]
        return flat if len(hi.shape) == 2 else flat.rearrange("p (a b) -> p a b", b=hi.shape[-1])

    def load(self, sp, *chosen):
        for n, ((dram, r, rows), _, _) in enumerate(self.pieces):
            if n >= 2:
                sp.wait_ge(self.s_lo, n - 1)
            if callable(dram):
                dram = dram(*chosen)
            if rows:
                dram = dram[:, r:r + rows]
            sp.dma_start(self.view(n), dram).then_inc(self.s_in[n % 2], 16)

    def high(self, act):
        for n, (_, hi, _) in enumerate(self.pieces):
            act.wait_ge(self.s_in[n % 2], 16 * (n // 2 + 1))
            act.copy(hi, self.view(n)).then_inc(self.s_hi, 1)

    def low(self, dve):
        for n, (_, hi, lo) in enumerate(self.pieces):
            dve.wait_ge(self.s_hi, n + 1)
            dve.tensor_tensor(lo, self.view(n), hi.bitcast(F32), ALU.subtract).then_inc(self.s_lo, 1)

    def wait(self, pe):
        pe.wait_ge(self.s_lo, len(self.pieces))


def product(pe, out, lhs, rhs, at, terms, first=True, last=True):
    n = 0
    for term in terms:
        for a, b in ((0, 0), (0, 1), (1, 0)):
            l, r = at(lhs[a], rhs[b], term)
            n += 1
            ins = pe.matmul(out, l, r, start=first and n == 1, stop=last and n == 3 * len(terms))
    return ins


class Normed:

    def __init__(self, k, sb, name, x, mean, rstd, ident, bank, affine=None):
        self.k, self.x, self.mean, self.rstd, self.ident, self.bank = k, x, mean, rstd, ident, bank
        self.affine = affine
        self.xn = sb(f"{name}_xn", [P, 2, D], F32)
        self.hi = sb(f"{name}_hi", [128, KT, 2, P], F32R)
        self.lo = sb(f"{name}_lo", [128, KT, 2, P], F32R)
        self.s_xn = k.sem(f"s_{name}_xn")
        self.s_aff = k.sem(f"s_{name}_aff")
        self.s_xt = k.sem(f"s_{name}_xt")
        self.s_hi = k.sem(f"s_{name}_hi")
        self.s_lo = k.sem(f"s_{name}_lo")
        self.s_used = k.sem(f"s_{name}_used")

    def parts(self):
        return self.hi, self.lo

    def rows(self, dve, i):
        for h in range(2):
            t = ds(2 * i + h, 1)
            out = self.xn[:, h, :]
            ins = dve.tensor_scalar(out, self.x[:, t, :].rearrange("p a f -> p (a f)"), self.mean[:, t], self.rstd[:, t],
                                    ALU.subtract, ALU.mult)
            if self.affine:
                gamma, beta = self.affine
                ins.then_inc(self.s_aff, 1)
                dve.wait_ge(self.s_aff, 4 * i + 2 * h + 1)
                dve.tensor_tensor(out, out, gamma, ALU.mult).then_inc(self.s_aff, 1)
                dve.wait_ge(self.s_aff, 4 * i + 2 * h + 2)
                ins = dve.tensor_tensor(out, out, beta, ALU.add)
            ins.then_inc(self.s_xn, 1)

    def transposes(self, pe, i):
        for h in range(2):
            pe.wait_ge(self.s_xn, 2 * i + h + 1)
            for c in range(KT):
                ins = pe.transpose(self.k.banks[:, self.bank + h, c * P:(c + 1) * P],
                                   self.xn[:, h, c * 128:(c + 1) * 128], self.ident[:P, :P])
            ins.then_inc(self.s_xt, 1)

    def psum(self, h):
        return self.k.banks[:, self.bank + h, 0:KT * P].rearrange("p (c n) -> p c n", n=P)

    def high(self, act, i):
        for h in range(2):
            act.wait_ge(self.s_xt, 2 * i + h + 1)
            act.wait_ge(self.s_used, i + 1)
            act.copy(self.hi[:, :, h, :], self.psum(h)).then_inc(self.s_hi, 1)

    def low(self, dve, i):
        for h in range(2):
            dve.wait_ge(self.s_xt, 2 * i + h + 1)
            dve.wait_ge(self.s_hi, 2 * i + h + 1)
            dve.tensor_tensor(self.lo[:, :, h, :], self.psum(h), self.hi[:, :, h, :].bitcast(F32),
                              ALU.subtract).then_inc(self.s_lo, 1)

    def wait(self, pe, i):
        pe.wait_ge(self.s_lo, 2 * i + 2)


def half_of(h):
    return lambda xt, w, c: (xt[:, c, h, :], w[:, c, :])


def feature_tile(f):
    return lambda w, xt, c: (w[:, c, f * 128:(f + 1) * 128], xt[:, c, :, :].rearrange("p h n -> p (h n)"))


def chain(eng, sem, start=0):
    n = [start]

    def link(ins):
        n[0] += 1
        ins.then_inc(sem, 1)
        eng.wait_ge(sem, n[0])

    return link


def statistics(k, name, x, mean, rstd, again=None):
    nc = k.nc
    with ExitStack() as ctx:
        stats = ctx.enter_context(nc.sbuf_tensor(f"{name}_stats", [P, NT, nc.vector.BN_STATS_DIM], F32))
        mv = ctx.enter_context(nc.sbuf_tensor(f"{name}_mv", [P, NT, 2], F32))
        var = ctx.enter_context(nc.sbuf_tensor(f"{name}_var", [P, 2, NT], F32))
        s_bn = k.sem(f"s_{name}_bn")
        s_ag = k.sem(f"s_{name}_ag")
        s_st = k.sem(f"s_{name}_st")
        s_sq = k.sem(f"s_{name}_sq")
        block = ctx.enter_context(nc.Block())

        @block.vector
        def _(dve):
            with dve.Fori(0, NT) as t:
                dve.bn_stats(stats[:, ds(t, 1), :].rearrange("p a f -> p (a f)"),
                             x[:, ds(t, 1), :].rearrange("p a f -> p (a f)")).then_inc(s_bn, 1)
            dve.wait_ge(s_bn, NT)
            for t in range(NT):
                dve.bn_aggr(mv[:, t, :], stats[:, t, :]).then_inc(s_ag, 1)
            dve.wait_ge(s_ag, NT)
            link = chain(dve, s_st)
            link(dve.memset(mean[:, NT:], 0.0))
            link(dve.memset(rstd[:, NT:], 0.0))
            link(dve.tensor_copy(mean[:, 0:NT], mv[:, :, 0]))
            link(dve.tensor_scalar(var[:, 0, :], mv[:, :, 1], EPS, None, ALU.add))
            dve.wait_ge(s_sq, 1)
            link(dve.reciprocal(rstd[:, 0:NT], var[:, 1, :]))
            if again is not None:
                link(dve.tensor_tensor(var[:, 0, :], rstd[:, 0:NT], rstd[:, 0:NT], ALU.mult))
                link(dve.tensor_tensor(var[:, 0, :], var[:, 0, :], mv[:, :, 1], ALU.mult))
                link(dve.tensor_scalar(var[:, 0, :], var[:, 0, :], EPS, None, ALU.add))
                dve.wait_ge(s_sq, 2)
                link(dve.reciprocal(again[:, 0:NT], var[:, 1, :]))
                link(dve.memset(again[:, NT:], 0.0))
                link(dve.tensor_tensor(again[:, :], again[:, :], rstd[:, :], ALU.mult))

        @block.scalar
        def _(act):
            act.wait_ge(s_st, 4)
            act.activation(var[:, 1, :], var[:, 0, :], ACT.Sqrt).then_inc(s_sq, 1)
            if again is not None:
                act.wait_ge(s_st, 8)
                act.activation(var[:, 1, :], var[:, 0, :], ACT.Sqrt).then_inc(s_sq, 1)


def attention_phase(k, x, y, mean, rstd, counts, ident, Wq, Wk, Wv):
    nc = k.nc
    banks = k.banks
    with ExitStack() as ctx:
        def sb(name, shape, dt):
            return ctx.enter_context(nc.sbuf_tensor(name, shape, dt))

        kst = sb("kst", [128, H, N], F32R)
        vs = sb("vs", [P, NT, H, DH + 1], F32)
        wq = [sb(f"wq_s{a}", [128, KT, D], F32R) for a in range(2)]

        with ExitStack() as inner:
            def sbi(name, shape, dt):
                return inner.enter_context(nc.sbuf_tensor(name, shape, dt))

            wk = [sbi(f"wk_s{a}", [128, KT, D], F32R) for a in range(2)]
            wv = [sbi(f"wv_s{a}", [128, KT, D], F32R) for a in range(2)]
            w = Weights(k, sbi, "akv", [(src.rearrange("(c p) f -> p c f", p=128), t[0][:], t[1][:])
                                        for src, t in ((Wk, wk), (Wv, wv), (Wq, wq))])
            xt = Normed(k, sbi, "akv", x, mean, rstd, ident, 0)
            s_one = k.sem("s_akv_one")
            s_kp = k.sem("s_akv_kp")
            s_kh = k.sem("s_akv_kh")
            s_kl = k.sem("s_akv_kl")
            s_vp = k.sem("s_akv_vp")
            s_vc = k.sem("s_akv_vc")
            block = inner.enter_context(nc.Block())
            rows = ((0, 64), (64, 128))

            def kcols(i):
                return ds(i * 2 * P, 2 * P)

            @block.sync
            def _(sp):
                w.load(sp)

            @block.gpsimd
            def _(pool):
                pool.memset(vs[:, :, :, DH:DH + 1], 1.0).then_inc(s_one, 1)

            @block.tensor
            def _(pe):
                pe.sem_inc(xt.s_used, 1)
                xt.transposes(pe, 0)
                w.wait(pe)
                with pe.Fori(0, NP) as i:
                    xt.wait(pe, i)
                    xt.transposes(pe, i + 1)
                    for a in range(4):
                        pe.wait_ge(s_kl, 4 * i + a + 1)
                        product(pe, banks[:, 2 + a % 2, 0:2 * P], wk, xt.parts(), feature_tile(a),
                                range(KT)).then_inc(s_kp, 1)
                    for h in range(2):
                        pe.wait_ge(s_vc, 2 * i + h + 1)
                        ins = product(pe, banks[:P, 4 + h, :], xt.parts(), wv, half_of(h), range(KT))
                        ins.then_inc(s_vp, 1)
                    pe.wait_ge(s_vp, 2 * i + 2)
                    pe.sem_inc(xt.s_used, 1)

            @block.scalar
            def _(act):
                act.sem_inc(s_vc, 2)
                w.high(act)
                xt.high(act, 0)
                act.wait_ge(s_one, 1)
                with act.Fori(0, NP) as i:
                    for a in range(4):
                        act.wait_ge(s_kp, 4 * i + a + 1)
                        for e, (r0, r1) in enumerate(rows):
                            ins = act.copy(kst[r0:r1, 2 * a + e, kcols(i)], banks[r0:r1, 2 + a % 2, 0:2 * P])
                        ins.then_inc(s_kh, 1)
                    for h in range(2):
                        act.wait_ge(s_vp, 2 * i + h + 1)
                        act.copy(vs[:, ds(2 * i + h, 1), :, 0:DH].rearrange("p a h d -> p (a h) d"),
                                 banks[:P, 4 + h, :].rearrange("p (h d) -> p h d", d=DH)).then_inc(s_vc, 1)
                    xt.high(act, i + 1)

            @block.vector
            def _(dve):
                dve.sem_inc(s_kl, 2)
                xt.rows(dve, 0)
                w.low(dve)
                xt.low(dve, 0)
                with dve.Fori(0, NP) as i:
                    xt.rows(dve, i + 1)
                    for a in range(4):
                        dve.wait_ge(s_kh, 4 * i + a + 1)
                        for e, (r0, r1) in enumerate(rows):
                            q0, q1 = rows[1 - e]
                            ins = dve.tensor_tensor(kst[q0:q1, 2 * a + e, kcols(i)], banks[r0:r1, 2 + a % 2, 0:2 * P],
                                                    kst[r0:r1, 2 * a + e, kcols(i)].bitcast(F32), ALU.subtract)
                        ins.then_inc(s_kl, 1)
                    xt.low(dve, i + 1)

        UNITS = NT // 2
        SR, ER, PR, AHEAD = 4, 4, 4, 3
        NU = H * UNITS
        QU = 2 * UNITS
        HG = H // 2
        qh = sb("qh", [128, H, 2 * P], F32R)
        ql = sb("ql", [128, H, 2 * P], F32R)
        er = sb("er", [P, ER, 2, 2 * P], F32)
        pr = sb("pr", [P, PR, 2, 2 * P], F32)
        so = sb("so", [DH + 1, 2, 2 * P], F32)
        zr = sb("zr", [P, 2, 2, HG], F32)
        on = sb("on", [P, 2, D // 2], F32)
        xt = Normed(k, sb, "att", x, mean, rstd, ident, 0)
        s_qp = k.sem("s_qp")
        s_qh = k.sem("s_qh")
        s_ql = k.sem("s_ql")
        s_s = k.sem("s_s")
        s_e = k.sem("s_e")
        s_c = k.sem("s_c")
        s_p = k.sem("s_p")
        s_av = k.sem("s_av")
        s_so = k.sem("s_so")
        s_ot = k.sem("s_ot")
        s_on = k.sem("s_on")
        s_n = k.sem("s_n")
        s_y = k.sem("s_y")
        block = ctx.enter_context(nc.Block())
        rows = ((0, 64), (64, 128))
        LO, HI = float(np.exp(np.float32(-5.0))), float(np.exp(np.float32(5.0)))

        @block.tensor
        def _(pe):
            def q_product(i, a):
                pe.wait_ge(s_ql, 4 * i + a + 1)
                product(pe, banks[:, 2, 0:2 * P], wq, xt.parts(), feature_tile(a), range(KT)).then_inc(s_qp, 1)

            def scores(i, n):
                h, u = divmod(n, UNITS)
                if n % QU == 0:
                    pe.wait_ge(s_ql, 4 * i + n // QU + 2)
                pe.wait_ge(s_e, NU * i + n + 1)
                for j in range(2):
                    cols = slice((2 * u + j) * P, (2 * u + j + 1) * P)
                    out = banks[:P, 4 + n % SR, j * 2 * P:(j + 1) * 2 * P]
                    pe.matmul(out, kst[:, h, cols], qh[:, h, :], start=True, stop=False)
                    ins = pe.matmul(out, kst[:, h, cols], ql[:, h, :], start=False, stop=True)
                ins.then_inc(s_s, 1)

            def back(i, h):
                if h == 0:
                    xt.wait(pe, i + 1)
                if h == HG:
                    pe.wait_ge(s_on, 2 * i + 2)
                pe.wait_ge(s_so, H * i + h + 3)
                for g in range(2):
                    ins = pe.transpose(banks[:P, g, h % HG * (DH + 1):(h % HG + 1) * (DH + 1)],
                                       so[:, h % 2, g * P:(g + 1) * P], ident[:DH + 1, :DH + 1])
                ins.then_inc(s_ot, 1)

            pe.sem_inc(xt.s_used, 1)
            pe.sem_inc(s_av, PR)
            xt.transposes(pe, 0)
            xt.wait(pe, 0)
            for a in range(4):
                q_product(0, a)
            pe.wait_ge(s_qp, 4)
            pe.sem_inc(xt.s_used, 1)
            for n in range(AHEAD):
                scores(0, n)
            with pe.Fori(0, NP) as i:
                for n in range(NU):
                    h, u = divmod(n, UNITS)
                    if n + AHEAD < NU:
                        scores(i, n + AHEAD)
                    else:
                        scores(i + 1, n + AHEAD - NU)
                    if n == 3:
                        pe.wait_ge(s_on, 2 * i + 1)
                        xt.transposes(pe, i + 1)
                    pe.wait_ge(s_p, NU * i + n + 1 + ER)
                    if u == 0:
                        pe.wait_ge(s_so, H * i + h + 1)
                        if h % 2 == 0:
                            pe.wait_ge(s_ql, 4 * i + h // 2 + 5)
                    for j in range(2):
                        ins = pe.matmul(banks[:DH + 1, 2 + h % 2, 0:2 * P], vs[:, 2 * u + j, h, :], pr[:, n % PR, j, :],
                                        start=u == 0 and j == 0, stop=u == UNITS - 1 and j == 1)
                    ins.then_inc(s_av, 1)
                    if n % QU == QU - 1 - AHEAD:
                        if n < QU:
                            xt.wait(pe, i + 1)
                        pe.wait_ge(s_so, H * i + h + 2)
                        q_product(i + 1, n // QU)
                    if h and u == 1:
                        back(i, h - 1)
                pe.wait_ge(s_qp, 4 * i + 8)
                pe.sem_inc(xt.s_used, 1)
                back(i, H - 1)

        @block.scalar
        def _(act):
            def q_high(i, a):
                act.wait_ge(s_qp, 4 * i + a + 1)
                for e, (r0, r1) in enumerate(rows):
                    for q0, q1 in rows:
                        ins = act.copy(qh[q0:q1, 2 * a + e, :], banks[r0:r1, 2, 0:2 * P])
                ins.then_inc(s_qh, 1)

            def out(i, h):
                act.wait_ge(s_av, NU * i + UNITS * (h + 1) + PR)
                if h >= 2:
                    act.wait_ge(s_ot, H * i + h - 1)
                act.copy(so[:, h % 2, :], banks[:DH + 1, 2 + h % 2, 0:2 * P]).then_inc(s_so, 1)

            act.sem_inc(s_e, SR)
            act.sem_inc(s_so, 2)
            xt.high(act, 0)
            for a in range(4):
                q_high(0, a)
            with act.Fori(0, NP) as i:
                for n in range(NU):
                    h, u = divmod(n, UNITS)
                    act.wait_ge(s_s, NU * i + n + 1)
                    act.wait_ge(s_p, NU * i + n + 1)
                    act.activation(er[:, n % ER, :, :].rearrange("p j n -> p (j n)"),
                                   banks[:P, 4 + n % SR, 0:4 * P], ACT.Exp, scale=1.0 / 8.0).then_inc(s_e, 1)
                    if n == 5:
                        xt.high(act, i + 1)
                    if n % QU == QU - 2:
                        q_high(i + 1, n // QU)
                    if h and u == 1:
                        out(i, h - 1)
                out(i, H - 1)

        @block.vector
        def _(dve):
            def q_low(i, a):
                dve.wait_ge(s_qh, 4 * i + a + 1)
                for e, (r0, r1) in enumerate(rows):
                    for q0, q1 in rows:
                        ins = dve.tensor_tensor(ql[q0:q1, 2 * a + e, :], banks[r0:r1, 2, 0:2 * P],
                                                qh[r0:r1, 2 * a + e, :].bitcast(F32), ALU.subtract)
                ins.then_inc(s_ql, 1)

            def clip(i, n):
                dve.wait_ge(s_e, NU * i + n + 1 + SR)
                dve.tensor_scalar(er[:, n % ER, :, :], er[:, n % ER, :, :], HI, LO, ALU.min, ALU.max).then_inc(s_c, 1)

            def divide(i, q):
                dve.wait_ge(s_ot, H * i + HG * (q + 1))
                out = banks[:P, 0:2, 0:HG * (DH + 1)].rearrange("p g (h d) -> p g h d", d=DH + 1)
                first = 6 * (2 * i + q)
                dve.tensor_scalar(zr[:, 0], out[:, :, :, DH:DH + 1].rearrange("p g h d -> p g (h d)"), 1e-6, None,
                                  ALU.add).then_inc(s_n, 1)
                dve.wait_ge(s_n, first + 1)
                dve.reciprocal(zr[:, 1], zr[:, 0]).then_inc(s_n, 1)
                dve.wait_ge(s_n, first + 2)
                for g in range(2):
                    ins = dve.tensor_tensor(on[:, g, :].rearrange("p (h d) -> p h d", d=DH), out[:, g, :, 0:DH],
                                            zr[:, 1, g, :].unsqueeze(2).to_broadcast([P, HG, DH]), ALU.mult)
                    ins.then_inc(s_n, 1)
                dve.wait_ge(s_n, first + 4)
                dve.sem_inc(s_on, 1)
                dve.wait_ge(s_y, 2 * i + 2)
                for g in range(2):
                    ys = y[:, ds(2 * i + g, 1), q * (D // 2):(q + 1) * (D // 2)].rearrange("p a f -> p (a f)")
                    dve.tensor_tensor(ys, ys, on[:, g, :], ALU.add).then_inc(s_n, 1)

            dve.sem_inc(s_ql, 1)
            dve.sem_inc(s_on, 1)
            dve.sem_inc(s_p, ER)
            xt.rows(dve, 0)
            xt.low(dve, 0)
            for a in range(4):
                q_low(0, a)
            with dve.Fori(0, NP) as i:
                clip(i, 0)
                for n in range(NU):
                    h, u = divmod(n, UNITS)
                    if n + 1 < NU:
                        clip(i, n + 1)
                    dve.wait_ge(s_c, NU * i + n + 1)
                    dve.wait_ge(s_av, NU * i + n + 1)
                    cnt = counts[:, ds(2 * i, 2), 2 * u:2 * u + 2, :].rearrange("p g j d -> p j g d")
                    dve.tensor_tensor(pr[:, n % PR, :, :].rearrange("p j (g d) -> p j g d", g=2),
                                      er[:, n % ER, :, :].rearrange("p j (g d) -> p j g d", g=2), cnt,
                                      ALU.mult).then_inc(s_p, 1)
                    if n == 0:
                        xt.rows(dve, i + 1)
                    if n in (1, 2):
                        t = ds(2 * i + n - 1, 1)
                        dve.tensor_scalar(y[:, t, :].rearrange("p a f -> p (a f)"),
                                          x[:, t, :].rearrange("p a f -> p (a f)"), mean[:, t], rstd[:, t],
                                          ALU.subtract, ALU.mult).then_inc(s_y, 1)
                    if n == 5:
                        xt.low(dve, i + 1)
                    if n % QU == QU - 2:
                        q_low(i + 1, n // QU)
                    if n == UNITS * HG + 2:
                        divide(i, 0)
                divide(i, 1)
                dve.wait_ge(s_n, 6 * (2 * i + 2))


def batchnorm_phase(k, x, y, ones_n, gamma, beta):
    nc, banks = k.nc, k.banks
    with ExitStack() as ctx:
        def sb(name, shape, dt):
            return ctx.enter_context(nc.sbuf_tensor(name, shape, dt))

        row = sb("bn_row", [P, 2, D], F32)
        sq = sb("bn_sq", [P, 2, D], F32)
        inv = sb("bn_inv", [P, 3, D], F32)
        s_row = k.sem("s_bnr")
        s_m = k.sem("s_bnm")
        s_d = k.sem("s_bnd")
        s_s = k.sem("s_bns")
        s_u = k.sem("s_bnu")
        s_v = k.sem("s_bnv")
        s_c = k.sem("s_bnc")
        s_o = k.sem("s_bno")
        s_p = k.sem("s_bnp")
        block = ctx.enter_context(nc.Block())

        def tile(a, t):
            return a[:, ds(t, 1), :].rearrange("p a f -> p (a f)")

        @block.sync
        def _(sp):
            sp.dma_start(row[:, 0, :], gamma.partition_broadcast(P)).then_inc(s_row, 16)
            sp.dma_start(row[:, 1, :], beta.partition_broadcast(P)).then_inc(s_row, 16)

        @block.tensor
        def _(pe):
            for t in range(NT):
                ins = pe.matmul(banks[:P, 0, :], ones_n[:P, :P], y[:, t, :], start=t == 0, stop=t == NT - 1)
            ins.then_inc(s_m, 1)
            pe.sem_inc(s_u, 2)
            for t in range(NT):
                pe.wait_ge(s_s, t + 1)
                pe.matmul(banks[:P, 1, :], ones_n[:P, :P], sq[:, t % 2, :], start=t == 0,
                          stop=t == NT - 1).then_inc(s_u, 1)

        @block.scalar
        def _(act):
            with act.Fori(0, NP) as i:
                for h in range(2):
                    act.wait_ge(s_d, 2 * i + h + 1)
                    act.wait_ge(s_u, 2 * i + h + 1)
                    act.activation(sq[:, h, :], tile(y, 2 * i + h), ACT.Square).then_inc(s_s, 1)
            act.wait_ge(s_c, 1)
            act.activation(inv[:, 1, :], inv[:, 0, :], ACT.Sqrt).then_inc(s_v, 1)

        @block.vector
        def _(dve):
            dve.wait_ge(s_m, 1)
            with dve.Fori(0, NT) as t:
                dve.tensor_tensor(tile(y, t), tile(y, t), banks[:P, 0, :], ALU.subtract).then_inc(s_d, 1)
            link = chain(dve, s_c)
            dve.wait_ge(s_u, NT + 2)
            link(dve.tensor_scalar(inv[:, 0, :], banks[:P, 1, :], EPS, None, ALU.add))
            dve.wait_ge(s_v, 1)
            link(dve.reciprocal(inv[:, 2, :], inv[:, 1, :]))
            dve.wait_ge(s_row, 32)
            link(dve.tensor_tensor(inv[:, 2, :], inv[:, 2, :], row[:, 0, :], ALU.mult))
            dve.wait_ge(s_d, NT)
            with dve.Fori(0, NP) as i:
                for h in range(2):
                    dve.tensor_tensor(tile(y, 2 * i + h), tile(y, 2 * i + h), inv[:, 2, :], ALU.mult).then_inc(s_o, 1)
                for h in range(2):
                    dve.wait_ge(s_o, 4 * i + h + 1)
                    dve.tensor_tensor(tile(y, 2 * i + h), tile(y, 2 * i + h), row[:, 1, :], ALU.add).then_inc(s_o, 1)

        @block.gpsimd
        def _(pool):
            with pool.Fori(0, NP) as i:
                for h in range(2):
                    pool.wait_ge(s_o, 4 * i + 3 + h)
                    pool.tensor_tensor(tile(y, 2 * i + h), tile(y, 2 * i + h), tile(x, 2 * i + h),
                                       ALU.add).then_inc(s_p, 1)


def mix_phase(k, name, x, y, mean, rstd, ident, mask, wqkv, qkv_b, q_cols, wout, out_b, affine=None, base=None):
    nc, banks = k.nc, k.banks
    with ExitStack() as ctx:
        def sb(nm, shape, dt):
            return ctx.enter_context(nc.sbuf_tensor(f"{name}_{nm}", shape, dt))

        def sem(nm):
            return k.sem(f"s_{name}_{nm}")

        kvw = [sb(f"kvw{a}", [128, KT, D], F32R) for a in range(2)]
        ksb = [sb(f"ksb{a}", [128, KT, 128], F32R) for a in range(2)]
        wq = [sb(f"wq{a}", [128, KT, D], F32R) for a in range(2)]
        bq = sb("bq", [128, KT], F32)
        rows = sb("rows", [P, 5, D], F32)
        s_row = sem("row")
        gb = (rows[:, 3, :], rows[:, 4, :]) if affine else None
        bias = qkv_b is not None

        with ExitStack() as inner:
            def sbi(nm, shape, dt):
                return inner.enter_context(nc.sbuf_tensor(nm, shape, dt))

            wk = [sbi(f"{name}_wk{a}", [128, KT, D], F32R) for a in range(2)]
            wv = [sbi(f"{name}_wv{a}", [128, KT, D], F32R) for a in range(2)]
            wo = [sbi(f"{name}_wo{a}", [128, KT, D], F32R) for a in range(2)]
            wsrc = wqkv.rearrange("(c p) f -> p c f", p=128)
            w = Weights(k, sbi, f"{name}k", [
                (wsrc[:, :, D:2 * D], wk[0][:], wk[1][:]), (wsrc[:, :, 2 * D:3 * D], wv[0][:], wv[1][:]),
                (wout.rearrange("(c p) f -> p c f", p=128), wo[0][:], wo[1][:]),
                (wsrc[:, :, 0:D], wq[0][:], wq[1][:])])
            xt = Normed(k, sbi, f"{name}k", x, mean, rstd, ident, 0, gb)
            kx = sbi(f"{name}_kx", [P, 2, 2, D], F32)
            kf = sbi(f"{name}_kf", [P, 2, D], F32)
            kh, kl, vh, vl = (sbi(f"{name}_{nm}", [P, 2, D], F32R) for nm in ("kh", "kl", "vh", "vl"))
            vf = sbi(f"{name}_vf", [P, 2, D], F32) if bias else None
            ones = sbi(f"{name}_ones", [P, 2], F32)
            kvm = sbi(f"{name}_kvm", [128, KT, 128], F32)
            ksm = sbi(f"{name}_ksm", [128, KT], F32)
            kvt = [sbi(f"{name}_kvt{a}", [128, KT, 128], F32R) for a in range(2)]
            s_kp, s_vp = sem("kp"), sem("vp")
            s_kb, s_vb = sem("kb"), sem("vb")
            s_ke, s_kf = sem("ke"), sem("kf")
            s_kh, s_kl, s_vh, s_vl = sem("kh"), sem("kl"), sem("vh"), sem("vl")
            s_kv = sem("kv")
            s_one, s_f, s_w, s_wh = sem("one"), sem("f"), sem("w"), sem("wh")
            block = inner.enter_context(nc.Block())

            @block.sync
            def _(sp):
                sp.dma_start(rows[:, 2, :], out_b.partition_broadcast(P)).then_inc(s_row, 16)
                if affine:
                    sp.dma_start(rows[:, 3, :], affine[0].partition_broadcast(P)).then_inc(s_row, 16)
                    sp.dma_start(rows[:, 4, :], affine[1].partition_broadcast(P)).then_inc(s_row, 16)
                if bias:
                    sp.dma_start(rows[:, 0, :], qkv_b[D:2 * D].partition_broadcast(P)).then_inc(s_row, 16)
                    sp.dma_start(rows[:, 1, :], qkv_b[2 * D:3 * D].partition_broadcast(P)).then_inc(s_row, 16)
                    sp.dma_start(bq[:, :], q_cols).then_inc(s_row, 16)
                w.load(sp)

            nrow = 16 + (32 if affine else 0) + (48 if bias else 0)

            @block.gpsimd
            def _(pool):
                pool.memset(ones[:, :], 1.0).then_inc(s_one, 1)

            @block.tensor
            def _(pe):
                pe.sem_inc(xt.s_used, 1)
                pe.sem_inc(s_kv, 2)
                xt.transposes(pe, 0)
                w.wait(pe)
                pe.wait_ge(s_one, 2)
                with pe.Fori(0, NP) as i:
                    xt.wait(pe, i)
                    xt.transposes(pe, i + 1)
                    for h in range(2):
                        product(pe, banks[:P, 2 + h, :], xt.parts(), wk, half_of(h), range(KT)).then_inc(s_kp, 1)
                    for h in range(2):
                        ins = product(pe, banks[:P, 4 + h, :], xt.parts(), wv, half_of(h), range(KT))
                        ins.then_inc(s_vp, 1)
                    pe.wait_ge(s_vp, 2 * i + 2)
                    pe.sem_inc(xt.s_used, 1)
                    for h in range(2):
                        pe.wait_ge(s_kl, 2 * i + h + 1)
                        pe.wait_ge(s_vl, 2 * i + h + 1)
                        for j in range(KT):
                            c = slice(128 * j, 128 * (j + 1))
                            for n, (a, b) in enumerate(((vh, kh), (vh, kl), (vl, kh))):
                                pe.matmul(banks[:, 6, c], a[:, h, c], b[:, h, c], start=False, stop=False,
                                          skip_group_check=True)
                            ins = pe.matmul(banks[:, 7, 2 * j:2 * j + 2], kf[:, h, c], ones[:, :], start=False,
                                            stop=False, skip_group_check=True)
                        ins.then_inc(s_kv, 1)
                for j in range(KT):
                    if j == 0:
                        pe.wait_ge(s_f, 5)
                    ins = product(pe, banks[:, 2 + j, :], kvt, wo, lambda a, b, c: (a[:, c, :], b[:, c, :]), [j])
                    ins.then_inc(s_w, 1)

            @block.scalar
            def _(act):
                w.high(act)
                xt.high(act, 0)
                with act.Fori(0, NP) as i:
                    for h in range(2):
                        if bias:
                            act.wait_ge(s_kb, 2 * i + h + 1)
                            src = kf[:, h, :]
                        else:
                            act.wait_ge(s_kp, 2 * i + h + 1)
                            src = banks[:P, 2 + h, :]
                        act.activation(kx[:, h, 0, :], src, ACT.Exp)
                        act.activation(kx[:, h, 1, :], src, ACT.Relu).then_inc(s_ke, 1)
                    for h in range(2):
                        act.wait_ge(s_kf, 2 * i + h + 1)
                        act.copy(kh[:, h, :], kf[:, h, :]).then_inc(s_kh, 1)
                    for h in range(2):
                        if bias:
                            act.wait_ge(s_vb, 2 * i + h + 1)
                        act.wait_ge(s_vp, 2 * i + h + 1)
                        act.wait_ge(s_kv, 2 * i + h + 1)
                        act.copy(vh[:, h, :], vf[:, h, :] if bias else banks[:P, 4 + h, :]).then_inc(s_vh, 1)
                    xt.high(act, i + 1)
                act.wait_ge(s_f, 3)
                act.copy(kvt[0][:, :, :], kvm[:, :, :]).then_inc(s_f, 1)
                for j in range(KT):
                    act.wait_ge(s_w, j + 1)
                    act.copy(kvw[0][:, j, :], banks[:, 2 + j, :]).then_inc(s_wh, 1)

            @block.vector
            def _(dve):
                dve.wait_ge(s_row, nrow)
                dve.memset(banks[:, 6:8, :], 0.0).then_inc(s_one, 1)
                xt.rows(dve, 0)
                w.low(dve)
                xt.low(dve, 0)
                with dve.Fori(0, NP) as i:
                    xt.rows(dve, i + 1)
                    if bias:
                        for h in range(2):
                            dve.wait_ge(s_kp, 2 * i + h + 1)
                            dve.wait_ge(s_kv, 2 * i + h + 1)
                            dve.tensor_tensor(kf[:, h, :], banks[:P, 2 + h, :], rows[:, 0, :], ALU.add).then_inc(s_kb, 1)
                    for h in range(2):
                        dve.wait_ge(s_ke, 2 * i + h + 1)
                        dve.wait_ge(s_kv, 2 * i + h + 1)
                        dve.scalar_tensor_tensor(kf[:, h, :], kx[:, h, 0, :], 1.0, kx[:, h, 1, :], ALU.min,
                                                 ALU.add).then_inc(s_kf, 1)
                    for h in range(2):
                        dve.wait_ge(s_kh, 2 * i + h + 1)
                        dve.tensor_tensor(kl[:, h, :], kf[:, h, :], kh[:, h, :].bitcast(F32),
                                          ALU.subtract).then_inc(s_kl, 1)
                    if bias:
                        for h in range(2):
                            dve.wait_ge(s_vp, 2 * i + h + 1)
                            dve.tensor_tensor(vf[:, h, :], banks[:P, 4 + h, :], rows[:, 1, :], ALU.add).then_inc(s_vb, 1)
                    for h in range(2):
                        dve.wait_ge(s_vh, 2 * i + h + 1)
                        dve.tensor_tensor(vl[:, h, :], vf[:, h, :] if bias else banks[:P, 4 + h, :],
                                          vh[:, h, :].bitcast(F32), ALU.subtract).then_inc(s_vl, 1)
                    xt.low(dve, i + 1)
                dve.wait_ge(s_kv, 2 * NP + 2)
                kvb = banks[:, 6, :].rearrange("p (j d) -> p j d", d=128)
                many = mask[:, :].unsqueeze(1).to_broadcast([128, KT, 128])
                dve.tensor_tensor(kvm[:, :, :], kvb, many, ALU.mult).then_inc(s_f, 1)
                dve.tensor_copy(ksm[:, :], banks[:, 7, 0:2 * KT].rearrange("p (j a) -> p j a", a=2)[:, :, 0]).then_inc(s_f, 1)
                dve.wait_ge(s_f, 2)
                dve.sem_inc(s_f, 1)
                dve.wait_ge(s_f, 4)
                dve.tensor_tensor(kvt[1][:, :, :], kvm[:, :, :], kvt[0][:, :, :].bitcast(F32), ALU.subtract).then_inc(s_f, 1)
                dve.wait_ge(s_f, 5)
                for j in range(KT):
                    dve.tensor_scalar(kvm[:, j, :], mask[:, :], ksm[:, j:j + 1], None, ALU.mult).then_inc(s_f, 1)
                dve.wait_ge(s_f, 5 + KT)
                dve.tensor_copy(ksb[0][:, :, :], kvm[:, :, :]).then_inc(s_f, 1)
                dve.wait_ge(s_f, 6 + KT)
                dve.tensor_tensor(ksb[1][:, :, :], kvm[:, :, :], ksb[0][:, :, :].bitcast(F32), ALU.subtract)
                dve.wait_ge(s_wh, KT)
                for j in range(KT):
                    dve.tensor_tensor(kvw[1][:, j, :], banks[:, 2 + j, :], kvw[0][:, j, :].bitcast(F32), ALU.subtract)

        qx = sb("qx", [128, 2, KT, 2 * P], F32)
        qf = sb("qf", [128, KT, 2 * P], F32)
        qp = [sb(f"qp{a}", [128, KT, 2 * P], F32R) for a in range(2)]
        rz = sb("rz", [128, 2, KT, 2 * P], F32)
        qz = sb("qz", [128, KT, 2 * P], F32)
        qs = [sb(f"qs{a}", [128, KT, 2, P], F32R) for a in range(2)]
        tmp = sb("tmp", [P, 2, D], F32)
        xt = Normed(k, sb, f"{name}q", x, mean, rstd, ident, 0, gb)
        once = base
        s_qp, s_qe, s_qf, s_qh, s_ql = sem("qp"), sem("qe"), sem("qf"), sem("qh"), sem("ql")
        s_z, s_ze, s_zr, s_qz, s_zh, s_zl = sem("z"), sem("ze"), sem("zr"), sem("qz"), sem("zh"), sem("zl")
        s_o, s_t, s_y, s_b = sem("o"), sem("t"), sem("y"), sem("b")
        block = ctx.enter_context(nc.Block())

        def tile(a, t):
            return a[:, ds(t, 1), :].rearrange("p a f -> p (a f)")

        def qbank(f):
            return banks[:, 2 + f // 2, f % 2 * 2 * P:(f % 2 + 1) * 2 * P]

        def zbank(f):
            return banks[:, 4 + f // 2, f % 2 * 2 * P:(f % 2 + 1) * 2 * P]

        @block.tensor
        def _(pe):
            pe.sem_inc(xt.s_used, 1)
            xt.transposes(pe, 0)
            with pe.Fori(0, NP) as i:
                xt.wait(pe, i)
                xt.transposes(pe, i + 1)
                for f in range(KT):
                    ins = product(pe, qbank(f), wq, xt.parts(), feature_tile(f), range(KT))
                    ins.then_inc(s_qp, 1)
                pe.wait_ge(s_qp, KT * (i + 1))
                pe.sem_inc(xt.s_used, 1)
                for f in range(KT):
                    pe.wait_ge(s_ql, KT * i + f + 1)
                    product(pe, zbank(f), ksb, qp, lambda a, b, c: (a[:, c, :], b[:, c, :]), [f]).then_inc(s_z, 1)
                pe.wait_ge(s_zl, i + 1)
                for h in range(2):
                    pe.wait_ge(s_t, 2 * i + h + 1)
                    product(pe, banks[:P, 6 + h, :], qs, kvw, half_of(h), range(KT)).then_inc(s_o, 1)

        @block.scalar
        def _(act):
            xt.high(act, 0)
            with act.Fori(0, NP) as i:
                for f in range(KT):
                    act.wait_ge(s_qp, KT * i + f // 2 * 2 + 2)
                    b = bq[:, f:f + 1] if bias else 0.0
                    act.activation(qx[:, 0, f, :], qbank(f), ACT.Exp, bias=b)
                    act.activation(qx[:, 1, f, :], qbank(f), ACT.Relu, bias=b).then_inc(s_qe, 1)
                for f in range(KT):
                    act.wait_ge(s_qf, KT * i + f + 1)
                    act.copy(qp[0][:, f, :], qf[:, f, :]).then_inc(s_qh, 1)
                act.wait_ge(s_qz, i + 1)
                act.copy(qs[0][:, :, :, :].rearrange("p c h n -> p c (h n)"), qz[:, :, :]).then_inc(s_zh, 1)
                xt.high(act, i + 1)

        @block.vector
        def _(dve):
            dve.sem_inc(s_t, 2)
            xt.rows(dve, 0)
            xt.low(dve, 0)
            with dve.Fori(0, NP) as i:
                xt.rows(dve, i + 1)
                for f in range(KT):
                    dve.wait_ge(s_qe, KT * i + f + 1)
                    dve.scalar_tensor_tensor(qf[:, f, :], qx[:, 0, f, :], 1.0, qx[:, 1, f, :], ALU.min,
                                             ALU.add).then_inc(s_qf, 1)
                for f in range(KT):
                    dve.wait_ge(s_qh, KT * i + f + 1)
                    dve.tensor_tensor(qp[1][:, f, :], qf[:, f, :], qp[0][:, f, :].bitcast(F32),
                                      ALU.subtract).then_inc(s_ql, 1)
                dve.wait_ge(s_z, KT * (i + 1))
                for g in range(2):
                    dve.tensor_scalar(rz[:, 0, 2 * g:2 * g + 2, :], banks[:, 4 + g, 0:4 * P].rearrange("p (f n) -> p f n", f=2),
                                      eps_of(name), None, ALU.add).then_inc(s_ze, 1)
                dve.wait_ge(s_ze, 2 * i + 2)
                dve.reciprocal(rz[:, 1], rz[:, 0]).then_inc(s_zr, 1)
                dve.wait_ge(s_zr, i + 1)
                dve.tensor_tensor(qz[:, :, :], qf[:, :, :], rz[:, 1], ALU.mult).then_inc(s_qz, 1)
                dve.wait_ge(s_zh, i + 1)
                dve.tensor_tensor(qs[1][:, :, :, :].rearrange("p c h n -> p c (h n)"), qz[:, :, :],
                                  qs[0][:, :, :, :].bitcast(F32).rearrange("p c h n -> p c (h n)"),
                                  ALU.subtract).then_inc(s_zl, 1)
                xt.low(dve, i + 1)
                for h in range(2):
                    t = 2 * i + h
                    if once is not None:
                        dve.tensor_scalar(tile(y, t), tile(x, t), once[0][:, ds(t, 1)], once[1][:, ds(t, 1)],
                                          ALU.subtract, ALU.mult).then_inc(s_b, 1)
                        dve.wait_ge(s_b, 2 * t + 1)
                        dve.tensor_tensor(tile(y, t), tile(y, t), tile(x, t), ALU.add).then_inc(s_b, 1)
                    dve.wait_ge(s_o, t + 1)
                    dve.tensor_tensor(tmp[:, h, :], banks[:P, 6 + h, :], rows[:, 2, :], ALU.add).then_inc(s_t, 1)
                    dve.wait_ge(s_t, t + 1 + 2)
                    if once is not None:
                        dve.wait_ge(s_b, 2 * t + 2)
                    dve.tensor_tensor(tile(y, t), tile(y, t), tmp[:, h, :], ALU.add).then_inc(s_y, 1)


def eps_of(name):
    return {"mix0": 1e-6, "mix1": 1e-8}[name]


def flat(a, t):
    return a[:, ds(t, 1), :].rearrange("p a f -> p (a f)")


def plain(a, b, c):
    return a[:, c, :], b[:, c, :]


def experts_phase(k, x, mean, rstd, ident, sel, gate_w, w1, sw1, w2, sw2, b1_cols, b2_rows):
    nc, banks = k.nc, k.banks
    EX, FT = 8, 12
    with ExitStack() as ctx:
        def sb(nm, shape, dt):
            return ctx.enter_context(nc.sbuf_tensor(f"moe_{nm}", shape, dt))

        def sem(nm):
            return k.sem(f"s_moe_{nm}")

        v1 = [sb(f"v1{a}", [128, KT, 1024], F32R) for a in range(2)]
        vs1 = [sb(f"vs1{a}", [128, KT, D], F32R) for a in range(2)]
        v2 = [sb(f"v2{a}", [128, FT, D], F32R) for a in range(2)]
        vg = [sb(f"vg{a}", [128, KT, EX], F32R) for a in range(2)]
        vb = [sb(f"vb{a}", [EX + 1, D], F32R) for a in range(2)]
        sel_r = sb("sel", [EX, EX, 128], F32R)
        b1 = sb("b1", [128, FT], F32)
        w = Weights(k, sb, "moe", [
            (gate_w.rearrange("(c p) e -> p c e", p=128), vg[0][:], vg[1][:]),
            (b2_rows, vb[0][:, :], vb[1][:, :]),
            (sw1.rearrange("(c p) f -> p c f", p=128), vs1[0][:], vs1[1][:]),
            (w1.rearrange("(c p) f -> p c f", p=128), v1[0][:], v1[1][:]),
            (w2.rearrange("e p f -> p e f"), v2[0][:, 0:EX], v2[1][:, 0:EX]),
            (sw2.rearrange("(c p) f -> p c f", p=128), v2[0][:, EX:], v2[1][:, EX:])])
        xt = Normed(k, sb, "moex", x, mean, rstd, ident, 0)
        ht = [sb(f"ht{a}", [128, FT, 2, P], F32R) for a in range(2)]
        hr = sb("hr", [128, 2, 2 * P], F32)
        hp = sb("hp", [128, 2, 2 * P], F32)
        iota8 = sb("iota8", [P, EX], F32)
        g1 = sb("g1", [P, 8, 2, EX], F32)
        g0 = sb("g0", [P, 8, 2], F32)
        cth = sb("cth", [EX + 1, 2, P], F32R)
        ctl = sb("ctl", [EX + 1, 2, P], F32R)
        s_c0 = sem("c0")
        s_bl = sem("bl")
        s_g = sem("g")
        s_gs = sem("gs")
        s_ge = sem("ge")
        s_ct = sem("ct")
        s_c1, s_cc = sem("c1"), sem("cc")
        s_h = sem("h")
        s_r = sem("r")
        s_p = sem("p")
        s_hh = sem("hh")
        s_hl = sem("hl")
        s_o = sem("o")
        s_y = sem("y")
        block = ctx.enter_context(nc.Block())
        LINKS = 22
        order = list(range(EX, FT)) + list(range(EX))

        @block.sync
        def _(sp):
            sp.dma_start(b1[:, :], b1_cols).then_inc(s_bl, 16)
            sp.dma_start(hp[0:EX, :, :].rearrange("p a b -> p (a b)"), sel[:, 0:4 * P]).then_inc(s_bl, 16)
            sp.dma_start(hr[0:EX, :, :].rearrange("p a b -> p (a b)"), sel[:, 4 * P:8 * P]).then_inc(s_bl, 16)
            sp.dma_start(g1[0:EX, 0:2, :, :].rearrange("p a b c -> p (a b c)")[:, 0:EX * 128 - 8 * P],
                         sel[:, 8 * P:EX * 128]).then_inc(s_bl, 16)
            w.load(sp)

        @block.gpsimd
        def _(pool):
            pool.iota(iota8[:, :], [[1, EX]], base=0, channel_multiplier=0,
                      allow_small_or_imprecise_dtypes=True).then_inc(s_c0, 1)

        @block.tensor
        def _(pe):
            pe.sem_inc(xt.s_used, 1)
            pe.sem_inc(s_o, 1)
            xt.transposes(pe, 0)
            w.wait(pe)
            pe.wait_ge(s_c0, 4)
            with pe.Fori(0, NP) as i:
                xt.wait(pe, i)
                xt.transposes(pe, i + 1)
                pe.wait_ge(s_cc, i + 1)
                for h in range(2):
                    ins = product(pe, banks[:P, 5, EX * h:EX * (h + 1)], xt.parts(), vg, half_of(h), range(KT))
                ins.then_inc(s_g, 1)
                for q, f in enumerate(order):
                    if q == 3:
                        pe.wait_ge(s_gs, LINKS * (i + 1))
                        for h in range(2):
                            ins = pe.transpose(banks[0:EX, 5, 128 + h * P:128 + (h + 1) * P], g1[:, 7, h, :],
                                               ident[:P, :P])
                        ins.then_inc(s_ct, 1)
                    if q == FT - EX:
                        pe.wait_ge(s_cc, i + 2)
                    pe.wait_ge(s_hl, FT * i + q + 1)
                    bank = banks[:, 2 + q % 3, :]
                    ws, col = (v1, f) if f < EX else (vs1, f - EX)
                    ins = product(pe, bank[:, 0:2 * P], ws, xt.parts(), feature_tile(col), range(KT))
                    if f < EX:
                        for n, part in enumerate((cth, ctl)):
                            ins = pe.matmul(bank[:, 2 * P:4 * P], sel_r[:, f, :],
                                            part[0:EX, :, :].rearrange("p h n -> p (h n)"), start=n == 0, stop=n == 1)
                    ins.then_inc(s_h, 1)
                pe.wait_ge(s_h, FT * (i + 1))
                pe.sem_inc(xt.s_used, 1)
                for h in range(2):
                    pe.wait_ge(s_y, 2 * i + h + 1)
                    out = banks[:P, 6 + h, :]
                    for n, (a, b) in enumerate(((cth, vb[0]), (cth, vb[1]), (ctl, vb[0]))):
                        pe.matmul(out, a[:, h, :], b[:, :], start=n == 0, stop=False)
                    for q, f in enumerate(order):
                        pe.wait_ge(s_hl, FT * i + q + 1 + 3)
                        ins = product(pe, out, ht, v2, half_of(h), [f], first=False, last=q == FT - 1)
                    ins.then_inc(s_o, 1)

        @block.scalar
        def _(act):
            w.high(act)
            xt.high(act, 0)
            act.wait_ge(s_bl, 64)
            with act.Fori(0, NP) as i:
                act.wait_ge(s_gs, LINKS * i + 2)
                act.activation(g1[:, 1], g1[:, 0], ACT.Exp).then_inc(s_ge, 1)
                for q in range(FT + 1):
                    if q < FT:
                        f = order[q]
                        act.wait_ge(s_h, FT * i + q + 1)
                        act.wait_ge(s_hl, FT * i + q + 2)
                        act.activation(hr[:, q % 2, :], banks[:, 2 + q % 3, 0:2 * P], ACT.Relu,
                                       bias=b1[:, f:f + 1]).then_inc(s_r, 1)
                    if q:
                        m, f = q - 1, order[q - 1]
                        if f < EX:
                            act.wait_ge(s_p, EX * i + f + 1)
                        else:
                            act.wait_ge(s_r, FT * i + m + 1)
                        act.copy(ht[0][:, f, :, :].rearrange("p h n -> p (h n)"),
                                 (hp if f < EX else hr)[:, m % 2, :]).then_inc(s_hh, 1)
                xt.high(act, i + 1)

        @block.vector
        def _(dve):
            dve.sem_inc(s_hl, 3)
            dve.sem_inc(s_y, 2)
            dve.wait_ge(s_bl, 64)
            flat_sel = sel_r[:, :, :].rearrange("p e m -> p (e m)")
            dve.tensor_copy(flat_sel[:, 0:4 * P], hp[0:EX, :, :].rearrange("p a b -> p (a b)"))
            dve.tensor_copy(flat_sel[:, 4 * P:8 * P], hr[0:EX, :, :].rearrange("p a b -> p (a b)")).then_inc(s_c0, 1)
            dve.tensor_copy(flat_sel[:, 8 * P:], g1[0:EX, 0:2, :, :].rearrange("p a b c -> p (a b c)")[:, 0:EX * 128 - 8 * P])\
               .then_inc(s_c0, 1)
            dve.memset(cth[:, :, :].bitcast(F32), 1.0).then_inc(s_cc, 1)
            dve.memset(ctl[:, :, :].bitcast(F32), 0.0).then_inc(s_c0, 1)
            dve.wait_ge(s_c0, 4)
            xt.rows(dve, 0)
            w.low(dve)
            xt.low(dve, 0)
            with dve.Fori(0, NP) as i:
                xt.rows(dve, i + 1)
                n = [0]

                def link(ins):
                    n[0] += 1
                    ins.then_inc(s_gs, 1)
                    dve.wait_ge(s_gs, LINKS * i + n[0])

                def wide(a):
                    return a.unsqueeze(2).to_broadcast([P, 2, EX])

                gate = banks[:P, 5, 0:2 * EX].rearrange("p (h e) -> p h e", e=EX)
                many = iota8[:, :].unsqueeze(1).to_broadcast([P, 2, EX])
                dve.wait_ge(s_g, i + 1)
                link(dve.tensor_reduce(g0[:, 0], gate, AX.X, ALU.max))
                link(dve.tensor_tensor(g1[:, 0], gate, wide(g0[:, 0]), ALU.subtract))
                dve.wait_ge(s_ge, i + 1)
                link(dve.tensor_reduce(g0[:, 1], g1[:, 1], AX.X, ALU.add))
                link(dve.reciprocal(g0[:, 2], g0[:, 1]))
                link(dve.tensor_tensor(g1[:, 2], g1[:, 1], wide(g0[:, 2]), ALU.mult))
                for c, seen in ((4, g1[:, 2]), (5, g1[:, 3])):
                    link(dve.tensor_reduce(g0[:, 3], seen, AX.X, ALU.max))
                    link(dve.tensor_tensor(g1[:, 6], seen, wide(g0[:, 3]), ALU.is_lt))
                    link(dve.scalar_tensor_tensor(g1[:, 6], g1[:, 6], float(EX), many, ALU.mult, ALU.add))
                    link(dve.tensor_reduce(g0[:, 4], g1[:, 6], AX.X, ALU.min))
                    link(dve.tensor_tensor(g1[:, c], many, wide(g0[:, 4]), ALU.is_equal))
                    if c == 4:
                        link(dve.scalar_tensor_tensor(g1[:, 3], g1[:, 4], -2.0, g1[:, 2], ALU.mult, ALU.add))
                link(dve.tensor_tensor(g1[:, 4], g1[:, 4], g1[:, 5], ALU.add))
                link(dve.tensor_tensor(g1[:, 6], g1[:, 2], g1[:, 4], ALU.mult))
                link(dve.tensor_reduce(g0[:, 3], g1[:, 6], AX.X, ALU.add))
                link(dve.tensor_scalar(g0[:, 4], g0[:, 3], 1e-20, None, ALU.add))
                link(dve.reciprocal(g0[:, 5], g0[:, 4]))
                link(dve.tensor_tensor(g1[:, 7], g1[:, 6], wide(g0[:, 5]), ALU.mult))
                assert n[0] == LINKS
                dve.wait_ge(s_ct, i + 1)
                tr = banks[0:EX, 5, 128:128 + 2 * P].rearrange("p (h n) -> p h n", n=P)
                dve.wait_ge(s_o, 2 * i + 1)
                dve.tensor_copy(cth[0:EX, :, :], tr).then_inc(s_c1, 1)
                dve.wait_ge(s_c1, i + 1)
                dve.tensor_tensor(ctl[0:EX, :, :], tr, cth[0:EX, :, :].bitcast(F32), ALU.subtract).then_inc(s_cc, 1)
                for q in range(FT + 1):
                    if q < FT and order[q] < EX:
                        f = order[q]
                        dve.wait_ge(s_r, FT * i + q + 1)
                        dve.tensor_tensor(hp[:, q % 2, :], hr[:, q % 2, :], banks[:, 2 + q % 3, 2 * P:4 * P],
                                          ALU.mult).then_inc(s_p, 1)
                    if q:
                        m, f = q - 1, order[q - 1]
                        dve.wait_ge(s_hh, FT * i + m + 1)
                        dve.tensor_tensor(ht[1][:, f, :, :].rearrange("p h n -> p (h n)"),
                                          (hp if f < EX else hr)[:, m % 2, :],
                                          ht[0][:, f, :, :].bitcast(F32).rearrange("p h n -> p (h n)"),
                                          ALU.subtract).then_inc(s_hl, 1)
                xt.low(dve, i + 1)
                for h in range(2):
                    dve.wait_ge(s_o, 2 * i + h + 2)
                    dve.tensor_tensor(flat(x, 2 * i + h), flat(x, 2 * i + h), banks[:P, 6 + h, :],
                                      ALU.add).then_inc(s_y, 1)


def graph_phase(k, x, y, mean, rstd, ident, counts_d, esum_d, wm, wu, bias_rows, gamma, beta):
    nc, banks = k.nc, k.banks
    with ExitStack() as ctx:
        def sb(nm, shape, dt):
            return ctx.enter_context(nc.sbuf_tensor(f"gn_{nm}", shape, dt))

        def sem(nm):
            return k.sem(f"s_gn_{nm}")

        wms = [sb(f"wm{a}", [128, KT, D], F32R) for a in range(2)]
        wus = [sb(f"wu{a}", [128, 2 * KT, D], F32R) for a in range(2)]
        wbs = [sb(f"wb{a}", [2, 2, D], F32R) for a in range(2)]
        w = Weights(k, sb, "gn", [(wm.rearrange("(c p) f -> p c f", p=128), wms[0][:], wms[1][:]),
                                  (wu.rearrange("(c p) f -> p c f", p=128), wus[0][:], wus[1][:]),
                                  (bias_rows, wbs[0][:], wbs[1][:])])
        xa = [sb(f"xa{a}", [P, NT, D], F32R) for a in range(2)]
        xf = sb("xf", [P, 2, D], F32)
        ones = sb("ones", [P, 2], F32R)
        cin = sb("cin", [P, NT, P], U16)
        ein = sb("ein", [P, D], F32)
        cs = [sb(f"cs{a}", [P, NT, P], F32R) for a in range(2)]
        dg = sb("dg", [P, 4], F32)
        ag = sb("ag", [P, D + 2], F32)
        at = [sb(f"at{a}", [128, KT, 2, P], F32R) for a in range(2)]
        gt = sb("gt", [2, 2, P], F32R)
        mt = [sb(f"mt{a}", [128, KT, 2, P], F32R) for a in range(2)]
        xt = Normed(k, sb, "gnx", x, mean, rstd, ident, 0)
        og = sb("og", [P, 2, D], F32)
        s_xf, s_xh, s_x1 = sem("xf"), sem("xh"), sem("x1")
        s_in = [sem(f"in{a}") for a in range(2)]
        s_ch, s_cl = sem("ch"), sem("cl")
        s_ag = sem("ag")
        s_dg = sem("dg")
        s_at = sem("at")
        s_ah, s_al = sem("ah"), sem("al")
        s_mp, s_mh, s_ml = sem("mp"), sem("mh"), sem("ml")
        s_u, s_ge, s_gx = sem("u"), sem("ge"), sem("gx")
        block = ctx.enter_context(nc.Block())
        LINKS = 6

        @block.sync
        def _(sp):
            w.load(sp)
            with sp.Fori(0, NT) as t:
                sp.wait_ge(s_cl, t + 1)
                sp.dma_start(cin[:, :, :], counts_d[ds(t, 1), :, :, :].rearrange("t p a d -> (t p) a d")).then_inc(s_in[0], 16)
                sp.wait_ge(s_dg, LINKS * t + 1)
                sp.dma_start(ein[:, :], esum_d[ds(t, 1), :, :].rearrange("t p f -> (t p) f")).then_inc(s_in[1], 16)

        @block.tensor
        def _(pe):
            pe.sem_inc(xt.s_used, 1)
            pe.sem_inc(s_ag, 1)
            xt.transposes(pe, 0)
            pe.wait_ge(s_x1, NT + 1)
            w.wait(pe)
            with pe.Fori(0, NP) as i:
                xt.wait(pe, i)
                xt.transposes(pe, i + 1)
                for h in range(2):
                    pe.wait_ge(s_cl, 2 * i + h + 2)
                    pe.wait_ge(s_dg, LINKS * (2 * i + h) + 1)
                    for n in range(NT):
                        for m, (a, b) in enumerate(((0, 0), (0, 1), (1, 0))):
                            pe.matmul(banks[:P, 2, :], cs[a][:, n, :], xa[b][:, n, :], start=n == 0 and m == 0,
                                      stop=n == NT - 1 and m == 2)
                    for n in range(NT):
                        for a in range(2):
                            ins = pe.matmul(banks[:P, 3, 0:2], cs[a][:, n, :], ones[:, :], start=n == 0 and a == 0,
                                            stop=n == NT - 1 and a == 1)
                    ins.then_inc(s_ag, 1)
                    pe.wait_ge(s_dg, LINKS * (2 * i + h + 1) + 1)
                    pe.wait_ge(s_al, 2 * i + h + 1)
                    for c in range(KT):
                        pe.transpose(banks[:, 4, c * P:(c + 1) * P], ag[:, c * 128:(c + 1) * 128], ident[:P, :P])
                    pe.transpose(banks[0:2, 5, 0:P], ag[:, D:D + 2], ident[:P, :P]).then_inc(s_at, 1)
                pe.wait_ge(s_al, 2 * i + 3)
                for f in range(KT):
                    pe.wait_ge(s_ml, i * KT + f + 1)
                    out = banks[:, 6 + f % 2, 0:2 * P]
                    product(pe, out, wms, at, feature_tile(f), range(KT), last=False)
                    g = gt[:, :, :].rearrange("p h n -> p (h n)")
                    for a in range(2):
                        ins = pe.matmul(out, wbs[a][:, 0, f * 128:(f + 1) * 128], g, start=False, stop=a == 1)
                    ins.then_inc(s_mp, 1)
                for h in range(2):
                    if h == 0:
                        pe.wait_ge(s_ml, (i + 1) * KT + 2)
                    pe.wait_ge(s_ge, 2 * i + h + 1)
                    out = banks[:P, 5, :]
                    product(pe, out, xt.parts(), wus, half_of(h), range(KT), last=False)
                    product(pe, out, mt, wus, lambda a, b, c: (a[:, c, h, :], b[:, KT + c, :]), range(KT), first=False,
                            last=False)
                    for a in range(2):
                        ins = pe.matmul(out, gt[:, h, :], wbs[a][:, 1, :], start=False, stop=a == 1)
                    ins.then_inc(s_u, 1)
                pe.wait_ge(s_u, 2 * i + 2)
                pe.wait_ge(s_ge, 2 * i + 3)
                pe.sem_inc(xt.s_used, 1)

        @block.scalar
        def _(act):
            act.sem_inc(s_ge, 1)
            for t in range(NT):
                act.wait_ge(s_xf, t + 1)
                act.copy(xa[0][:, t, :], xf[:, t % 2, :]).then_inc(s_xh, 1)
            w.high(act)
            xt.high(act, 0)
            with act.Fori(0, NP) as i:
                for h in range(2):
                    act.wait_ge(s_in[0], (2 * i + h) * 16 + 16)
                    act.wait_ge(s_ag, 2 * i + h + 1)
                    act.copy(cs[0][:, :, :], cin[:, :, :]).then_inc(s_ch, 1)
                    act.wait_ge(s_at, 2 * i + h + 1)
                    act.copy(at[0][:, :, h, :], banks[:, 4, 0:KT * P].rearrange("p (c n) -> p c n", n=P))
                    act.copy(gt[:, h, :], banks[0:2, 5, 0:P]).then_inc(s_ah, 1)
                for f in range(KT):
                    act.wait_ge(s_mp, KT * i + f + 1)
                    act.copy(mt[0][:, f, :, :].rearrange("p h n -> p (h n)"), banks[:, 6 + f % 2, 0:2 * P]).then_inc(s_mh, 1)
                for h in range(2):
                    act.wait_ge(s_u, 2 * i + h + 1)
                    act.activation(og[:, h, :], banks[:P, 5, :], ACT.Gelu).then_inc(s_ge, 1)
                xt.high(act, i + 1)

        @block.vector
        def _(dve):
            dve.sem_inc(s_cl, 1)
            dve.sem_inc(s_al, 1)
            dve.sem_inc(s_ml, 2)
            dve.sem_inc(s_dg, 1)
            for t in range(NT + 1):
                if t < NT:
                    if t >= 2:
                        dve.wait_ge(s_x1, t - 1)
                    dve.tensor_scalar(xf[:, t % 2, :], x[:, t, :], mean[:, t:t + 1], rstd[:, t:t + 1], ALU.subtract,
                                      ALU.mult).then_inc(s_xf, 1)
                if 1 <= t <= NT:
                    dve.wait_ge(s_xh, t)
                    dve.wait_ge(s_xf, t)
                    dve.tensor_tensor(xa[1][:, t - 1, :], xf[:, (t - 1) % 2, :], xa[0][:, t - 1, :].bitcast(F32),
                                      ALU.subtract).then_inc(s_x1, 1)
            dve.memset(ones[:, :].bitcast(F32), 1.0).then_inc(s_x1, 1)
            dve.wait_ge(s_x1, NT + 1)
            dve.sem_inc(s_gx, 1)
            dve.memset(ag[:, D + 1:D + 2], 1.0)
            xt.rows(dve, 0)
            w.low(dve)
            xt.low(dve, 0)
            with dve.Fori(0, NP) as i:
                xt.rows(dve, i + 1)
                for h in range(2):
                    t = 2 * i + h
                    dve.wait_ge(s_ch, t + 1)
                    dve.tensor_tensor(cs[1][:, :, :], cin[:, :, :], cs[0][:, :, :].bitcast(F32),
                                      ALU.subtract).then_inc(s_cl, 1)
                    n = [1]

                    def link(ins):
                        n[0] += 1
                        ins.then_inc(s_dg, 1)
                        dve.wait_ge(s_dg, LINKS * t + n[0])

                    dve.wait_ge(s_ag, t + 2)
                    dve.wait_ge(s_in[1], t * 16 + 16)
                    link(dve.tensor_copy(dg[:, 0:2], banks[:P, 3, 0:2]))
                    link(dve.tensor_scalar(dg[:, 2:3], dg[:, 0:1], 1.0, None, ALU.max))
                    link(dve.reciprocal(dg[:, 3:4], dg[:, 2:3]))
                    link(dve.tensor_tensor(ag[:, D:D + 1], dg[:, 0:1], dg[:, 3:4], ALU.mult))
                    link(dve.tensor_tensor(ag[:, 0:D], banks[:P, 2, :], ein[:, :], ALU.add))
                    link(dve.tensor_scalar(ag[:, 0:D], ag[:, 0:D], dg[:, 3:4], None, ALU.mult))
                    assert n[0] == LINKS + 1
                    dve.wait_ge(s_ah, t + 1)
                    dve.tensor_tensor(at[1][:, :, h, :], banks[:, 4, 0:KT * P].rearrange("p (c n) -> p c n", n=P),
                                      at[0][:, :, h, :].bitcast(F32), ALU.subtract).then_inc(s_al, 1)
                for f in range(KT):
                    dve.wait_ge(s_mh, KT * i + f + 1)
                    dve.tensor_tensor(mt[1][:, f, :, :].rearrange("p h n -> p (h n)"), banks[:, 6 + f % 2, 0:2 * P],
                                      mt[0][:, f, :, :].bitcast(F32).rearrange("p h n -> p (h n)"),
                                      ALU.subtract).then_inc(s_ml, 1)
                for h in range(2):
                    t = 2 * i + h
                    dve.wait_ge(s_gx, 4 * i + 1)
                    dve.tensor_scalar(xf[:, h, :], flat(x, t), mean[:, ds(t, 1)], rstd[:, ds(t, 1)], ALU.subtract,
                                      ALU.mult).then_inc(s_gx, 1)
                for h in range(2):
                    t = 2 * i + h
                    dve.wait_ge(s_gx, 4 * i + 3 + h)
                    dve.wait_ge(s_ge, t + 2)
                    dve.tensor_tensor(flat(x, t), xf[:, h, :], og[:, h, :], ALU.add).then_inc(s_gx, 1)
                xt.low(dve, i + 1)

    with ExitStack() as ctx:
        row = ctx.enter_context(nc.sbuf_tensor("gn_row", [P, 2, D], F32))
        s_row = k.sem("s_gn_row")
        s_fin = k.sem("s_gn_fin")
        m2 = ctx.enter_context(nc.sbuf_tensor("gn_m2", [P, NT + 2], F32))
        r2 = ctx.enter_context(nc.sbuf_tensor("gn_r2", [P, NT + 2], F32))
        statistics(k, "gn2", x, m2, r2)
        block = ctx.enter_context(nc.Block())

        @block.sync
        def _(sp):
            sp.dma_start(row[:, 0, :], gamma.partition_broadcast(P)).then_inc(s_row, 16)
            sp.dma_start(row[:, 1, :], beta.partition_broadcast(P)).then_inc(s_row, 16)

        @block.vector
        def _(dve):
            dve.wait_ge(s_row, 32)
            with dve.Fori(0, NP) as i:
                for step in range(4):
                    for h in range(2):
                        t = 2 * i + h
                        if step:
                            dve.wait_ge(s_fin, 8 * i + 2 * step - 1 + h)
                        if step == 0:
                            ins = dve.tensor_scalar(flat(x, t), flat(x, t), m2[:, ds(t, 1)], r2[:, ds(t, 1)],
                                                    ALU.subtract, ALU.mult)
                        elif step < 3:
                            ins = dve.tensor_tensor(flat(x, t), flat(x, t), row[:, step - 1, :],
                                                    (ALU.mult, ALU.add)[step - 1])
                        else:
                            ins = dve.tensor_tensor(flat(y, t), flat(y, t), flat(x, t), ALU.add)
                        ins.then_inc(s_fin, 1)


def pooled_phase(k, x, mean, rstd, ident, attn_w, attn_b, gate_w, gate_b, w1, b1_cols, w2, b2):
    nc, banks = k.nc, k.banks
    EX, HT, TOP = 8, 2, 2
    with ExitStack() as ctx:
        def sb(nm, shape, dt):
            return ctx.enter_context(nc.sbuf_tensor(f"po_{nm}", shape, dt))

        def sem(nm):
            return k.sem(f"s_po_{nm}")

        chosen = sb("chosen", [1, TOP], I32)
        gcol = sb("gcol", [P, TOP], F32)
        ones = sb("ones", [P, 128], F32)

        with ExitStack() as inner:
            def sbi(nm, shape, dt):
                return inner.enter_context(nc.sbuf_tensor(f"po_{nm}", shape, dt))

            aw = sbi("aw", [P, D], F32)
            ab = sbi("ab", [P, 1], F32)
            gw = sbi("gw", [128, KT, EX], F32)
            gb = sbi("gb", [1, EX], F32)
            xa = sbi("xa", [P, NT, D], F32)
            xw = sbi("xw", [P, 2, D], F32)
            sc = sbi("sc", [P, 2, NT], F32)
            top = sbi("top", [128, 2], F32)
            glob = sbi("glob", [128, 1], F32)
            tot = sbi("tot", [128, 1], F32)
            pl = sbi("pl", [128, KT], F32)
            r1 = sbi("r1", [1, 8, EX], F32)
            r0 = sbi("r0", [1, 8], F32)
            gn = sbi("gn", [1, TOP], F32)
            iota8 = sbi("iota8", [1, EX], F32)
            s_in, s_c, s_x, s_m, s_w, s_s = sem("in"), sem("c"), sem("x"), sem("m"), sem("w"), sem("s")
            s_all, s_e, s_pl, s_gl, s_ge, s_gb = sem("all"), sem("e"), sem("pl"), sem("gl"), sem("ge"), sem("gb")
            block = inner.enter_context(nc.Block())

            @block.sync
            def _(sp):
                sp.dma_start(aw[:, :], attn_w.partition_broadcast(P)).then_inc(s_in, 16)
                sp.dma_start(ab[:, :], attn_b.partition_broadcast(P)).then_inc(s_in, 16)
                sp.dma_start(gw[:, :, :], gate_w.rearrange("(c p) e -> p c e", p=128)).then_inc(s_in, 16)
                sp.dma_start(gb[:, :], gate_b.partition_broadcast(1)).then_inc(s_in, 16)

            @block.gpsimd
            def _(pool):
                pool.memset(ones[:, :], 1.0)
                pool.iota(iota8[:, :], [[1, EX]], base=0, channel_multiplier=0,
                          allow_small_or_imprecise_dtypes=True).then_inc(s_c, 1)
                pool.wait_ge(s_s, 4)
                pool.partition_all_reduce(glob[:, :], top[:, 0:1], 128, bass.bass_isa.ReduceOp.max).then_inc(s_all, 1)

            @block.vector
            def _(dve):
                dve.wait_ge(s_in, 64)
                for t in range(NT + 2):
                    if t < NT:
                        dve.tensor_scalar(xa[:, t, :], x[:, t, :], mean[:, t:t + 1], rstd[:, t:t + 1], ALU.subtract,
                                          ALU.mult).then_inc(s_x, 1)
                    if t >= 2:
                        dve.wait_ge(s_m, t - 1)
                        dve.tensor_reduce(sc[:, 0, t - 2:t - 1], xw[:, t % 2, :], AX.X, ALU.add).then_inc(s_w, 1)
                    if 1 <= t <= NT:
                        dve.wait_ge(s_x, t)
                        if t >= 3:
                            dve.wait_ge(s_w, t - 2)
                        dve.tensor_tensor(xw[:, (t - 1) % 2, :], xa[:, t - 1, :], aw[:, :], ALU.mult).then_inc(s_m, 1)
                dve.memset(top[:, :], -3e38).then_inc(s_w, 1)
                dve.wait_ge(s_w, NT + 1)
                link = chain(dve, s_s)
                link(dve.tensor_scalar(sc[:, 0, :], sc[:, 0, :], ab[:, :], None, ALU.add))
                link(dve.tensor_reduce(top[:P, 0:1], sc[:, 0, :], AX.X, ALU.max))
                link(dve.tensor_copy(r0[:, 0:1], gb[:, 0:1]))
                link(dve.tensor_copy(r0[:, 1:2], gb[:, 0:1]))
                dve.wait_ge(s_all, 1)
                link(dve.tensor_scalar(top[:, 1:2], glob[:, :], -1.0, None, ALU.mult))
                dve.wait_ge(s_pl, 1)
                link(dve.reciprocal(tot[:, :], banks[:, 1, 0:1]))
                link(dve.tensor_scalar(pl[:, :], banks[:, 0, 0:KT], tot[:, :], None, ALU.mult))
                dve.wait_ge(s_gl, 1)
                link(dve.tensor_tensor(r1[:, 0], banks[0:1, 2, 0:EX], gb[:, :], ALU.add))
                link(dve.tensor_reduce(r0[:, 0:1], r1[:, 0], AX.X, ALU.max))
                link(dve.tensor_scalar(r1[:, 1], r1[:, 0], r0[:, 0:1], None, ALU.subtract))
                dve.wait_ge(s_ge, 1)
                link(dve.tensor_reduce(r0[:, 1:2], r1[:, 2], AX.X, ALU.add))
                link(dve.reciprocal(r0[:, 2:3], r0[:, 1:2]))
                link(dve.tensor_scalar(r1[:, 3], r1[:, 2], r0[:, 2:3], None, ALU.mult))
                dve.wait_ge(s_c, 1)
                for j, seen in ((0, r1[:, 3]), (1, r1[:, 4])):
                    best, least = r0[:, 3 + j:4 + j], r0[:, 5:6]
                    link(dve.tensor_reduce(best, seen, AX.X, ALU.max))
                    link(dve.tensor_scalar(r1[:, 5], seen, best, float(EX), ALU.is_lt, ALU.mult))
                    link(dve.tensor_tensor(r1[:, 5], r1[:, 5], iota8[:, :], ALU.add))
                    link(dve.tensor_reduce(least, r1[:, 5], AX.X, ALU.min))
                    link(dve.tensor_copy(chosen[:, j:j + 1], least))
                    if j == 0:
                        link(dve.tensor_scalar(r1[:, 6], iota8[:, :], least, -2.0, ALU.is_equal, ALU.mult))
                        link(dve.tensor_tensor(r1[:, 4], r1[:, 6], r1[:, 3], ALU.add))
                link(dve.tensor_tensor(r0[:, 6:7], r0[:, 3:4], r0[:, 4:5], ALU.add))
                link(dve.tensor_scalar(r0[:, 6:7], r0[:, 6:7], 1e-9, None, ALU.add))
                link(dve.reciprocal(r0[:, 7:8], r0[:, 6:7]))
                link(dve.tensor_scalar(gn[:, :], r0[:, 3:5], r0[:, 7:8], None, ALU.mult))
                dve.sem_inc(s_gb, 1)
                dve.wait_ge(s_gb, 2)
                dve.tensor_copy(gcol[:, :], banks[:P, 3, 0:TOP])

            @block.scalar
            def _(act):
                act.wait_ge(s_s, 5)
                act.activation(sc[:, 1, :], sc[:, 0, :], ACT.Exp, bias=top[:P, 1:2]).then_inc(s_e, 1)
                act.wait_ge(s_s, 10)
                act.activation(r1[:, 2], r1[:, 1], ACT.Exp).then_inc(s_ge, 1)

            @block.tensor
            def _(pe):
                pe.wait_ge(s_c, 1)
                pe.wait_ge(s_e, 1)
                for c in range(KT):
                    for t in range(NT):
                        pe.matmul(banks[:, 0, c:c + 1], xa[:, t, c * 128:(c + 1) * 128], sc[:, 1, t:t + 1],
                                  start=t == 0, stop=t == NT - 1)
                for t in range(NT):
                    ins = pe.matmul(banks[:, 1, 0:1], ones[:, :], sc[:, 1, t:t + 1], start=t == 0, stop=t == NT - 1)
                ins.then_inc(s_pl, 1)
                pe.wait_ge(s_s, 7)
                for c in range(KT):
                    ins = pe.matmul(banks[0:1, 2, 0:EX], pl[:, c:c + 1], gw[:, c, :], start=c == 0, stop=c == KT - 1)
                ins.then_inc(s_gl, 1)
                pe.wait_ge(s_gb, 1)
                pe.matmul(banks[:P, 3, 0:TOP], ones[0:1, 0:P], gn[:, :], start=True, stop=True).then_inc(s_gb, 1)

        FT = TOP * HT
        v1 = [sb(f"v1{a}", [128, KT, FT * 128], F32R) for a in range(2)]
        v2 = [sb(f"v2{a}", [128, FT, D], F32R) for a in range(2)]
        vb = [sb(f"vb{a}", [1, TOP, D], F32R) for a in range(2)]
        b1 = sb("b1", [128, FT], F32)
        one_r = sb("one_r", [1, P + 1], F32R)

        def source(a, j, form, **sizes):
            return lambda e: a[ds(e[j], 1)].rearrange(form, **sizes)

        pieces = []
        for j in range(TOP):
            c = slice(j * HT * 128, (j + 1) * HT * 128)
            pieces.append((source(w1, j, "a (c p) f -> p (a c) f", p=128), v1[0][:, :, c], v1[1][:, :, c]))
        for j in range(TOP):
            c = slice(j * HT, (j + 1) * HT)
            pieces.append((source(w2, j, "a (c p) f -> p (a c) f", p=128), v2[0][:, c, :], v2[1][:, c, :]))
            pieces.append((source(b2, j, "a f -> a f"), vb[0][:, j, :], vb[1][:, j, :]))
        w = Weights(k, sb, "po", pieces)
        xt = Normed(k, sb, "pox", x, mean, rstd, ident, 0)
        hf = sb("hf", [128, 2, 2 * P], F32)
        ht = [sb(f"ht{a}", [128, FT, 2, P], F32R) for a in range(2)]
        eo = sb("eo", [P, 2, D], F32)
        s_b1, s_one = sem("b1"), sem("one")
        s_h = sem("h")
        s_f = sem("f")
        s_hh, s_hl = sem("hh"), sem("hl")
        s_o = sem("o")
        s_g = sem("g")
        s_y = sem("y")
        block = ctx.enter_context(nc.Block())

        @block.sync
        def _(sp):
            e = [sp.value_load(chosen[0:1, j:j + 1], min_val=0, max_val=EX - 1) for j in range(TOP)]
            for j in range(TOP):
                sp.dma_start(b1[:, j * HT:(j + 1) * HT], b1_cols[ds(e[j], 1)].rearrange("a p f -> (a p) f"))\
                  .then_inc(s_b1, 16)
            w.load(sp, e)

        @block.tensor
        def _(pe):
            pe.sem_inc(xt.s_used, 1)
            xt.transposes(pe, 0)
            w.wait(pe)
            pe.wait_ge(s_one, 1)
            with pe.Fori(0, NP) as i:
                xt.wait(pe, i)
                xt.transposes(pe, i + 1)
                for f in range(FT):
                    pe.wait_ge(s_hl, FT * i + f + 1)
                    product(pe, banks[:, 2 + f % 2, 0:2 * P], v1, xt.parts(), feature_tile(f),
                            range(KT)).then_inc(s_h, 1)
                pe.wait_ge(s_h, FT * (i + 1))
                pe.sem_inc(xt.s_used, 1)
                pe.wait_ge(s_hl, FT * (i + 1) + 2)
                for n in range(2 * TOP):
                    h, j = divmod(n, TOP)
                    pe.wait_ge(s_g, 2 * TOP * i + n + 1)
                    out = banks[:P, 4 + n % 2, :]
                    product(pe, out, ht, v2, half_of(h), range(j * HT, (j + 1) * HT), last=False)
                    for a in range(2):
                        ins = pe.matmul(out, one_r[:, 0:P], vb[a][:, j, :], start=False, stop=a == 1)
                    ins.then_inc(s_o, 1)

        @block.scalar
        def _(act):
            act.sem_inc(s_g, 2)
            w.high(act)
            xt.high(act, 0)
            act.wait_ge(s_b1, 16 * TOP)
            with act.Fori(0, NP) as i:
                for f in range(FT):
                    act.wait_ge(s_h, FT * i + f + 1)
                    act.wait_ge(s_hl, FT * i + f + 1)
                    act.activation(hf[:, f % 2, :], banks[:, 2 + f % 2, 0:2 * P], ACT.Gelu,
                                   bias=b1[:, f:f + 1]).then_inc(s_f, 1)
                    act.wait_ge(s_f, FT * i + f + 1)
                    act.copy(ht[0][:, f, :, :].rearrange("p h n -> p (h n)"), hf[:, f % 2, :]).then_inc(s_hh, 1)
                xt.high(act, i + 1)
                for n in range(2 * TOP):
                    act.wait_ge(s_o, 2 * TOP * i + n + 1)
                    act.wait_ge(s_y, 2 * TOP * i + n + 1)
                    act.activation(eo[:, n % 2, :], banks[:P, 4 + n % 2, :], ACT.Gelu).then_inc(s_g, 1)

        @block.vector
        def _(dve):
            dve.sem_inc(s_hl, 2)
            dve.sem_inc(s_y, 2)
            dve.memset(one_r[:, :].bitcast(F32), 1.0).then_inc(s_one, 1)
            xt.rows(dve, 0)
            w.low(dve)
            xt.low(dve, 0)
            with dve.Fori(0, NP) as i:
                xt.rows(dve, i + 1)
                for f in range(FT):
                    dve.wait_ge(s_hh, FT * i + f + 1)
                    dve.tensor_tensor(ht[1][:, f, :, :].rearrange("p h n -> p (h n)"), hf[:, f % 2, :],
                                      ht[0][:, f, :, :].bitcast(F32).rearrange("p h n -> p (h n)"),
                                      ALU.subtract).then_inc(s_hl, 1)
                xt.low(dve, i + 1)
                for n in range(2 * TOP):
                    h, j = divmod(n, TOP)
                    t = 2 * i + h
                    dve.wait_ge(s_g, 2 * TOP * i + n + 3)
                    if j:
                        dve.wait_ge(s_y, 2 * TOP * i + n + 2)
                    dve.scalar_tensor_tensor(flat(x, t), eo[:, n % 2, :], gcol[:, j:j + 1], flat(x, t), ALU.mult,
                                             ALU.add).then_inc(s_y, 1)


def graph_transformer(nc, x_in, src, dst, edge_attr, ident_in, mask_in, sel_in, mean_in,
                      wq, wk, wv, bn_gamma, bn_beta, mix0_wqkv, mix0_wout, mix0_bout,
                      f0_gate, f0_w1, f0_sw1, f0_w2, f0_sw2, f0_b1, f0_b2,
                      gn_wm, gn_wu, gn_bias, gn_gamma, gn_beta,
                      mix1_wqkv, mix1_b, mix1_bq, mix1_wout, mix1_bout, mix1_gamma, mix1_beta,
                      f1_attn_w, f1_attn_b, f1_gate_w, f1_gate_b, f1_w1, f1_b1, f1_w2, f1_b2, out):
    counts_d = nc.dram_tensor("edge_counts", [NT, P, NT, P], U16).ap()
    esum_d = nc.dram_tensor("edge_sums", [NT, P, D], F32).ap()
    with ExitStack() as ctx:
        k = Kernel(nc, ctx)
        ident = k.keep("ident", [128, 128], F32)
        mask = k.keep("mask", [128, 128], F32)
        ones_n = k.keep("ones_n", [128, 128], F32)
        mean = k.keep("mean", [P, NT + 2], F32)
        rstd = k.keep("rstd", [P, NT + 2], F32)
        again = k.keep("again", [P, NT + 2], F32)
        s_const = k.sem("s_const")
        s_x = k.sem("s_x")
        s_store = k.sem("s_store")

        with ExitStack() as outer:
            counts = outer.enter_context(nc.sbuf_tensor("counts", [P, NT, NT, P], U16))
            with ExitStack() as inner:
                esum = inner.enter_context(nc.sbuf_tensor("esum", [P, NT, D], F32))
                with nc.Block() as block:
                    @block.sync
                    def _(sp):
                        sp.dma_start(ident[:, :], ident_in).then_inc(s_const, 16)
                        sp.dma_start(mask[:, :], mask_in).then_inc(s_const, 16)
                        sp.dma_start(ones_n[:, :], mean_in).then_inc(s_const, 16)
                        sp.wait_ge(s_const, 48)
                edge_phase(k, src, dst, edge_attr, counts, esum, ident)
                with nc.Block() as block:
                    @block.sync
                    def _(sp):
                        for t in range(NT):
                            sp.dma_start(counts_d[t], counts[:, t, :, :]).then_inc(s_store, 16)
                            sp.dma_start(esum_d[t], esum[:, t, :]).then_inc(s_store, 16)
                        sp.wait_ge(s_store, 2 * NT * 16)
        with ExitStack() as rows:
            x = rows.enter_context(nc.sbuf_tensor("rows_x", [P, NT + 2, D], F32))
            y = rows.enter_context(nc.sbuf_tensor("rows_y", [P, NT + 2, D], F32))
            with ExitStack() as inner:
                counts = inner.enter_context(nc.sbuf_tensor("counts_back", [P, NT, NT, P], U16))
                with nc.Block() as block:
                    @block.sync
                    def _(sp):
                        for t in range(NT):
                            sp.dma_start(x[:, t, :], x_in[t * P:(t + 1) * P, :]).then_inc(s_x, 16)
                            sp.dma_start(counts[:, t, :, :], counts_d[t]).then_inc(s_x, 16)
                        sp.wait_ge(s_x, 2 * NT * 16)

                    @block.gpsimd
                    def _(pool):
                        pool.memset(x[:, NT:, :], 0.0)
                        pool.memset(y[:, NT:, :], 0.0)
                statistics(k, "st0", x, mean, rstd)
                attention_phase(k, x, y, mean, rstd, counts, ident, wq, wk, wv)
            batchnorm_phase(k, x, y, ones_n, bn_gamma, bn_beta)
            k.clear()
            mix_phase(k, "mix0", x, y, mean, rstd, ident, mask, mix0_wqkv, None, None, mix0_wout, mix0_bout)
            x, y = y, x
            statistics(k, "st1", x, mean, rstd)
            experts_phase(k, x, mean, rstd, ident, sel_in, f0_gate, f0_w1, f0_sw1, f0_w2, f0_sw2, f0_b1, f0_b2)
            k.clear()
            statistics(k, "st2", x, mean, rstd, again)
            mix_phase(k, "mix1", x, y, mean, again, ident, mask, mix1_wqkv, mix1_b, mix1_bq, mix1_wout, mix1_bout,
                      affine=(mix1_gamma, mix1_beta), base=(mean, rstd))
            graph_phase(k, x, y, mean, rstd, ident, counts_d, esum_d, gn_wm, gn_wu, gn_bias, gn_gamma, gn_beta)
            statistics(k, "st3", y, mean, rstd)
            pooled_phase(k, y, mean, rstd, ident, f1_attn_w, f1_attn_b, f1_gate_w, f1_gate_b, f1_w1, f1_b1, f1_w2, f1_b2)
            s_out = k.sem("s_out")
            with nc.Block() as block:
                @block.sync
                def _(sp):
                    for t in range(NT):
                        sp.dma_start(out[t * P:(t + 1) * P, :], y[:, t, :]).then_inc(s_out, 16)
                    sp.wait_ge(s_out, NT * 16)


def lay_out(i):
    def swap(name, *axes):
        return i[name].transpose(*axes) if axes else i[name].T

    def edges(name, pad):
        a = np.pad(i[name], (0, G * GE - E), constant_values=pad)
        return a.reshape(G * GC, EC).T

    bm, bu = i["L1_gnn_bm"], i["L1_gnn_bu"]
    zero = np.zeros_like(bm)
    return {
        "x": i["x"],
        "src": edges("src", 4095),
        "dst": edges("dst", N - 1),
        "edge_attr": np.pad(i["edge_attr_512"], ((0, G * GE - E), (0, 0))),
        "identity": np.eye(128, dtype=np.float32),
        "head_mask": np.kron(np.eye(2), np.ones((DH, DH))).astype(np.float32),
        "selector": np.repeat(np.eye(8, dtype=np.float32), 128, 1),
        "mean_of_nodes": np.full((128, 128), 1.0 / N, np.float32),
        "wq": i["L0_gnn_Wq"], "wk": i["L0_gnn_Wk"], "wv": i["L0_gnn_Wv"],
        "bn_gamma": i["L0_gnn_bn_gamma"], "bn_beta": i["L0_gnn_bn_beta"],
        "mix0_wqkv": i["L0_mix_w_qkv"], "mix0_wout": i["L0_mix_w_out"], "mix0_bout": i["L0_mix_b_out"],
        "f0_gate": swap("L0_ffn_gate_w"),
        "f0_w1": swap("L0_ffn_w1", 1, 0, 2).reshape(D, -1),
        "f0_sw1": i["L0_ffn_sw1"], "f0_w2": i["L0_ffn_w2"], "f0_sw2": i["L0_ffn_sw2"],
        "f0_b1": np.concatenate([swap("L0_ffn_b1"), i["L0_ffn_sb1"].reshape(4, 128).T], 1),
        "f0_b2": np.concatenate([i["L0_ffn_b2"], i["L0_ffn_sb2"][None]]),
        "gn_wm": swap("L1_gnn_Wm"), "gn_wu": swap("L1_gnn_Wu"),
        "gn_bias": np.stack([np.stack([bm, zero]), np.stack([zero, bu])]),
        "gn_gamma": i["L1_gnn_gamma"], "gn_beta": i["L1_gnn_beta"],
        "mix1_wqkv": swap("L1_mix_qkv_w"), "mix1_b": i["L1_mix_qkv_b"],
        "mix1_bq": i["L1_mix_qkv_b"][:D].reshape(4, 128).T,
        "mix1_wout": swap("L1_mix_out_w"), "mix1_bout": i["L1_mix_out_b"],
        "mix1_gamma": i["L1_mix_ln_gamma"], "mix1_beta": i["L1_mix_ln_beta"],
        "f1_attn_w": i["L1_ffn_attn_w"].reshape(D), "f1_attn_b": i["L1_ffn_attn_b"],
        "f1_gate_w": i["L1_ffn_gate_w"], "f1_gate_b": i["L1_ffn_gate_b"],
        "f1_w1": i["L1_ffn_w1"], "f1_b1": swap("L1_ffn_b1").reshape(2, 128, 8).transpose(2, 1, 0),
        "f1_w2": i["L1_ffn_w2"], "f1_b2": i["L1_ffn_b2"],
    }


def kernel(**inputs):
    import concourse.bacc as _bacc
    from concourse.bass_utils import run_bass_kernel_spmd as _run

    nc = _bacc.Bacc("TRN2", target_bir_lowering=False, num_devices=1)
    arrays, args = {}, []
    for name, a in lay_out({name: np.asarray(a) for name, a in inputs.items()}).items():
        arrays[f"in_{name}_dram"] = np.ascontiguousarray(a)
        args.append(nc.dram_tensor(f"in_{name}_dram", a.shape, mybir.dt.from_np(a.dtype), kind="ExternalInput").ap())
    args.append(nc.dram_tensor("out_dram", (N, D), F32, kind="ExternalOutput").ap())
    graph_transformer(nc, *args)
    return _run(nc, [arrays], core_ids=[0]).results[0]["out_dram"]
```

```python
import concourse.bass as bass
from concourse import mybir
from contextlib import ExitStack

import numpy as np

F32 = mybir.dt.float32
F32R = mybir.dt.float32r
BF16 = mybir.dt.bfloat16
FP16 = mybir.dt.float16
I32 = mybir.dt.int32
U32 = mybir.dt.uint32
U16 = mybir.dt.uint16
ALU = mybir.AluOpType
ACT = mybir.ActivationFunctionType
AX = mybir.AxisListType
ds = bass.ds

N = 1250
D = 512
E = 41250
H = 8
DH = D // H
P = 125
NT = N // P
NP = NT // 2
KT = D // 128
EC = 128
GC = 6
GE = GC * EC
G = -(-E // GE)
STAGE = 2 * D
POOL_LO = (1, 3, 5)
EPS = 1e-5


class Kernel:

    def __init__(self, nc, ctx):
        self.nc, self.ctx = nc, ctx
        self.banks = ctx.enter_context(nc.psum_tensor("banks", [128, 8, 512], F32))
        self.sems = []

    def sem(self, name):
        self.sems.append(self.nc.alloc_semaphore(name=name))
        return self.sems[-1]

    def clear(self):
        self.nc.clear_and_free_semaphores(self.sems)
        self.nc.all_engine_barrier()
        self.sems = []

    def keep(self, name, shape, dt):
        return self.ctx.enter_context(self.nc.sbuf_tensor(name, shape, dt))


def edge_phase(k, src, dst, edge_attr, counts, esum, deg, ident):
    nc = k.nc
    ctx = ExitStack()
    with ctx:
        def sb(name, shape, dt):
            return ctx.enter_context(nc.sbuf_tensor(name, shape, dt))

        SW = 418
        idx_i = sb("idx_i", [128, 2, G * GC], I32)
        dst_f = sb("dst_f", [128, G * GC], F32)
        src_f = sb("src_f", [128, G * GC], F32)
        gext = sb("gext", [128, 2, G], F32)
        gall = sb("gall", [128, 2, G], F32)
        tcol = sb("tcol", [1, 2, NT, G], F32)
        gnum = sb("gnum", [1, 2, NT, G], F32)
        tmask = sb("tmask", [1, 3, NT, G], F32)
        tlim = sb("tlim", [1, 6, NT], F32)
        tab = sb("tab", [1, 3, NT], I32)
        iota_s = sb("iota_s", [128, 3 * SW], FP16)
        iota_t = sb("iota_t", [128, NT, P + 1], FP16)
        raw = sb("raw", [128, GC, D], F32)
        e_hi = sb("e_hi", [128, GC, D], F32R)
        e_lo = sb("e_lo", [128, GC, D], F32R)
        oh_s = sb("oh_s", [128, GC, 3 * SW], BF16)
        oh_d = sb("oh_d", [128, GC, P + 1], F32R)
        oh_db = sb("oh_db", [128, GC, P + 1], BF16)
        zero_b = sb("zero_b", [128, D], BF16)
        ct = sb("ct", [128, 3 * SW], F32)

        s_idx = k.sem("s_idx")
        s_iota = k.sem("s_iota")
        s_prep = k.sem("s_prep")
        s_all = k.sem("s_all")
        s_tab = k.sem("s_tab")
        s_raw = [k.sem(f"s_raw{c}") for c in range(GC)]
        s_hi = [k.sem(f"s_hi{c}") for c in range(GC)]
        s_lo = [k.sem(f"s_lo{c}") for c in range(GC)]
        s_oh = [k.sem(f"s_oh{c}") for c in range(GC)]
        s_use = [k.sem(f"s_use{c}") for c in range(GC)]
        s_fin = k.sem("s_fin")
        s_ct = k.sem("s_ct")
        s_es = k.sem("s_es")
        s_deg = k.sem("s_deg")
        s_tr = k.sem("s_tr")
        s_tre = k.sem("s_tre")

        banks = k.banks
        block = ctx.enter_context(nc.Block())
        edge_h = edge_attr.rearrange("(c p) f -> c p f", p=EC)

        def visits(eng, t):
            v0 = eng.value_load(tab[0:1, 0, ds(t, 1)], min_val=0, max_val=NT * G)
            v1 = eng.value_load(tab[0:1, 1, ds(t, 1)], min_val=1, max_val=NT * G)
            return v0, v1

        @block.sync
        def _(sp):
            sp.dma_start(idx_i[:, 0, :], src).then_inc(s_idx, 16)
            sp.dma_start(idx_i[:, 1, :], dst).then_inc(s_idx, 16)
            sp.wait_ge(s_tab, 1)
            with sp.Fori(0, NT) as t:
                v0, v1 = visits(sp, t)
                shift = sp.value_load(tab[0:1, 2, ds(t, 1)], min_val=0, max_val=2 * NT * G)
                with sp.Fori(v0, v1) as v:
                    g = sp.snap(nc.s_assert_within(v + shift - NT * G, 0, G - 1))
                    for c in range(GC):
                        sp.wait_ge(s_lo[c], v + 1)
                        sp.dma_start(raw[:, c, :], edge_h[ds(GC * g + c, 1), :, :].rearrange("a p f -> (a p) f"))\
                          .then_inc(s_raw[c], 16)

        @block.gpsimd
        def _(pool):
            pool.iota(iota_s[:, :], [[1, 3 * SW]], base=0, channel_multiplier=0,
                      allow_small_or_imprecise_dtypes=True)
            pool.iota(iota_t[:, :, :], [[P, NT], [1, P + 1]], base=0, channel_multiplier=0,
                      allow_small_or_imprecise_dtypes=True)
            pool.iota(tcol[:, 0, :, :], [[P, NT], [0, G]], base=0, channel_multiplier=0,
                      allow_small_or_imprecise_dtypes=True)
            pool.iota(tcol[:, 1, :, :], [[P, NT], [0, G]], base=P, channel_multiplier=0,
                      allow_small_or_imprecise_dtypes=True)
            pool.iota(gnum[:, 0, :, :], [[0, NT], [1, G]], base=1, channel_multiplier=0,
                      allow_small_or_imprecise_dtypes=True)
            pool.iota(gnum[:, 1, :, :], [[0, NT], [-1, G]], base=G, channel_multiplier=0,
                      allow_small_or_imprecise_dtypes=True).then_inc(s_iota, 1)
            pool.wait_ge(s_prep, 5)
            pool.partition_all_reduce(gall[:, :, :].rearrange("p a g -> p (a g)"),
                                      gext[:, :, :].rearrange("p a g -> p (a g)"), 128,
                                      bass.bass_isa.ReduceOp.max).then_inc(s_all, 1)
            for c in POOL_LO:
                pool.sem_inc(s_lo[c], 1)
            pool.wait_ge(s_tab, 1)
            with pool.Fori(0, NT) as t:
                v0, v1 = visits(pool, t)
                with pool.Fori(v0, v1) as v:
                    for c in POOL_LO:
                        pool.wait_ge(s_hi[c], v + 1)
                        pool.wait_ge(s_use[c], v + 1)
                        pool.tensor_tensor(e_lo[:, c, :], raw[:, c, :], e_hi[:, c, :].bitcast(F32),
                                           ALU.subtract).then_inc(s_lo[c], 1)

        @block.scalar
        def _(act):
            act.sem_inc(s_deg, 1)
            act.sem_inc(s_ct, 1)
            act.sem_inc(s_tre, 1)
            act.wait_ge(s_tab, 1)
            with act.Fori(0, NT) as t:
                v0, v1 = visits(act, t)
                with act.Fori(v0, v1) as v:
                    for c in range(GC):
                        act.wait_ge(s_raw[c], v * 16 + 16)
                        act.wait_ge(s_use[c], v + 1)
                        act.copy(e_hi[:, c, :], raw[:, c, :]).then_inc(s_hi[c], 1)
                act.wait_ge(s_fin, t + 1)
                act.wait_ge(s_tr, t + 1)
                act.wait_ge(s_deg, t + 1)
                act.copy(ct[:P, :].rearrange("p (b f) -> p b f", b=3), banks[:P, 0:3, 0:SW]).then_inc(s_ct, 1)
                act.wait_ge(s_tr, t + 2)
                act.copy(counts[:, ds(t, 1), 0:8, :].rearrange("p t (b a) f -> p (t b) (a f)", b=2),
                               banks[:P, 4:6, 0:4 * P])
                act.copy(counts[:, ds(t, 1), 8:NT, :].rearrange("p t a f -> p (t a f)"),
                               banks[:P, 6, 0:2 * P]).then_inc(s_tre, 1)

        @block.vector
        def _(dve):
            dve.wait_ge(s_idx, 32)
            dve.tensor_copy(src_f[:, :], idx_i[:, 0, :]).then_inc(s_prep, 1)
            dve.tensor_copy(dst_f[:, :], idx_i[:, 1, :]).then_inc(s_prep, 1)
            dve.memset(zero_b[:, :], 0.0).then_inc(s_prep, 1)
            dve.wait_ge(s_prep, 3)
            dg = dst_f[:, :].rearrange("p (g c) -> p g c", c=GC)
            dve.tensor_reduce(gext[:, 0, :], dg, AX.X, ALU.max).then_inc(s_prep, 1)
            dve.tensor_reduce(gext[:, 1, :], dg, AX.X, ALU.min, negate=True).then_inc(s_prep, 1)
            dve.wait_ge(s_all, 1)
            dve.wait_ge(s_iota, 1)
            step = [5]

            def link(ins):
                step[0] += 1
                ins.then_inc(s_prep, 1)
                dve.wait_ge(s_prep, step[0])

            gmax = gall[0:1, 0:1, :].to_broadcast([1, NT, G])
            gmin = gall[0:1, 1:2, :].to_broadcast([1, NT, G])
            link(dve.tensor_tensor(tmask[:, 0], gmax, tcol[:, 0], ALU.is_ge))
            link(dve.scalar_tensor_tensor(tmask[:, 1], gmin, -1.0, tcol[:, 1], ALU.mult, ALU.is_lt))
            link(dve.tensor_tensor(tmask[:, 2], tmask[:, 0], tmask[:, 1], ALU.mult))
            link(dve.tensor_tensor(tmask[:, 0], tmask[:, 2], gnum[:, 0], ALU.mult))
            link(dve.tensor_tensor(tmask[:, 1], tmask[:, 2], gnum[:, 1], ALU.mult))
            hi, lo, cnt, one, v1, v0 = (tlim[:, i, :] for i in range(6))
            link(dve.tensor_reduce(hi, tmask[:, 0], AX.X, ALU.max))
            link(dve.tensor_reduce(lo, tmask[:, 1], AX.X, ALU.max))
            link(dve.tensor_scalar(lo, lo, -1.0, float(G), ALU.mult, ALU.add))
            link(dve.tensor_scalar(lo, lo, float(G - 1), None, ALU.min))
            link(dve.tensor_tensor(cnt, hi, lo, ALU.subtract))
            link(dve.tensor_scalar(cnt, cnt, 1.0, None, ALU.max))
            link(dve.memset(one, 1.0))
            link(dve.tensor_tensor_scan(v1, one, cnt, 0.0, ALU.mult, ALU.add))
            link(dve.tensor_tensor(v0, v1, cnt, ALU.subtract))
            link(dve.tensor_tensor(lo, lo, v0, ALU.subtract))
            link(dve.tensor_copy(tab[:, 0, :], v0))
            link(dve.tensor_copy(tab[:, 1, :], v1))
            link(dve.tensor_scalar(tab[:, 2, :], lo, float(NT * G), None, ALU.add))
            for c in range(GC):
                if c not in POOL_LO:
                    dve.sem_inc(s_lo[c], 1)
            dve.sem_inc(s_es, 1)
            dve.sem_inc(s_tab, 1)
            with dve.Fori(0, NT) as t:
                v0, v1 = visits(dve, t)
                shift = dve.value_load(tab[0:1, 2, ds(t, 1)], min_val=0, max_val=2 * NT * G)
                with dve.Fori(v0, v1) as v:
                    g = dve.snap(nc.s_assert_within(v + shift - NT * G, 0, G - 1))
                    for c in range(GC):
                        chunk = ds(g * GC + c, 1)
                        dve.wait_ge(s_use[c], v + 1)
                        dve.tensor_scalar(oh_s[:, c, :], iota_s[:, :], src_f[:, chunk], None, ALU.is_equal)
                        tile_nodes = iota_t[:, ds(t, 1), :].rearrange("p a f -> p (a f)")
                        dve.tensor_scalar(oh_d[:, c, :], tile_nodes, dst_f[:, chunk], None, ALU.is_equal)
                        dve.tensor_scalar(oh_db[:, c, :], tile_nodes, dst_f[:, chunk], None,
                                          ALU.is_equal).then_inc(s_oh[c], 1)
                        if c not in POOL_LO:
                            dve.wait_ge(s_hi[c], v + 1)
                            dve.tensor_tensor(e_lo[:, c, :], raw[:, c, :], e_hi[:, c, :].bitcast(F32),
                                              ALU.subtract).then_inc(s_lo[c], 1)
                dve.wait_ge(s_fin, t + 1)
                dve.wait_ge(s_ct, t + 2)
                dve.tensor_reduce(deg[:, ds(t, 1)], ct[:P, :], AX.X, ALU.add).then_inc(s_deg, 1)
                dve.tensor_copy(esum[:, ds(t, 1), :].rearrange("p a f -> p (a f)"), banks[:P, 3, :]).then_inc(s_es, 1)

        @block.tensor
        def _(pe):
            for c in range(GC):
                pe.sem_inc(s_use[c], 1)
            pe.sem_inc(s_tr, 1)
            pe.wait_ge(s_tab, 1)
            with pe.Fori(0, NT) as t:
                v0, v1 = visits(pe, t)
                pe.wait_ge(s_ct, t + 1)
                pe.wait_ge(s_es, t + 1)
                for b in range(3):
                    pe.matmul(banks[:P, b, 0:SW], zero_b[:, 0:P], zero_b[:, 0:SW], start=True, stop=False)
                pe.matmul(banks[:P, 3, :], zero_b[:, 0:P], zero_b[:, :], start=True, stop=False)
                with pe.Fori(v0, v1) as v:
                    for c in range(GC):
                        pe.wait_ge(s_oh[c], v + 1)
                        for b in range(3):
                            pe.matmul(banks[:P, b, 0:SW], oh_db[:, c, 0:P], oh_s[:, c, b * SW:(b + 1) * SW],
                                      start=False, stop=False)
                        pe.wait_ge(s_hi[c], v + 1)
                        pe.matmul(banks[:P, 3, :], oh_d[:, c, 0:P], e_hi[:, c, :], start=False, stop=False)
                        pe.wait_ge(s_lo[c], v + 2)
                        pe.matmul(banks[:P, 3, :], oh_d[:, c, 0:P], e_lo[:, c, :], start=False,
                                  stop=False).then_inc(s_use[c], 1)
                for b in range(3):
                    pe.matmul(banks[:P, b, 0:SW], zero_b[:, 0:P], zero_b[:, 0:SW], start=False, stop=True)
                pe.matmul(banks[:P, 3, :], zero_b[:, 0:P], zero_b[:, :], start=False, stop=True).then_inc(s_fin, 1)
                pe.wait_ge(s_ct, t + 2)
                pe.wait_ge(s_tre, t + 1)
                for a in range(NT):
                    last = pe.transpose(banks[:P, 4 + a // 4, a % 4 * P:(a % 4 + 1) * P], ct[:P, a * P:(a + 1) * P],
                                        ident[:P, :P])
                last.then_inc(s_tr, 1)


class Weights:

    def __init__(self, k, sb, name, pieces, stages=2):
        self.pieces, self.stages = [], stages
        for dram, hi, lo in pieces:
            rows = min(max(1, STAGE // hi.shape[-1]), hi.shape[1])
            self.pieces += [((dram, r, rows), hi[:, r:r + rows], lo[:, r:r + rows])
                            for r in range(0, hi.shape[1], rows)] if len(hi.shape) == 3 else [((dram, 0, 0), hi, lo)]
        self.stage = sb(f"{name}_stage", [128, stages, STAGE], F32)
        self.s_in = [k.sem(f"s_{name}_w_in{b}") for b in range(stages)]
        self.s_hi = k.sem(f"s_{name}_w_hi")
        self.s_lo = k.sem(f"s_{name}_w_lo")

    def view(self, n):
        hi = self.pieces[n][1]
        rows, size = hi.shape[0], hi.free_size()
        flat = self.stage[:rows, n % self.stages, 0:size]
        return flat if len(hi.shape) == 2 else flat.rearrange("p (a b) -> p a b", b=hi.shape[-1])

    def load(self, sp, *chosen, first=0, last=None):
        for n, ((dram, r, rows), _, _) in list(enumerate(self.pieces))[first:last]:
            if n >= self.stages:
                sp.wait_ge(self.s_lo, n - self.stages + 1)
            if callable(dram):
                dram = dram(*chosen)
            if rows:
                dram = dram[:, r:r + rows]
            sp.dma_start(self.view(n), dram).then_inc(self.s_in[n % self.stages], 16)

    def high(self, act):
        for n, (_, hi, _) in enumerate(self.pieces):
            act.wait_ge(self.s_in[n % self.stages], 16 * (n // self.stages + 1))
            act.copy(hi, self.view(n)).then_inc(self.s_hi, 1)

    def low(self, dve):
        for n, (_, hi, lo) in enumerate(self.pieces):
            dve.wait_ge(self.s_hi, n + 1)
            dve.tensor_tensor(lo, self.view(n), hi.bitcast(F32), ALU.subtract).then_inc(self.s_lo, 1)

    def split(self, pool):
        for n, (_, hi, lo) in enumerate(self.pieces):
            pool.wait_ge(self.s_in[n % self.stages], 16 * (n // self.stages + 1))
            pool.tensor_copy(hi, self.view(n)).then_inc(self.s_hi, 1)
            pool.wait_ge(self.s_hi, n + 1)
            pool.tensor_tensor(lo, self.view(n), hi.bitcast(F32), ALU.subtract).then_inc(self.s_lo, 1)

    def wait(self, pe, pieces=None):
        pe.wait_ge(self.s_lo, pieces or len(self.pieces))


def product(pe, out, lhs, rhs, at, terms, first=True, last=True):
    n = 0
    for term in terms:
        for a, b in ((0, 0), (0, 1), (1, 0)):
            l, r = at(lhs[a], rhs[b], term)
            n += 1
            ins = pe.matmul(out, l, r, start=first and n == 1, stop=last and n == 3 * len(terms))
    return ins


class Normed:

    def __init__(self, k, sb, name, x, mean, rstd, ident, bank, affine=None):
        self.k, self.x, self.mean, self.rstd, self.ident, self.bank = k, x, mean, rstd, ident, bank
        self.affine = affine
        self.xn = sb(f"{name}_xn", [P, 2, D], F32)
        self.hi = sb(f"{name}_hi", [128, KT, 2, P], F32R)
        self.lo = sb(f"{name}_lo", [128, KT, 2, P], F32R)
        self.s_xn = k.sem(f"s_{name}_xn")
        self.s_aff = k.sem(f"s_{name}_aff")
        self.s_xt = k.sem(f"s_{name}_xt")
        self.s_hi = k.sem(f"s_{name}_hi")
        self.s_lo = k.sem(f"s_{name}_lo")
        self.s_used = k.sem(f"s_{name}_used")

    def parts(self):
        return self.hi, self.lo

    def rows(self, dve, i):
        pair = i % NP if isinstance(i, int) else dve.snap(self.k.nc.s_assert_within(i % NP, 0, NP - 1))
        for h in range(2):
            t = ds(2 * pair + h, 1)
            out = self.xn[:, h, :]
            ins = dve.tensor_scalar(out, self.x[:, t, :].rearrange("p a f -> p (a f)"), self.mean[:, t], self.rstd[:, t],
                                    ALU.subtract, ALU.mult)
            if self.affine:
                gamma, beta = self.affine
                ins.then_inc(self.s_aff, 1)
                dve.wait_ge(self.s_aff, 4 * i + 2 * h + 1)
                dve.tensor_tensor(out, out, gamma, ALU.mult).then_inc(self.s_aff, 1)
                dve.wait_ge(self.s_aff, 4 * i + 2 * h + 2)
                ins = dve.tensor_tensor(out, out, beta, ALU.add)
            ins.then_inc(self.s_xn, 1)

    def transposes(self, pe, i):
        for h in range(2):
            pe.wait_ge(self.s_xn, 2 * i + h + 1)
            for c in range(KT):
                ins = pe.transpose(self.k.banks[:, self.bank + h, c * P:(c + 1) * P],
                                   self.xn[:, h, c * 128:(c + 1) * 128], self.ident[:P, :P])
            ins.then_inc(self.s_xt, 1)

    def psum(self, h):
        return self.k.banks[:, self.bank + h, 0:KT * P].rearrange("p (c n) -> p c n", n=P)

    def high(self, act, i):
        for h in range(2):
            act.wait_ge(self.s_xt, 2 * i + h + 1)
            act.wait_ge(self.s_used, i + 1)
            act.copy(self.hi[:, :, h, :], self.psum(h)).then_inc(self.s_hi, 1)

    def low(self, dve, i):
        for h in range(2):
            dve.wait_ge(self.s_xt, 2 * i + h + 1)
            dve.wait_ge(self.s_hi, 2 * i + h + 1)
            dve.tensor_tensor(self.lo[:, :, h, :], self.psum(h), self.hi[:, :, h, :].bitcast(F32),
                              ALU.subtract).then_inc(self.s_lo, 1)

    def wait(self, pe, i):
        pe.wait_ge(self.s_lo, 2 * i + 2)


def half_of(h):
    return lambda xt, w, c: (xt[:, c, h, :], w[:, c, :])


def feature_tile(f):
    return lambda w, xt, c: (w[:, c, f * 128:(f + 1) * 128], xt[:, c, :, :].rearrange("p h n -> p (h n)"))


def chain(eng, sem, start=0):
    n = [start]

    def link(ins):
        n[0] += 1
        ins.then_inc(sem, 1)
        eng.wait_ge(sem, n[0])

    return link


def statistics(k, name, x, mean, rstd, again=None):
    nc = k.nc
    with ExitStack() as ctx:
        stats = ctx.enter_context(nc.sbuf_tensor(f"{name}_stats", [P, NT, nc.vector.BN_STATS_DIM], F32))
        mv = ctx.enter_context(nc.sbuf_tensor(f"{name}_mv", [P, NT, 2], F32))
        var = ctx.enter_context(nc.sbuf_tensor(f"{name}_var", [P, 2, NT], F32))
        s_bn = k.sem(f"s_{name}_bn")
        s_ag = k.sem(f"s_{name}_ag")
        s_st = k.sem(f"s_{name}_st")
        s_sq = k.sem(f"s_{name}_sq")
        block = ctx.enter_context(nc.Block())

        @block.vector
        def _(dve):
            with dve.Fori(0, NT) as t:
                dve.bn_stats(stats[:, ds(t, 1), :].rearrange("p a f -> p (a f)"),
                             x[:, ds(t, 1), :].rearrange("p a f -> p (a f)")).then_inc(s_bn, 1)
            dve.wait_ge(s_bn, NT)
            for t in range(NT):
                dve.bn_aggr(mv[:, t, :], stats[:, t, :]).then_inc(s_ag, 1)
            dve.wait_ge(s_ag, NT)
            link = chain(dve, s_st)
            link(dve.tensor_copy(mean[:, 0:NT], mv[:, :, 0]))
            link(dve.tensor_scalar(var[:, 0, :], mv[:, :, 1], EPS, None, ALU.add))
            dve.wait_ge(s_sq, 1)
            link(dve.reciprocal(rstd[:, 0:NT], var[:, 1, :]))
            if again is not None:
                link(dve.tensor_tensor(var[:, 0, :], rstd[:, 0:NT], rstd[:, 0:NT], ALU.mult))
                link(dve.tensor_tensor(var[:, 0, :], var[:, 0, :], mv[:, :, 1], ALU.mult))
                link(dve.tensor_scalar(var[:, 0, :], var[:, 0, :], EPS, None, ALU.add))
                dve.wait_ge(s_sq, 2)
                link(dve.reciprocal(again[:, 0:NT], var[:, 1, :]))
                link(dve.tensor_tensor(again[:, :], again[:, :], rstd[:, :], ALU.mult))

        @block.scalar
        def _(act):
            act.wait_ge(s_st, 2)
            act.activation(var[:, 1, :], var[:, 0, :], ACT.Sqrt).then_inc(s_sq, 1)
            if again is not None:
                act.wait_ge(s_st, 6)
                act.activation(var[:, 1, :], var[:, 0, :], ACT.Sqrt).then_inc(s_sq, 1)


def attention_phase(k, x, y, mean, rstd, counts, ident, Wq, Wk, Wv):
    nc = k.nc
    banks = k.banks
    with ExitStack() as ctx:
        def sb(name, shape, dt):
            return ctx.enter_context(nc.sbuf_tensor(name, shape, dt))

        kst = sb("kst", [128, H, N], F32R)
        vs = sb("vs", [P, NT, H, DH + 1], F32)
        wq = [sb(f"wq_s{a}", [128, KT, D], F32R) for a in range(2)]

        with ExitStack() as inner:
            def sbi(name, shape, dt):
                return inner.enter_context(nc.sbuf_tensor(name, shape, dt))

            wk = [sbi(f"wk_s{a}", [128, KT, D], F32R) for a in range(2)]
            wv = [sbi(f"wv_s{a}", [128, KT, D], F32R) for a in range(2)]
            w = Weights(k, sbi, "akv", [(src.rearrange("(c p) f -> p c f", p=128), t[0][:], t[1][:])
                                        for src, t in ((Wk, wk), (Wv, wv))], stages=3)
            late = Weights(k, sbi, "aq", [(Wq.rearrange("(c p) f -> p c f", p=128), wq[0][:], wq[1][:])])
            xt = Normed(k, sbi, "akv", x, mean, rstd, ident, 0)
            s_one = k.sem("s_akv_one")
            s_kp = k.sem("s_akv_kp")
            s_kh = k.sem("s_akv_kh")
            s_kl = k.sem("s_akv_kl")
            s_vp = k.sem("s_akv_vp")
            s_vc = k.sem("s_akv_vc")
            block = inner.enter_context(nc.Block())
            rows = ((0, 64), (64, 128))

            def kcols(i):
                return ds(i * 2 * P, 2 * P)

            @block.sync
            def _(sp):
                w.load(sp)
                late.load(sp)

            @block.gpsimd
            def _(pool):
                pool.memset(vs[:, :, :, DH:DH + 1], 1.0).then_inc(s_one, 1)
                late.split(pool)

            @block.tensor
            def _(pe):
                pe.sem_inc(xt.s_used, 1)
                xt.transposes(pe, 0)
                w.wait(pe, len(w.pieces) // 2)
                with pe.Fori(0, NP) as i:
                    xt.wait(pe, i)
                    xt.transposes(pe, i + 1)
                    for a in range(4):
                        pe.wait_ge(s_kl, 4 * i + a + 1)
                        product(pe, banks[:, 2 + a % 2, 0:2 * P], wk, xt.parts(), feature_tile(a),
                                range(KT)).then_inc(s_kp, 1)
                    w.wait(pe)
                    for h in range(2):
                        pe.wait_ge(s_vc, 2 * i + h + 1)
                        ins = product(pe, banks[:P, 4 + h, :], xt.parts(), wv, half_of(h), range(KT))
                        ins.then_inc(s_vp, 1)
                    pe.wait_ge(s_vp, 2 * i + 2)
                    pe.sem_inc(xt.s_used, 1)

            @block.scalar
            def _(act):
                act.sem_inc(s_vc, 2)
                w.high(act)
                xt.high(act, 0)
                act.wait_ge(s_one, 1)
                with act.Fori(0, NP) as i:
                    for a in range(4):
                        act.wait_ge(s_kp, 4 * i + a + 1)
                        for e, (r0, r1) in enumerate(rows):
                            ins = act.copy(kst[r0:r1, 2 * a + e, kcols(i)], banks[r0:r1, 2 + a % 2, 0:2 * P])
                        ins.then_inc(s_kh, 1)
                    for h in range(2):
                        act.wait_ge(s_vp, 2 * i + h + 1)
                        act.copy(vs[:, ds(2 * i + h, 1), :, 0:DH].rearrange("p a h d -> p (a h) d"),
                                 banks[:P, 4 + h, :].rearrange("p (h d) -> p h d", d=DH)).then_inc(s_vc, 1)
                    xt.high(act, i + 1)

            @block.vector
            def _(dve):
                dve.sem_inc(s_kl, 2)
                xt.rows(dve, 0)
                w.low(dve)
                xt.low(dve, 0)
                with dve.Fori(0, NP) as i:
                    xt.rows(dve, i + 1)
                    for a in range(4):
                        dve.wait_ge(s_kh, 4 * i + a + 1)
                        for e, (r0, r1) in enumerate(rows):
                            q0, q1 = rows[1 - e]
                            ins = dve.tensor_tensor(kst[q0:q1, 2 * a + e, kcols(i)], banks[r0:r1, 2 + a % 2, 0:2 * P],
                                                    kst[r0:r1, 2 * a + e, kcols(i)].bitcast(F32), ALU.subtract)
                        ins.then_inc(s_kl, 1)
                    xt.low(dve, i + 1)

        UNITS = NT // 2
        SR, ER, PR, AHEAD = 4, 4, 4, 3
        NU = H * UNITS
        QU = 2 * UNITS
        HG = H // 2
        qh = sb("qh", [128, H, 2 * P], F32R)
        ql = sb("ql", [128, H, 2 * P], F32R)
        er = sb("er", [P, ER, 2, 2 * P], F32)
        pr = sb("pr", [P, PR, 2, 2 * P], F32)
        so = sb("so", [DH + 1, 2, 2 * P], F32)
        zr = sb("zr", [P, 2, 2, HG], F32)
        on = sb("on", [P, 2, D // 2], F32)
        xt = Normed(k, sb, "att", x, mean, rstd, ident, 0)
        s_qp = k.sem("s_qp")
        s_qh = k.sem("s_qh")
        s_ql = k.sem("s_ql")
        s_s = k.sem("s_s")
        s_e = k.sem("s_e")
        s_c = k.sem("s_c")
        s_p = k.sem("s_p")
        s_av = k.sem("s_av")
        s_so = k.sem("s_so")
        s_ot = k.sem("s_ot")
        s_on = k.sem("s_on")
        s_n = k.sem("s_n")
        s_y = k.sem("s_y")
        block = ctx.enter_context(nc.Block())
        rows = ((0, 64), (64, 128))
        LO, HI = float(np.exp(np.float32(-5.0))), float(np.exp(np.float32(5.0)))

        @block.tensor
        def _(pe):
            def q_product(i, a):
                pe.wait_ge(s_ql, 4 * i + a + 1)
                product(pe, banks[:, 2, 0:2 * P], wq, xt.parts(), feature_tile(a), range(KT)).then_inc(s_qp, 1)

            def scores(i, n):
                h, u = divmod(n, UNITS)
                if n % QU == 0:
                    pe.wait_ge(s_ql, 4 * i + n // QU + 2)
                pe.wait_ge(s_e, NU * i + n + 1)
                for j in range(2):
                    cols = slice((2 * u + j) * P, (2 * u + j + 1) * P)
                    out = banks[:P, 4 + n % SR, j * 2 * P:(j + 1) * 2 * P]
                    pe.matmul(out, kst[:, h, cols], qh[:, h, :], start=True, stop=False)
                    ins = pe.matmul(out, kst[:, h, cols], ql[:, h, :], start=False, stop=True)
                ins.then_inc(s_s, 1)

            def back(i, h):
                if h == 0:
                    xt.wait(pe, i + 1)
                if h == HG:
                    pe.wait_ge(s_on, 2 * i + 2)
                pe.wait_ge(s_so, H * i + h + 3)
                for g in range(2):
                    ins = pe.transpose(banks[:P, g, h % HG * (DH + 1):(h % HG + 1) * (DH + 1)],
                                       so[:, h % 2, g * P:(g + 1) * P], ident[:DH + 1, :DH + 1])
                ins.then_inc(s_ot, 1)

            pe.sem_inc(xt.s_used, 1)
            pe.sem_inc(s_av, PR)
            xt.transposes(pe, 0)
            xt.wait(pe, 0)
            for a in range(4):
                q_product(0, a)
            pe.wait_ge(s_qp, 4)
            pe.sem_inc(xt.s_used, 1)
            for n in range(AHEAD):
                scores(0, n)
            with pe.Fori(0, NP) as i:
                for n in range(NU):
                    h, u = divmod(n, UNITS)
                    if n + AHEAD < NU:
                        scores(i, n + AHEAD)
                    else:
                        scores(i + 1, n + AHEAD - NU)
                    if n == 3:
                        pe.wait_ge(s_on, 2 * i + 1)
                        xt.transposes(pe, i + 1)
                    pe.wait_ge(s_p, NU * i + n + 1 + ER)
                    if u == 0:
                        pe.wait_ge(s_so, H * i + h + 1)
                        if h % 2 == 0:
                            pe.wait_ge(s_ql, 4 * i + h // 2 + 5)
                    for j in range(2):
                        ins = pe.matmul(banks[:DH + 1, 2 + h % 2, 0:2 * P], vs[:, 2 * u + j, h, :], pr[:, n % PR, j, :],
                                        start=u == 0 and j == 0, stop=u == UNITS - 1 and j == 1)
                    ins.then_inc(s_av, 1)
                    if n % QU == QU - 1 - AHEAD:
                        if n < QU:
                            xt.wait(pe, i + 1)
                        pe.wait_ge(s_so, H * i + h + 2)
                        q_product(i + 1, n // QU)
                    if h and u == 1:
                        back(i, h - 1)
                pe.wait_ge(s_qp, 4 * i + 8)
                pe.sem_inc(xt.s_used, 1)
                back(i, H - 1)

        @block.scalar
        def _(act):
            def q_high(i, a):
                act.wait_ge(s_qp, 4 * i + a + 1)
                for e, (r0, r1) in enumerate(rows):
                    for q0, q1 in rows:
                        ins = act.copy(qh[q0:q1, 2 * a + e, :], banks[r0:r1, 2, 0:2 * P])
                ins.then_inc(s_qh, 1)

            def out(i, h):
                act.wait_ge(s_av, NU * i + UNITS * (h + 1) + PR)
                if h >= 2:
                    act.wait_ge(s_ot, H * i + h - 1)
                act.copy(so[:, h % 2, :], banks[:DH + 1, 2 + h % 2, 0:2 * P]).then_inc(s_so, 1)

            act.sem_inc(s_e, SR)
            act.sem_inc(s_so, 2)
            xt.high(act, 0)
            for a in range(4):
                q_high(0, a)
            with act.Fori(0, NP) as i:
                for n in range(NU):
                    h, u = divmod(n, UNITS)
                    act.wait_ge(s_s, NU * i + n + 1)
                    act.wait_ge(s_p, NU * i + n + 1)
                    act.activation(er[:, n % ER, :, :].rearrange("p j n -> p (j n)"),
                                   banks[:P, 4 + n % SR, 0:4 * P], ACT.Exp, scale=1.0 / 8.0).then_inc(s_e, 1)
                    if n == 5:
                        xt.high(act, i + 1)
                    if n % QU == QU - 2:
                        q_high(i + 1, n // QU)
                    if h and u == 1:
                        out(i, h - 1)
                out(i, H - 1)

        @block.vector
        def _(dve):
            def q_low(i, a):
                dve.wait_ge(s_qh, 4 * i + a + 1)
                for e, (r0, r1) in enumerate(rows):
                    for q0, q1 in rows:
                        ins = dve.tensor_tensor(ql[q0:q1, 2 * a + e, :], banks[r0:r1, 2, 0:2 * P],
                                                qh[r0:r1, 2 * a + e, :].bitcast(F32), ALU.subtract)
                ins.then_inc(s_ql, 1)

            def clip(i, n):
                dve.wait_ge(s_e, NU * i + n + 1 + SR)
                dve.tensor_scalar(er[:, n % ER, :, :], er[:, n % ER, :, :], HI, LO, ALU.min, ALU.max).then_inc(s_c, 1)

            def divide(i, q):
                dve.wait_ge(s_ot, H * i + HG * (q + 1))
                out = banks[:P, 0:2, 0:HG * (DH + 1)].rearrange("p g (h d) -> p g h d", d=DH + 1)
                first = 6 * (2 * i + q)
                dve.tensor_scalar(zr[:, 0], out[:, :, :, DH:DH + 1].rearrange("p g h d -> p g (h d)"), 1e-6, None,
                                  ALU.add).then_inc(s_n, 1)
                dve.wait_ge(s_n, first + 1)
                dve.reciprocal(zr[:, 1], zr[:, 0]).then_inc(s_n, 1)
                dve.wait_ge(s_n, first + 2)
                for g in range(2):
                    ins = dve.tensor_tensor(on[:, g, :].rearrange("p (h d) -> p h d", d=DH), out[:, g, :, 0:DH],
                                            zr[:, 1, g, :].unsqueeze(2).to_broadcast([P, HG, DH]), ALU.mult)
                    ins.then_inc(s_n, 1)
                dve.wait_ge(s_n, first + 4)
                dve.sem_inc(s_on, 1)
                dve.wait_ge(s_y, 2 * i + 2)
                for g in range(2):
                    ys = y[:, ds(2 * i + g, 1), q * (D // 2):(q + 1) * (D // 2)].rearrange("p a f -> p (a f)")
                    dve.tensor_tensor(ys, ys, on[:, g, :], ALU.add).then_inc(s_n, 1)

            dve.sem_inc(s_ql, 1)
            dve.sem_inc(s_on, 1)
            dve.sem_inc(s_p, ER)
            xt.rows(dve, 0)
            xt.low(dve, 0)
            for a in range(4):
                q_low(0, a)
            with dve.Fori(0, NP) as i:
                clip(i, 0)
                for n in range(NU):
                    h, u = divmod(n, UNITS)
                    if n + 1 < NU:
                        clip(i, n + 1)
                    dve.wait_ge(s_c, NU * i + n + 1)
                    dve.wait_ge(s_av, NU * i + n + 1)
                    cnt = counts[:, ds(2 * i, 2), 2 * u:2 * u + 2, :].rearrange("p g j d -> p j g d")
                    dve.tensor_tensor(pr[:, n % PR, :, :].rearrange("p j (g d) -> p j g d", g=2),
                                      er[:, n % ER, :, :].rearrange("p j (g d) -> p j g d", g=2), cnt,
                                      ALU.mult).then_inc(s_p, 1)
                    if n == 0:
                        xt.rows(dve, i + 1)
                    if n in (1, 2):
                        t = ds(2 * i + n - 1, 1)
                        dve.tensor_scalar(y[:, t, :].rearrange("p a f -> p (a f)"),
                                          x[:, t, :].rearrange("p a f -> p (a f)"), mean[:, t], rstd[:, t],
                                          ALU.subtract, ALU.mult).then_inc(s_y, 1)
                    if n == 5:
                        xt.low(dve, i + 1)
                    if n % QU == QU - 2:
                        q_low(i + 1, n // QU)
                    if n == UNITS * HG + 2:
                        divide(i, 0)
                divide(i, 1)
                dve.wait_ge(s_n, 6 * (2 * i + 2))


def batchnorm_phase(k, x, y, ones_n, gamma, beta):
    nc, banks = k.nc, k.banks
    with ExitStack() as ctx:
        def sb(name, shape, dt):
            return ctx.enter_context(nc.sbuf_tensor(name, shape, dt))

        row = sb("bn_row", [P, 2, D], F32)
        sq = sb("bn_sq", [P, 2, D], F32)
        inv = sb("bn_inv", [P, 3, D], F32)
        s_row = k.sem("s_bnr")
        s_m = k.sem("s_bnm")
        s_d = k.sem("s_bnd")
        s_s = k.sem("s_bns")
        s_u = k.sem("s_bnu")
        s_v = k.sem("s_bnv")
        s_c = k.sem("s_bnc")
        s_o = k.sem("s_bno")
        s_p = k.sem("s_bnp")
        block = ctx.enter_context(nc.Block())

        def tile(a, t):
            return a[:, ds(t, 1), :].rearrange("p a f -> p (a f)")

        @block.sync
        def _(sp):
            sp.dma_start(row[:, 0, :], gamma.partition_broadcast(P)).then_inc(s_row, 16)
            sp.dma_start(row[:, 1, :], beta.partition_broadcast(P)).then_inc(s_row, 16)

        @block.tensor
        def _(pe):
            for t in range(NT):
                ins = pe.matmul(banks[:P, 0, :], ones_n[:P, :P], y[:, t, :], start=t == 0, stop=t == NT - 1)
            ins.then_inc(s_m, 1)
            pe.sem_inc(s_u, 2)
            for t in range(NT):
                pe.wait_ge(s_s, t + 1)
                pe.matmul(banks[:P, 1, :], ones_n[:P, :P], sq[:, t % 2, :], start=t == 0,
                          stop=t == NT - 1).then_inc(s_u, 1)

        @block.scalar
        def _(act):
            with act.Fori(0, NP) as i:
                for h in range(2):
                    act.wait_ge(s_d, 2 * i + h + 1)
                    act.wait_ge(s_u, 2 * i + h + 1)
                    act.activation(sq[:, h, :], tile(y, 2 * i + h), ACT.Square).then_inc(s_s, 1)
            act.wait_ge(s_c, 1)
            act.activation(inv[:, 1, :], inv[:, 0, :], ACT.Sqrt).then_inc(s_v, 1)

        @block.vector
        def _(dve):
            dve.wait_ge(s_m, 1)
            with dve.Fori(0, NT) as t:
                dve.tensor_tensor(tile(y, t), tile(y, t), banks[:P, 0, :], ALU.subtract).then_inc(s_d, 1)
            link = chain(dve, s_c)
            dve.wait_ge(s_u, NT + 2)
            link(dve.tensor_scalar(inv[:, 0, :], banks[:P, 1, :], EPS, None, ALU.add))
            dve.wait_ge(s_v, 1)
            link(dve.reciprocal(inv[:, 2, :], inv[:, 1, :]))
            dve.wait_ge(s_row, 32)
            link(dve.tensor_tensor(inv[:, 2, :], inv[:, 2, :], row[:, 0, :], ALU.mult))
            dve.wait_ge(s_d, NT)
            with dve.Fori(0, NP) as i:
                for h in range(2):
                    dve.tensor_tensor(tile(y, 2 * i + h), tile(y, 2 * i + h), inv[:, 2, :], ALU.mult).then_inc(s_o, 1)
                for h in range(2):
                    dve.wait_ge(s_o, 4 * i + h + 1)
                    dve.tensor_tensor(tile(y, 2 * i + h), tile(y, 2 * i + h), row[:, 1, :], ALU.add).then_inc(s_o, 1)

        @block.gpsimd
        def _(pool):
            with pool.Fori(0, NP) as i:
                for h in range(2):
                    pool.wait_ge(s_o, 4 * i + 3 + h)
                    pool.tensor_tensor(tile(y, 2 * i + h), tile(y, 2 * i + h), tile(x, 2 * i + h),
                                       ALU.add).then_inc(s_p, 1)


def mix_phase(k, name, x, y, mean, rstd, ident, mask, head_cols, head_rows, wqkv, qkv_b, q_cols, wout, out_b, affine=None, base=None):
    nc, banks = k.nc, k.banks
    with ExitStack() as ctx:
        def sb(nm, shape, dt):
            return ctx.enter_context(nc.sbuf_tensor(f"{name}_{nm}", shape, dt))

        def sem(nm):
            return k.sem(f"s_{name}_{nm}")

        kvw = [sb(f"kvw{a}", [128, KT, D], F32R) for a in range(2)]
        ks8 = [sb(f"ks8{a}", [128, KT, H], F32R) for a in range(2)]
        sel = sb("sel", [H, KT, 128], F32R)
        wq = [sb(f"wq{a}", [128, KT, D], F32R) for a in range(2)]
        bq = sb("bq", [128, KT], F32)
        rows = sb("rows", [P, 5, D], F32)
        s_row = sem("row")
        gb = (rows[:, 3, :], rows[:, 4, :]) if affine else None
        bias = qkv_b is not None

        with ExitStack() as inner:
            def sbi(nm, shape, dt):
                return inner.enter_context(nc.sbuf_tensor(nm, shape, dt))

            wk = [sbi(f"{name}_wk{a}", [128, KT, D], F32R) for a in range(2)]
            wv = [sbi(f"{name}_wv{a}", [128, KT, D], F32R) for a in range(2)]
            wo = [sbi(f"{name}_wo{a}", [128, KT, D], F32R) for a in range(2)]
            wsrc = wqkv.rearrange("(c p) f -> p c f", p=128)
            w = Weights(k, sbi, f"{name}k", [
                (wsrc[:, :, D:2 * D], wk[0][:], wk[1][:]), (wsrc[:, :, 2 * D:3 * D], wv[0][:], wv[1][:])], stages=3)
            late = Weights(k, sbi, f"{name}l", [
                (wout.rearrange("(c p) f -> p c f", p=128), wo[0][:], wo[1][:]),
                (wsrc[:, :, 0:D], wq[0][:], wq[1][:])])
            xt = Normed(k, sbi, f"{name}k", x, mean, rstd, ident, 0, gb)
            kx = sbi(f"{name}_kx", [P, 2, 2, D], F32)
            kf = sbi(f"{name}_kf", [P, 2, D], F32)
            kh, kl, vh, vl = (sbi(f"{name}_{nm}", [P, 2, D], F32R) for nm in ("kh", "kl", "vh", "vl"))
            vf = sbi(f"{name}_vf", [P, 2, D], F32) if bias else None
            ones = sbi(f"{name}_ones", [P, 2], F32)
            kvm = sbi(f"{name}_kvm", [128, KT, 128], F32)
            ksm = sbi(f"{name}_ksm", [128, KT], F32)
            ks8f = sbi(f"{name}_ks8f", [128, KT, H], F32)
            hcol = sbi(f"{name}_hcol", [128, KT, H], F32)
            hrow = sbi(f"{name}_hrow", [H, KT, 128], F32)
            kvt = [sbi(f"{name}_kvt{a}", [128, KT, 128], F32R) for a in range(2)]
            s_kp, s_vp = sem("kp"), sem("vp")
            s_kb, s_vb = sem("kb"), sem("vb")
            s_ke, s_kf = sem("ke"), sem("kf")
            s_kh, s_kl, s_vh, s_vl = sem("kh"), sem("kl"), sem("vh"), sem("vl")
            s_kv = sem("kv")
            s_one, s_f, s_w, s_wh = sem("one"), sem("f"), sem("w"), sem("wh")
            block = inner.enter_context(nc.Block())

            @block.sync
            def _(sp):
                sp.dma_start(rows[:, 2, :], out_b.partition_broadcast(P)).then_inc(s_row, 16)
                sp.dma_start(hcol[:, :, :], head_cols).then_inc(s_row, 16)
                sp.dma_start(hrow[:, :, :], head_rows).then_inc(s_row, 16)
                if affine:
                    sp.dma_start(rows[:, 3, :], affine[0].partition_broadcast(P)).then_inc(s_row, 16)
                    sp.dma_start(rows[:, 4, :], affine[1].partition_broadcast(P)).then_inc(s_row, 16)
                if bias:
                    sp.dma_start(rows[:, 0, :], qkv_b[D:2 * D].partition_broadcast(P)).then_inc(s_row, 16)
                    sp.dma_start(rows[:, 1, :], qkv_b[2 * D:3 * D].partition_broadcast(P)).then_inc(s_row, 16)
                    sp.dma_start(bq[:, :], q_cols).then_inc(s_row, 16)
                w.load(sp)
                late.load(sp)

            nrow = 48 + (32 if affine else 0) + (48 if bias else 0)

            @block.gpsimd
            def _(pool):
                pool.memset(ones[:, :], 1.0).then_inc(s_one, 1)
                late.split(pool)

            @block.tensor
            def _(pe):
                pe.sem_inc(xt.s_used, 1)
                pe.sem_inc(s_kv, 2)
                xt.transposes(pe, 0)
                w.wait(pe, len(w.pieces) // 2)
                pe.wait_ge(s_one, 2)
                with pe.Fori(0, NP) as i:
                    xt.wait(pe, i)
                    xt.transposes(pe, i + 1)
                    for h in range(2):
                        product(pe, banks[:P, 2 + h, :], xt.parts(), wk, half_of(h), range(KT)).then_inc(s_kp, 1)
                    w.wait(pe)
                    for h in range(2):
                        ins = product(pe, banks[:P, 4 + h, :], xt.parts(), wv, half_of(h), range(KT))
                        ins.then_inc(s_vp, 1)
                    pe.wait_ge(s_vp, 2 * i + 2)
                    pe.sem_inc(xt.s_used, 1)
                    for h in range(2):
                        pe.wait_ge(s_kl, 2 * i + h + 1)
                        pe.wait_ge(s_vl, 2 * i + h + 1)
                        for j in range(KT):
                            c = slice(128 * j, 128 * (j + 1))
                            for n, (a, b) in enumerate(((vh, kh), (vh, kl), (vl, kh))):
                                pe.matmul(banks[:, 6, c], a[:, h, c], b[:, h, c], start=False, stop=False,
                                          skip_group_check=True)
                            ins = pe.matmul(banks[:, 7, 2 * j:2 * j + 2], kf[:, h, c], ones[:, :], start=False,
                                            stop=False, skip_group_check=True)
                        ins.then_inc(s_kv, 1)
                for j in range(KT):
                    if j == 0:
                        pe.wait_ge(s_f, 5)
                        late.wait(pe)
                    ins = product(pe, banks[:, 2 + j, :], kvt, wo, lambda a, b, c: (a[:, c, :], b[:, c, :]), [j])
                    ins.then_inc(s_w, 1)

            @block.scalar
            def _(act):
                w.high(act)
                xt.high(act, 0)
                with act.Fori(0, NP) as i:
                    for h in range(2):
                        if bias:
                            act.wait_ge(s_kb, 2 * i + h + 1)
                            src = kf[:, h, :]
                        else:
                            act.wait_ge(s_kp, 2 * i + h + 1)
                            src = banks[:P, 2 + h, :]
                        act.activation(kx[:, h, 0, :], src, ACT.Exp)
                        act.activation(kx[:, h, 1, :], src, ACT.Relu).then_inc(s_ke, 1)
                    for h in range(2):
                        act.wait_ge(s_kf, 2 * i + h + 1)
                        act.copy(kh[:, h, :], kf[:, h, :]).then_inc(s_kh, 1)
                    for h in range(2):
                        if bias:
                            act.wait_ge(s_vb, 2 * i + h + 1)
                        act.wait_ge(s_vp, 2 * i + h + 1)
                        act.wait_ge(s_kv, 2 * i + h + 1)
                        act.copy(vh[:, h, :], vf[:, h, :] if bias else banks[:P, 4 + h, :]).then_inc(s_vh, 1)
                    xt.high(act, i + 1)
                act.wait_ge(s_f, 3)
                act.copy(kvt[0][:, :, :], kvm[:, :, :]).then_inc(s_f, 1)
                for j in range(KT):
                    act.wait_ge(s_w, j + 1)
                    act.copy(kvw[0][:, j, :], banks[:, 2 + j, :]).then_inc(s_wh, 1)

            @block.vector
            def _(dve):
                dve.wait_ge(s_row, nrow)
                dve.memset(banks[:, 6:8, :], 0.0).then_inc(s_one, 1)
                xt.rows(dve, 0)
                w.low(dve)
                xt.low(dve, 0)
                with dve.Fori(0, NP) as i:
                    xt.rows(dve, i + 1)
                    if bias:
                        for h in range(2):
                            dve.wait_ge(s_kp, 2 * i + h + 1)
                            dve.wait_ge(s_kv, 2 * i + h + 1)
                            dve.tensor_tensor(kf[:, h, :], banks[:P, 2 + h, :], rows[:, 0, :], ALU.add).then_inc(s_kb, 1)
                    for h in range(2):
                        dve.wait_ge(s_ke, 2 * i + h + 1)
                        dve.wait_ge(s_kv, 2 * i + h + 1)
                        dve.scalar_tensor_tensor(kf[:, h, :], kx[:, h, 0, :], 1.0, kx[:, h, 1, :], ALU.min,
                                                 ALU.add).then_inc(s_kf, 1)
                    for h in range(2):
                        dve.wait_ge(s_kh, 2 * i + h + 1)
                        dve.tensor_tensor(kl[:, h, :], kf[:, h, :], kh[:, h, :].bitcast(F32),
                                          ALU.subtract).then_inc(s_kl, 1)
                    if bias:
                        for h in range(2):
                            dve.wait_ge(s_vp, 2 * i + h + 1)
                            dve.tensor_tensor(vf[:, h, :], banks[:P, 4 + h, :], rows[:, 1, :], ALU.add).then_inc(s_vb, 1)
                    for h in range(2):
                        dve.wait_ge(s_vh, 2 * i + h + 1)
                        dve.tensor_tensor(vl[:, h, :], vf[:, h, :] if bias else banks[:P, 4 + h, :],
                                          vh[:, h, :].bitcast(F32), ALU.subtract).then_inc(s_vl, 1)
                    xt.low(dve, i + 1)
                dve.wait_ge(s_kv, 2 * NP + 2)
                kvb = banks[:, 6, :].rearrange("p (j d) -> p j d", d=128)
                many = mask[:, :].unsqueeze(1).to_broadcast([128, KT, 128])
                dve.tensor_tensor(kvm[:, :, :], kvb, many, ALU.mult).then_inc(s_f, 1)
                dve.tensor_copy(ksm[:, :], banks[:, 7, 0:2 * KT].rearrange("p (j a) -> p j a", a=2)[:, :, 0]).then_inc(s_f, 1)
                dve.wait_ge(s_f, 2)
                dve.sem_inc(s_f, 1)
                dve.wait_ge(s_f, 4)
                dve.tensor_tensor(kvt[1][:, :, :], kvm[:, :, :], kvt[0][:, :, :].bitcast(F32), ALU.subtract).then_inc(s_f, 1)
                dve.wait_ge(s_f, 5)
                dve.tensor_tensor(ks8f[:, :, :], hcol[:, :, :], ksm[:, :].unsqueeze(2).to_broadcast([128, KT, H]),
                                  ALU.mult).then_inc(s_f, 1)
                dve.tensor_copy(sel[:, :, :], hrow[:, :, :])
                dve.wait_ge(s_f, 6)
                dve.tensor_copy(ks8[0][:, :, :], ks8f[:, :, :]).then_inc(s_f, 1)
                dve.wait_ge(s_f, 7)
                dve.tensor_tensor(ks8[1][:, :, :], ks8f[:, :, :], ks8[0][:, :, :].bitcast(F32), ALU.subtract)
                dve.wait_ge(s_wh, KT)
                for j in range(KT):
                    dve.tensor_tensor(kvw[1][:, j, :], banks[:, 2 + j, :], kvw[0][:, j, :].bitcast(F32), ALU.subtract)

        qx = sb("qx", [128, 2, KT, 2 * P], F32)
        qf = sb("qf", [128, KT, 2 * P], F32)
        qp = [sb(f"qp{a}", [128, KT, 2 * P], F32R) for a in range(2)]
        rz = sb("rz", [H, 2, 2 * P], F32)
        zs = [sb(f"zs{a}", [H, 2 * P], F32R) for a in range(2)]
        qz = sb("qz", [128, KT, 2 * P], F32)
        qs = [sb(f"qs{a}", [128, KT, 2, P], F32R) for a in range(2)]
        tmp = sb("tmp", [P, 2, D], F32)
        ab = sb("ab", [P, 2, NT], F32)
        xt = Normed(k, sb, f"{name}q", x, mean, rstd, ident, 0, gb)
        once = base
        s_qp, s_qe, s_qf, s_qh, s_ql = sem("qp"), sem("qe"), sem("qf"), sem("qh"), sem("ql")
        s_z = sem("z")
        s_ze, s_zr, s_zh, s_zl = sem("ze"), sem("zr"), sem("zh"), sem("zl")
        s_zb = sem("zb")
        s_qz, s_sh, s_sl = sem("qz"), sem("sh"), sem("sl")
        s_o, s_t, s_y, s_b, s_ab = sem("o"), sem("t"), sem("y"), sem("b"), sem("ab")
        block = ctx.enter_context(nc.Block())

        def tile(a, t):
            return a[:, ds(t, 1), :].rearrange("p a f -> p (a f)")

        def qbank(f):
            return banks[:, 2 + f // 2, f % 2 * 2 * P:(f % 2 + 1) * 2 * P]

        def zbank(f):
            return banks[:, 4 + f // 2, f % 2 * 2 * P:(f % 2 + 1) * 2 * P]

        @block.tensor
        def _(pe):
            def q_products(i, tiles):
                for f in tiles:
                    product(pe, qbank(f), wq, xt.parts(), feature_tile(f), range(KT)).then_inc(s_qp, 1)

            def taken(i):
                pe.wait_ge(s_qp, KT * (i + 1))
                pe.sem_inc(xt.s_used, 1)

            pe.sem_inc(xt.s_used, 1)
            xt.transposes(pe, 0)
            xt.wait(pe, 0)
            q_products(0, range(KT))
            taken(0)
            xt.transposes(pe, 1)
            with pe.Fori(0, NP) as i:
                for f in range(KT):
                    pe.wait_ge(s_ql, KT * i + f + 1)
                    if f == 0:
                        pe.wait_ge(s_qz, i + 1)
                    ins = product(pe, banks[0:H, 4, 0:2 * P], ks8, qp, plain, [f], first=f == 0, last=f == KT - 1)
                ins.then_inc(s_z, 1)
                xt.wait(pe, i + 1)
                q_products(i + 1, range(2))
                pe.wait_ge(s_zl, i + 1)
                for f in range(KT):
                    for a in range(2):
                        ins = pe.matmul(zbank(f), sel[:, f, :], zs[a][:, :], start=a == 0, stop=a == 1)
                ins.then_inc(s_zb, 1)
                q_products(i + 1, range(2, KT))
                taken(i + 1)
                xt.transposes(pe, i + 2)
                for h in range(2):
                    if h == 0:
                        pe.wait_ge(s_sl, i + 1)
                    pe.wait_ge(s_t, 2 * i + h + 1)
                    product(pe, banks[:P, 6 + h, :], qs, kvw, half_of(h), range(KT)).then_inc(s_o, 1)

        @block.scalar
        def _(act):
            def elu(i):
                for f in range(KT):
                    act.wait_ge(s_qp, KT * i + f // 2 * 2 + 2)
                    b = bq[:, f:f + 1] if bias else 0.0
                    act.activation(qx[:, 0, f, :], qbank(f), ACT.Exp, bias=b)
                    act.activation(qx[:, 1, f, :], qbank(f), ACT.Relu, bias=b).then_inc(s_qe, 1)
                for f in range(KT):
                    act.wait_ge(s_qf, KT * i + f + 1)
                    act.copy(qp[0][:, f, :], qf[:, f, :]).then_inc(s_qh, 1)

            xt.high(act, 0)
            elu(0)
            xt.high(act, 1)
            with act.Fori(0, NP) as i:
                act.wait_ge(s_zr, i + 1)
                act.copy(zs[0][:, :], rz[:, 1, :]).then_inc(s_zh, 1)
                act.wait_ge(s_qz, i + 2)
                act.wait_ge(s_o, 2 * i + 1)
                act.copy(qs[0][:, :, :, :].rearrange("p c h n -> p c (h n)"), qz[:, :, :]).then_inc(s_sh, 1)
                elu(i + 1)
                xt.high(act, i + 2)

        @block.vector
        def _(dve):
            def elu(i):
                for f in range(KT):
                    dve.wait_ge(s_qe, KT * i + f + 1)
                    dve.scalar_tensor_tensor(qf[:, f, :], qx[:, 0, f, :], 1.0, qx[:, 1, f, :], ALU.min,
                                             ALU.add).then_inc(s_qf, 1)
                for f in range(KT):
                    dve.wait_ge(s_qh, KT * i + f + 1)
                    dve.tensor_tensor(qp[1][:, f, :], qf[:, f, :], qp[0][:, f, :].bitcast(F32),
                                      ALU.subtract).then_inc(s_ql, 1)

            dve.sem_inc(s_t, 2)
            dve.sem_inc(s_qz, 1)
            dve.sem_inc(s_o, 1)
            if once is not None:
                dve.tensor_scalar(ab[:, 0, :], once[1][:, :], 1.0, None, ALU.add).then_inc(s_ab, 1)
                dve.tensor_tensor(ab[:, 1, :], once[0][:, :], once[1][:, :], ALU.mult).then_inc(s_ab, 1)
                dve.wait_ge(s_ab, 2)
            xt.rows(dve, 0)
            xt.low(dve, 0)
            xt.rows(dve, 1)
            elu(0)
            xt.low(dve, 1)
            with dve.Fori(0, NP) as i:
                dve.wait_ge(s_z, i + 1)
                dve.tensor_scalar(rz[:, 0, :], banks[0:H, 4, 0:2 * P], eps_of(name), None, ALU.add).then_inc(s_ze, 1)
                dve.wait_ge(s_ze, i + 1)
                dve.reciprocal(rz[:, 1, :], rz[:, 0, :]).then_inc(s_zr, 1)
                dve.wait_ge(s_zh, i + 1)
                dve.tensor_tensor(zs[1][:, :], rz[:, 1, :], zs[0][:, :].bitcast(F32), ALU.subtract).then_inc(s_zl, 1)
                xt.rows(dve, i + 2)
                dve.wait_ge(s_zb, i + 1)
                for g in range(2):
                    ins = dve.tensor_tensor(qz[:, 2 * g:2 * g + 2, :], qf[:, 2 * g:2 * g + 2, :],
                                            banks[:, 4 + g, 0:4 * P].rearrange("p (f n) -> p f n", f=2), ALU.mult)
                ins.then_inc(s_qz, 1)
                dve.wait_ge(s_sh, i + 1)
                dve.tensor_tensor(qs[1][:, :, :, :].rearrange("p c h n -> p c (h n)"), qz[:, :, :],
                                  qs[0][:, :, :, :].bitcast(F32).rearrange("p c h n -> p c (h n)"),
                                  ALU.subtract).then_inc(s_sl, 1)
                elu(i + 1)
                xt.low(dve, i + 2)
                for h in range(2):
                    t = 2 * i + h
                    if once is not None:
                        dve.tensor_scalar(tile(y, t), tile(x, t), ab[:, 0, ds(t, 1)], ab[:, 1, ds(t, 1)],
                                          ALU.mult, ALU.subtract).then_inc(s_b, 1)
                    dve.wait_ge(s_o, t + 2)
                    dve.wait_ge(s_y, t + 1)
                    dve.tensor_tensor(tmp[:, h, :], banks[:P, 6 + h, :], rows[:, 2, :], ALU.add).then_inc(s_t, 1)

        @block.gpsimd
        def _(pool):
            pool.sem_inc(s_y, 2)
            with pool.Fori(0, NP) as i:
                for h in range(2):
                    t = 2 * i + h
                    if once is not None:
                        pool.wait_ge(s_b, t + 1)
                    pool.wait_ge(s_t, t + 3)
                    pool.tensor_tensor(tile(y, t), tile(y, t), tmp[:, h, :], ALU.add).then_inc(s_y, 1)


def eps_of(name):
    return {"mix0": 1e-6, "mix1": 1e-8}[name]


def flat(a, t):
    return a[:, ds(t, 1), :].rearrange("p a f -> p (a f)")


def plain(a, b, c):
    return a[:, c, :], b[:, c, :]


def experts_phase(k, x, mean, rstd, ident, sel, gate_w, w1, sw1, w2, sw2, b1_cols, b2_rows):
    nc, banks = k.nc, k.banks
    EX, FT = 8, 12
    with ExitStack() as ctx:
        def sb(nm, shape, dt):
            return ctx.enter_context(nc.sbuf_tensor(f"moe_{nm}", shape, dt))

        def sem(nm):
            return k.sem(f"s_moe_{nm}")

        v1 = [sb(f"v1{a}", [128, KT, 1024], F32R) for a in range(2)]
        vs1 = [sb(f"vs1{a}", [128, KT, D], F32R) for a in range(2)]
        v2 = [sb(f"v2{a}", [128, FT, D], F32R) for a in range(2)]
        vg = [sb(f"vg{a}", [128, KT, EX], F32R) for a in range(2)]
        vb = [sb(f"vb{a}", [EX + 1, D], F32R) for a in range(2)]
        sel_r = sb("sel", [EX, EX, 128], F32R)
        b1 = sb("b1", [128, FT], F32)
        w = Weights(k, sb, "moe", [
            (gate_w.rearrange("(c p) e -> p c e", p=128), vg[0][:], vg[1][:]),
            (b2_rows, vb[0][:, :], vb[1][:, :]),
            (sw1.rearrange("(c p) f -> p c f", p=128), vs1[0][:], vs1[1][:]),
            (w1.rearrange("(c p) f -> p c f", p=128), v1[0][:], v1[1][:])])
        late = Weights(k, sb, "moel", [
            (w2.rearrange("e p f -> p e f"), v2[0][:, 0:EX], v2[1][:, 0:EX]),
            (sw2.rearrange("(c p) f -> p c f", p=128), v2[0][:, EX:], v2[1][:, EX:])])
        xt = Normed(k, sb, "moex", x, mean, rstd, ident, 0)
        ht = [sb(f"ht{a}", [128, FT, 2, P], F32R) for a in range(2)]
        hr = sb("hr", [128, 2, 2 * P], F32)
        hp = sb("hp", [128, 2, 2 * P], F32)
        iota8 = sb("iota8", [P, EX], F32)
        g1 = sb("g1", [P, 8, 2, EX], F32)
        g0 = sb("g0", [P, 8, 2], F32)
        cth = sb("cth", [EX + 1, 2, P], F32R)
        ctl = sb("ctl", [EX + 1, 2, P], F32R)
        s_c0 = sem("c0")
        s_bl = sem("bl")
        s_g = sem("g")
        s_gs = sem("gs")
        s_ge = sem("ge")
        s_ct = sem("ct")
        s_c1, s_cc = sem("c1"), sem("cc")
        s_h = sem("h")
        s_r = sem("r")
        s_p = sem("p")
        s_hh = sem("hh")
        s_hl = sem("hl")
        s_o = sem("o")
        s_y = sem("y")
        block = ctx.enter_context(nc.Block())
        LINKS = 22
        order = list(range(EX, FT)) + list(range(EX))

        @block.sync
        def _(sp):
            sp.dma_start(b1[:, :], b1_cols).then_inc(s_bl, 16)
            sp.dma_start(hp[0:EX, :, :].rearrange("p a b -> p (a b)"), sel[:, 0:4 * P]).then_inc(s_bl, 16)
            sp.dma_start(hr[0:EX, :, :].rearrange("p a b -> p (a b)"), sel[:, 4 * P:8 * P]).then_inc(s_bl, 16)
            sp.dma_start(g1[0:EX, 0:2, :, :].rearrange("p a b c -> p (a b c)")[:, 0:EX * 128 - 8 * P],
                         sel[:, 8 * P:EX * 128]).then_inc(s_bl, 16)
            w.load(sp)
            late.load(sp)

        @block.gpsimd
        def _(pool):
            pool.iota(iota8[:, :], [[1, EX]], base=0, channel_multiplier=0,
                      allow_small_or_imprecise_dtypes=True).then_inc(s_c0, 1)
            late.split(pool)

        @block.tensor
        def _(pe):
            pe.sem_inc(xt.s_used, 1)
            pe.sem_inc(s_o, 1)
            xt.transposes(pe, 0)
            w.wait(pe)
            pe.wait_ge(s_c0, 4)
            with pe.Fori(0, NP) as i:
                xt.wait(pe, i)
                xt.transposes(pe, i + 1)
                pe.wait_ge(s_cc, i + 1)
                for h in range(2):
                    ins = product(pe, banks[:P, 5, EX * h:EX * (h + 1)], xt.parts(), vg, half_of(h), range(KT))
                ins.then_inc(s_g, 1)
                for q, f in enumerate(order):
                    if q == 3:
                        pe.wait_ge(s_gs, LINKS * (i + 1))
                        for h in range(2):
                            ins = pe.transpose(banks[0:EX, 5, 128 + h * P:128 + (h + 1) * P], g1[:, 7, h, :],
                                               ident[:P, :P])
                        ins.then_inc(s_ct, 1)
                    if q == FT - EX:
                        pe.wait_ge(s_cc, i + 2)
                    pe.wait_ge(s_hl, FT * i + q + 1)
                    bank = banks[:, 2 + q % 3, :]
                    ws, col = (v1, f) if f < EX else (vs1, f - EX)
                    ins = product(pe, bank[:, 0:2 * P], ws, xt.parts(), feature_tile(col), range(KT))
                    if f < EX:
                        for n, part in enumerate((cth, ctl)):
                            ins = pe.matmul(bank[:, 2 * P:4 * P], sel_r[:, f, :],
                                            part[0:EX, :, :].rearrange("p h n -> p (h n)"), start=n == 0, stop=n == 1)
                    ins.then_inc(s_h, 1)
                pe.wait_ge(s_h, FT * (i + 1))
                pe.sem_inc(xt.s_used, 1)
                late.wait(pe)
                for h in range(2):
                    pe.wait_ge(s_y, 2 * i + h + 1)
                    out = banks[:P, 6 + h, :]
                    for n, (a, b) in enumerate(((cth, vb[0]), (cth, vb[1]), (ctl, vb[0]))):
                        pe.matmul(out, a[:, h, :], b[:, :], start=n == 0, stop=False)
                    for q, f in enumerate(order):
                        pe.wait_ge(s_hl, FT * i + q + 1 + 3)
                        ins = product(pe, out, ht, v2, half_of(h), [f], first=False, last=q == FT - 1)
                    ins.then_inc(s_o, 1)

        @block.scalar
        def _(act):
            w.high(act)
            xt.high(act, 0)
            act.wait_ge(s_bl, 64)
            with act.Fori(0, NP) as i:
                act.wait_ge(s_gs, LINKS * i + 2)
                act.activation(g1[:, 1], g1[:, 0], ACT.Exp).then_inc(s_ge, 1)
                for q in range(FT + 1):
                    if q < FT:
                        f = order[q]
                        act.wait_ge(s_h, FT * i + q + 1)
                        act.wait_ge(s_hl, FT * i + q + 2)
                        act.activation(hr[:, q % 2, :], banks[:, 2 + q % 3, 0:2 * P], ACT.Relu,
                                       bias=b1[:, f:f + 1]).then_inc(s_r, 1)
                    if q:
                        m, f = q - 1, order[q - 1]
                        if f < EX:
                            act.wait_ge(s_p, EX * i + f + 1)
                        else:
                            act.wait_ge(s_r, FT * i + m + 1)
                        act.copy(ht[0][:, f, :, :].rearrange("p h n -> p (h n)"),
                                 (hp if f < EX else hr)[:, m % 2, :]).then_inc(s_hh, 1)
                xt.high(act, i + 1)

        @block.vector
        def _(dve):
            dve.sem_inc(s_hl, 3)
            dve.sem_inc(s_y, 2)
            dve.wait_ge(s_bl, 64)
            flat_sel = sel_r[:, :, :].rearrange("p e m -> p (e m)")
            dve.tensor_copy(flat_sel[:, 0:4 * P], hp[0:EX, :, :].rearrange("p a b -> p (a b)"))
            dve.tensor_copy(flat_sel[:, 4 * P:8 * P], hr[0:EX, :, :].rearrange("p a b -> p (a b)")).then_inc(s_c0, 1)
            dve.tensor_copy(flat_sel[:, 8 * P:], g1[0:EX, 0:2, :, :].rearrange("p a b c -> p (a b c)")[:, 0:EX * 128 - 8 * P])\
               .then_inc(s_c0, 1)
            dve.memset(cth[:, :, :].bitcast(F32), 1.0).then_inc(s_cc, 1)
            dve.memset(ctl[:, :, :].bitcast(F32), 0.0).then_inc(s_c0, 1)
            dve.wait_ge(s_c0, 4)
            xt.rows(dve, 0)
            w.low(dve)
            xt.low(dve, 0)
            with dve.Fori(0, NP) as i:
                xt.rows(dve, i + 1)
                n = [0]

                def link(ins):
                    n[0] += 1
                    ins.then_inc(s_gs, 1)
                    dve.wait_ge(s_gs, LINKS * i + n[0])

                def wide(a):
                    return a.unsqueeze(2).to_broadcast([P, 2, EX])

                gate = banks[:P, 5, 0:2 * EX].rearrange("p (h e) -> p h e", e=EX)
                many = iota8[:, :].unsqueeze(1).to_broadcast([P, 2, EX])
                dve.wait_ge(s_g, i + 1)
                link(dve.tensor_reduce(g0[:, 0], gate, AX.X, ALU.max))
                link(dve.tensor_tensor(g1[:, 0], gate, wide(g0[:, 0]), ALU.subtract))
                dve.wait_ge(s_ge, i + 1)
                link(dve.tensor_reduce(g0[:, 1], g1[:, 1], AX.X, ALU.add))
                link(dve.reciprocal(g0[:, 2], g0[:, 1]))
                link(dve.tensor_tensor(g1[:, 2], g1[:, 1], wide(g0[:, 2]), ALU.mult))
                for c, seen in ((4, g1[:, 2]), (5, g1[:, 3])):
                    link(dve.tensor_reduce(g0[:, 3], seen, AX.X, ALU.max))
                    link(dve.tensor_tensor(g1[:, 6], seen, wide(g0[:, 3]), ALU.is_lt))
                    link(dve.scalar_tensor_tensor(g1[:, 6], g1[:, 6], float(EX), many, ALU.mult, ALU.add))
                    link(dve.tensor_reduce(g0[:, 4], g1[:, 6], AX.X, ALU.min))
                    link(dve.tensor_tensor(g1[:, c], many, wide(g0[:, 4]), ALU.is_equal))
                    if c == 4:
                        link(dve.scalar_tensor_tensor(g1[:, 3], g1[:, 4], -2.0, g1[:, 2], ALU.mult, ALU.add))
                link(dve.tensor_tensor(g1[:, 4], g1[:, 4], g1[:, 5], ALU.add))
                link(dve.tensor_tensor(g1[:, 6], g1[:, 2], g1[:, 4], ALU.mult))
                link(dve.tensor_reduce(g0[:, 3], g1[:, 6], AX.X, ALU.add))
                link(dve.tensor_scalar(g0[:, 4], g0[:, 3], 1e-20, None, ALU.add))
                link(dve.reciprocal(g0[:, 5], g0[:, 4]))
                link(dve.tensor_tensor(g1[:, 7], g1[:, 6], wide(g0[:, 5]), ALU.mult))
                assert n[0] == LINKS
                dve.wait_ge(s_ct, i + 1)
                tr = banks[0:EX, 5, 128:128 + 2 * P].rearrange("p (h n) -> p h n", n=P)
                dve.wait_ge(s_o, 2 * i + 1)
                dve.tensor_copy(cth[0:EX, :, :], tr).then_inc(s_c1, 1)
                dve.wait_ge(s_c1, i + 1)
                dve.tensor_tensor(ctl[0:EX, :, :], tr, cth[0:EX, :, :].bitcast(F32), ALU.subtract).then_inc(s_cc, 1)
                for q in range(FT + 1):
                    if q < FT and order[q] < EX:
                        f = order[q]
                        dve.wait_ge(s_r, FT * i + q + 1)
                        dve.tensor_tensor(hp[:, q % 2, :], hr[:, q % 2, :], banks[:, 2 + q % 3, 2 * P:4 * P],
                                          ALU.mult).then_inc(s_p, 1)
                    if q:
                        m, f = q - 1, order[q - 1]
                        dve.wait_ge(s_hh, FT * i + m + 1)
                        dve.tensor_tensor(ht[1][:, f, :, :].rearrange("p h n -> p (h n)"),
                                          (hp if f < EX else hr)[:, m % 2, :],
                                          ht[0][:, f, :, :].bitcast(F32).rearrange("p h n -> p (h n)"),
                                          ALU.subtract).then_inc(s_hl, 1)
                xt.low(dve, i + 1)
                for h in range(2):
                    dve.wait_ge(s_o, 2 * i + h + 2)
                    dve.tensor_tensor(flat(x, 2 * i + h), flat(x, 2 * i + h), banks[:P, 6 + h, :],
                                      ALU.add).then_inc(s_y, 1)


def graph_phase(k, x, y, mean, rstd, ident, deg, counts_d, esum_d, wm, wu, bias_rows, gamma, beta):
    nc, banks = k.nc, k.banks
    with ExitStack() as ctx:
        def sb(nm, shape, dt):
            return ctx.enter_context(nc.sbuf_tensor(f"gn_{nm}", shape, dt))

        def sem(nm):
            return k.sem(f"s_gn_{nm}")

        wms = [sb(f"wm{a}", [128, KT, D], F32R) for a in range(2)]
        wus = [sb(f"wu{a}", [128, 2 * KT, D], F32R) for a in range(2)]
        wbs = [sb(f"wb{a}", [2, 2, D], F32R) for a in range(2)]
        w = Weights(k, sb, "gn", [(wm.rearrange("(c p) f -> p c f", p=128), wms[0][:], wms[1][:]),
                                  (bias_rows, wbs[0][:], wbs[1][:])])
        late = Weights(k, sb, "gnl", [(wu.rearrange("(c p) f -> p c f", p=128), wus[0][:], wus[1][:])], stages=1)
        xa = [sb(f"xa{a}", [P, NT, D], F32R) for a in range(2)]
        xf = sb("xf", [P, 2, D], F32)
        row = late.stage[:P, 0, :].rearrange("p (a f) -> p a f", a=2)
        cin = sb("cin", [P, NT, P], U16)
        ein = sb("ein", [P, D], F32)
        cs = [sb(f"cs{a}", [P, NT, P], F32R) for a in range(2)]
        rd = sb("rd", [P, 3, NT], F32)
        ag = sb("ag", [P, 2, D + 2], F32)
        at = [sb(f"at{a}", [128, KT, 2, P], F32R) for a in range(2)]
        gt = sb("gt", [2, 2, P], F32R)
        mt = [sb(f"mt{a}", [128, KT, 2, P], F32R) for a in range(2)]
        xt = Normed(k, sb, "gnx", x, mean, rstd, ident, 0)
        og = sb("og", [P, 2, D], F32)
        stats = sb("stats", [P, NT, nc.vector.BN_STATS_DIM], F32)
        mv = sb("mv", [P, NT, 2], F32)
        lr = sb("lr", [P, 3, NT], F32)
        s_row = sem("row")
        s_xf, s_xh, s_x1 = sem("xf"), sem("xh"), sem("x1")
        s_rd = sem("rd")
        s_in = [sem(f"in{a}") for a in range(2)]
        s_ch, s_cl = sem("ch"), sem("cl")
        s_ag = sem("ag")
        s_e1 = sem("e1")
        s_e2 = sem("e2")
        s_at = sem("at")
        s_ah, s_al = sem("ah"), sem("al")
        s_mp = sem("mp")
        s_mh, s_ml = sem("mh"), sem("ml")
        s_u = sem("u")
        s_ge = sem("ge")
        s_gx, s_go = sem("gx"), sem("go")
        s_bs, s_yb = sem("bs"), sem("yb")
        s_ln, s_sq, s_f1, s_f2 = sem("ln"), sem("sq"), sem("f1"), sem("f2")
        block = ctx.enter_context(nc.Block())

        def tile_of(eng, n):
            return n % NT if isinstance(n, int) else eng.snap(nc.s_assert_within(n % NT, 0, NT - 1))

        @block.sync
        def _(sp):
            def load(n):
                t = tile_of(sp, n)
                sp.wait_ge(s_cl, n + 1)
                sp.dma_start(cin[:, :, :], counts_d[ds(t, 1), :, :, :].rearrange("t p a d -> (t p) a d")).then_inc(s_in[0], 16)
                sp.wait_ge(s_e1, n + 1)
                sp.dma_start(ein[:, :], esum_d[ds(t, 1), :, :].rearrange("t p f -> (t p) f")).then_inc(s_in[1], 16)

            load(0)
            w.load(sp)
            late.load(sp, last=2)
            load(1)
            late.load(sp, first=2, last=4)
            load(2)
            late.load(sp, first=4)
            late.wait(sp)
            sp.dma_start(row[:, 0, :], gamma.partition_broadcast(P)).then_inc(s_row, 16)
            sp.dma_start(row[:, 1, :], beta.partition_broadcast(P)).then_inc(s_row, 16)
            with sp.Fori(0, NP) as i:
                load(2 * i + 3)
                load(2 * i + 4)
            for landed in s_in:
                sp.wait_ge(landed, (NT + 3) * 16)

        @block.gpsimd
        def _(pool):
            late.split(pool)
            pool.wait_ge(s_row, 32)
            with pool.Fori(0, NT) as t:
                pool.tensor_tensor(flat(y, t), flat(y, t), row[:, 1, :], ALU.add).then_inc(s_yb, 1)

        @block.tensor
        def _(pe):
            def sums(n, h):
                pe.wait_ge(s_cl, n + 2)
                pe.wait_ge(s_e1, n + 1)
                for c in range(NT):
                    for m, (a, b) in enumerate(((0, 0), (0, 1), (1, 0))):
                        ins = pe.matmul(banks[:P, 2 + h, :], cs[a][:, c, :], xa[b][:, c, :], start=c == 0 and m == 0,
                                        stop=c == NT - 1 and m == 2)
                ins.then_inc(s_ag, 1)

            pe.sem_inc(xt.s_used, 1)
            pe.sem_inc(s_ag, 1)
            pe.sem_inc(s_at, 2)
            pe.sem_inc(s_mp, 1)
            pe.sem_inc(s_u, 1)
            pe.wait_ge(s_x1, NT)
            for n in range(2):
                sums(n, n)
            xt.transposes(pe, 0)
            w.wait(pe)
            with pe.Fori(0, NP) as i:
                pe.wait_ge(s_ge, 2 * i + 1)
                for h in range(2):
                    pe.wait_ge(s_e2, 2 * i + h + 1)
                    for c in range(KT):
                        pe.transpose(banks[:, 4 + h, c * P:(c + 1) * P], ag[:, h, c * 128:(c + 1) * 128], ident[:P, :P])
                    if h == 0:
                        pe.wait_ge(s_ml, i * KT + 2)
                    pe.transpose(banks[0:2, 6 + h, 0:P], ag[:, h, D:D + 2], ident[:P, :P]).then_inc(s_at, 1)
                sums(2 * i + 2, 0)
                pe.wait_ge(s_al, 2 * i + 2)
                for f in range(KT):
                    pe.wait_ge(s_ml, i * KT + f + 1)
                    out = banks[:, 6 + f % 2, 0:2 * P]
                    product(pe, out, wms, at, feature_tile(f), range(KT), last=False)
                    g = gt[:, :, :].rearrange("p h n -> p (h n)")
                    for a in range(2):
                        ins = pe.matmul(out, wbs[a][:, 0, f * 128:(f + 1) * 128], g, start=False, stop=a == 1)
                    ins.then_inc(s_mp, 1)
                sums(2 * i + 3, 1)
                xt.wait(pe, i)
                xt.transposes(pe, i + 1)
                late.wait(pe)
                pe.wait_ge(s_ml, (i + 1) * KT + 2)
                for h in range(2):
                    out = banks[:P, 4 + h, :]
                    product(pe, out, xt.parts(), wus, half_of(h), range(KT), last=False)
                    product(pe, out, mt, wus, lambda a, b, c: (a[:, c, h, :], b[:, KT + c, :]), range(KT), first=False,
                            last=False)
                    for a in range(2):
                        ins = pe.matmul(out, gt[:, h, :], wbs[a][:, 1, :], start=False, stop=a == 1)
                    ins.then_inc(s_u, 1)
                pe.wait_ge(s_u, 2 * i + 3)
                pe.sem_inc(xt.s_used, 1)

        @block.scalar
        def _(act):
            def counts_high(n):
                act.wait_ge(s_in[0], n * 16 + 16)
                act.wait_ge(s_ag, n + 1)
                act.copy(cs[0][:, :, :], cin[:, :, :]).then_inc(s_ch, 1)

            act.sem_inc(s_ge, 1)
            for t in range(NT):
                act.wait_ge(s_xf, t + 1)
                act.copy(xa[0][:, t, :], xf[:, t % 2, :]).then_inc(s_xh, 1)
            counts_high(0)
            w.high(act)
            for n in (1, 2):
                counts_high(n)
            xt.high(act, 0)
            with act.Fori(0, NP) as i:
                act.wait_ge(s_mp, KT * i + 1)
                act.wait_ge(s_u, 2 * i + 1)
                for h in range(2):
                    act.wait_ge(s_at, 2 * i + h + 3)
                    act.copy(at[0][:, :, h, :], banks[:, 4 + h, 0:KT * P].rearrange("p (c n) -> p c n", n=P))
                    act.copy(gt[:, h, :], banks[0:2, 6 + h, 0:P]).then_inc(s_ah, 1)
                counts_high(2 * i + 3)
                for f in range(KT):
                    act.wait_ge(s_mp, KT * i + f + 2)
                    act.copy(mt[0][:, f, :, :].rearrange("p h n -> p (h n)"), banks[:, 6 + f % 2, 0:2 * P]).then_inc(s_mh, 1)
                counts_high(2 * i + 4)
                for h in range(2):
                    act.wait_ge(s_u, 2 * i + h + 2)
                    act.wait_ge(s_go, 2 * i + h + 1)
                    act.activation(og[:, h, :], banks[:P, 4 + h, :], ACT.Gelu).then_inc(s_ge, 1)
                xt.high(act, i + 1)
            act.wait_ge(s_ln, 1)
            act.activation(lr[:, 1, :], lr[:, 0, :], ACT.Sqrt).then_inc(s_sq, 1)

        @block.vector
        def _(dve):
            def counts_low(n):
                dve.wait_ge(s_ch, n + 1)
                dve.tensor_tensor(cs[1][:, :, :], cin[:, :, :], cs[0][:, :, :].bitcast(F32),
                                  ALU.subtract).then_inc(s_cl, 1)

            def average(n, h):
                t = tile_of(dve, n)
                dve.wait_ge(s_in[1], n * 16 + 16)
                dve.wait_ge(s_ag, n + 2)
                dve.wait_ge(s_at, n + 1)
                dve.tensor_tensor(ag[:, h, 0:D], banks[:P, 2 + h, :], ein[:, :], ALU.add).then_inc(s_e1, 1)
                dve.tensor_copy(ag[:, h, D:D + 1], rd[:, 2, ds(t, 1)])
                dve.wait_ge(s_e1, n + 2)
                dve.tensor_scalar(ag[:, h, 0:D], ag[:, h, 0:D], rd[:, 1, ds(t, 1)], None, ALU.mult).then_inc(s_e2, 1)

            dve.sem_inc(s_cl, 1)
            dve.sem_inc(s_e1, 1)
            dve.sem_inc(s_ml, 2)
            dve.sem_inc(s_go, 2)
            for t in range(NT + 1):
                if t < NT:
                    if t >= 2:
                        dve.wait_ge(s_x1, t - 1)
                    dve.tensor_scalar(xf[:, t % 2, :], x[:, t, :], mean[:, t:t + 1], rstd[:, t:t + 1], ALU.subtract,
                                      ALU.mult).then_inc(s_xf, 1)
                if 1 <= t <= NT:
                    dve.wait_ge(s_xh, t)
                    dve.wait_ge(s_xf, t)
                    dve.tensor_tensor(xa[1][:, t - 1, :], xf[:, (t - 1) % 2, :], xa[0][:, t - 1, :].bitcast(F32),
                                      ALU.subtract).then_inc(s_x1, 1)
            counts_low(0)
            link = chain(dve, s_rd)
            link(dve.tensor_scalar(rd[:, 0, :], deg[:, :], 1.0, None, ALU.max))
            link(dve.reciprocal(rd[:, 1, :], rd[:, 0, :]))
            link(dve.tensor_tensor(rd[:, 2, :], deg[:, :], rd[:, 1, :], ALU.mult))
            dve.memset(ag[:, :, D + 1:D + 2], 1.0)
            dve.wait_ge(s_x1, NT)
            w.low(dve)
            counts_low(1)
            average(0, 0)
            xt.rows(dve, 0)
            counts_low(2)
            average(1, 1)
            xt.low(dve, 0)
            with dve.Fori(0, NP) as i:
                for h in range(2):
                    dve.wait_ge(s_ah, 2 * i + h + 1)
                    dve.tensor_tensor(at[1][:, :, h, :], banks[:, 4 + h, 0:KT * P].rearrange("p (c n) -> p c n", n=P),
                                      at[0][:, :, h, :].bitcast(F32), ALU.subtract).then_inc(s_al, 1)
                for h in range(2):
                    t = 2 * i + h
                    dve.wait_ge(s_go, t + 1)
                    dve.tensor_scalar(xf[:, h, :], flat(x, t), mean[:, ds(t, 1)], rstd[:, ds(t, 1)], ALU.subtract,
                                      ALU.mult).then_inc(s_gx, 1)
                xt.rows(dve, i + 1)
                counts_low(2 * i + 3)
                average(2 * i + 2, 0)
                for f in range(KT):
                    dve.wait_ge(s_mh, KT * i + f + 1)
                    dve.tensor_tensor(mt[1][:, f, :, :].rearrange("p h n -> p (h n)"), banks[:, 6 + f % 2, 0:2 * P],
                                      mt[0][:, f, :, :].bitcast(F32).rearrange("p h n -> p (h n)"),
                                      ALU.subtract).then_inc(s_ml, 1)
                counts_low(2 * i + 4)
                average(2 * i + 3, 1)
                for h in range(2):
                    t = 2 * i + h
                    dve.wait_ge(s_gx, t + 1)
                    dve.wait_ge(s_ge, t + 2)
                    dve.tensor_tensor(flat(x, t), xf[:, h, :], og[:, h, :], ALU.add).then_inc(s_go, 1)
                xt.low(dve, i + 1)
                for h in range(2):
                    t = 2 * i + h
                    dve.wait_ge(s_go, t + 3)
                    dve.bn_stats(flat(stats, t), flat(x, t)).then_inc(s_bs, 1)
            dve.wait_ge(s_bs, NT)
            for t in range(NT):
                dve.bn_aggr(mv[:, t, :], stats[:, t, :]).then_inc(s_bs, 1)
            dve.wait_ge(s_bs, 2 * NT)
            dve.tensor_scalar(lr[:, 0, :], mv[:, :, 1], EPS, None, ALU.add).then_inc(s_ln, 1)
            dve.wait_ge(s_sq, 1)
            dve.reciprocal(lr[:, 2, :], lr[:, 1, :]).then_inc(s_ln, 1)
            dve.wait_ge(s_ln, 2)
            dve.wait_ge(s_row, 32)
            dve.wait_ge(s_yb, NT)
            with dve.Fori(0, NP) as i:
                for h in range(2):
                    t = 2 * i + h
                    dve.scalar_tensor_tensor(flat(x, t), flat(x, t), mv[:, ds(t, 1), 0], row[:, 0, :], ALU.subtract,
                                             ALU.mult).then_inc(s_f1, 1)
                for h in range(2):
                    t = 2 * i + h
                    dve.wait_ge(s_f1, t + 1)
                    dve.scalar_tensor_tensor(flat(y, t), flat(x, t), lr[:, 2, ds(t, 1)], flat(y, t), ALU.mult,
                                             ALU.add).then_inc(s_f2, 1)


def pooled_phase(k, x, mean, rstd, ident, attn_w, attn_b, gate_w, gate_b, w1, b1_cols, w2, b2):
    nc, banks = k.nc, k.banks
    EX, HT, TOP = 8, 2, 2
    with ExitStack() as ctx:
        def sb(nm, shape, dt):
            return ctx.enter_context(nc.sbuf_tensor(f"po_{nm}", shape, dt))

        def sem(nm):
            return k.sem(f"s_po_{nm}")

        chosen = sb("chosen", [1, TOP], I32)
        gcol = sb("gcol", [P, TOP], F32)
        ones = sb("ones", [P, 128], F32)

        with ExitStack() as inner:
            def sbi(nm, shape, dt):
                return inner.enter_context(nc.sbuf_tensor(f"po_{nm}", shape, dt))

            aw = sbi("aw", [P, D], F32)
            ab = sbi("ab", [P, 1], F32)
            gw = sbi("gw", [128, KT, EX], F32)
            gb = sbi("gb", [1, EX], F32)
            xa = sbi("xa", [P, NT, D], F32)
            xw = sbi("xw", [P, 2, D], F32)
            sc = sbi("sc", [P, 2, NT], F32)
            top = sbi("top", [128, 2], F32)
            glob = sbi("glob", [128, 1], F32)
            tot = sbi("tot", [128, 1], F32)
            pl = sbi("pl", [128, KT], F32)
            r1 = sbi("r1", [1, 8, EX], F32)
            r0 = sbi("r0", [1, 8], F32)
            gn = sbi("gn", [1, TOP], F32)
            iota8 = sbi("iota8", [1, EX], F32)
            s_in, s_c, s_x, s_m, s_w, s_s = sem("in"), sem("c"), sem("x"), sem("m"), sem("w"), sem("s")
            s_all, s_e, s_pl, s_gl, s_ge, s_gb = sem("all"), sem("e"), sem("pl"), sem("gl"), sem("ge"), sem("gb")
            block = inner.enter_context(nc.Block())

            @block.sync
            def _(sp):
                sp.dma_start(aw[:, :], attn_w.partition_broadcast(P)).then_inc(s_in, 16)
                sp.dma_start(ab[:, :], attn_b.partition_broadcast(P)).then_inc(s_in, 16)
                sp.dma_start(gw[:, :, :], gate_w.rearrange("(c p) e -> p c e", p=128)).then_inc(s_in, 16)
                sp.dma_start(gb[:, :], gate_b.partition_broadcast(1)).then_inc(s_in, 16)

            @block.gpsimd
            def _(pool):
                pool.memset(ones[:, :], 1.0)
                pool.iota(iota8[:, :], [[1, EX]], base=0, channel_multiplier=0,
                          allow_small_or_imprecise_dtypes=True).then_inc(s_c, 1)
                pool.wait_ge(s_s, 4)
                pool.partition_all_reduce(glob[:, :], top[:, 0:1], 128, bass.bass_isa.ReduceOp.max).then_inc(s_all, 1)

            @block.vector
            def _(dve):
                dve.wait_ge(s_in, 64)
                for t in range(NT + 2):
                    if t < NT:
                        dve.tensor_scalar(xa[:, t, :], x[:, t, :], mean[:, t:t + 1], rstd[:, t:t + 1], ALU.subtract,
                                          ALU.mult).then_inc(s_x, 1)
                    if t >= 2:
                        dve.wait_ge(s_m, t - 1)
                        dve.tensor_reduce(sc[:, 0, t - 2:t - 1], xw[:, t % 2, :], AX.X, ALU.add).then_inc(s_w, 1)
                    if 1 <= t <= NT:
                        dve.wait_ge(s_x, t)
                        if t >= 3:
                            dve.wait_ge(s_w, t - 2)
                        dve.tensor_tensor(xw[:, (t - 1) % 2, :], xa[:, t - 1, :], aw[:, :], ALU.mult).then_inc(s_m, 1)
                dve.memset(top[:, :], -3e38).then_inc(s_w, 1)
                dve.wait_ge(s_w, NT + 1)
                link = chain(dve, s_s)
                link(dve.tensor_scalar(sc[:, 0, :], sc[:, 0, :], ab[:, :], None, ALU.add))
                link(dve.tensor_reduce(top[:P, 0:1], sc[:, 0, :], AX.X, ALU.max))
                link(dve.tensor_copy(r0[:, 0:1], gb[:, 0:1]))
                link(dve.tensor_copy(r0[:, 1:2], gb[:, 0:1]))
                dve.wait_ge(s_all, 1)
                link(dve.tensor_scalar(top[:, 1:2], glob[:, :], -1.0, None, ALU.mult))
                dve.wait_ge(s_pl, 1)
                link(dve.reciprocal(tot[:, :], banks[:, 1, 0:1]))
                link(dve.tensor_scalar(pl[:, :], banks[:, 0, 0:KT], tot[:, :], None, ALU.mult))
                dve.wait_ge(s_gl, 1)
                link(dve.tensor_tensor(r1[:, 0], banks[0:1, 2, 0:EX], gb[:, :], ALU.add))
                link(dve.tensor_reduce(r0[:, 0:1], r1[:, 0], AX.X, ALU.max))
                link(dve.tensor_scalar(r1[:, 1], r1[:, 0], r0[:, 0:1], None, ALU.subtract))
                dve.wait_ge(s_ge, 1)
                link(dve.tensor_reduce(r0[:, 1:2], r1[:, 2], AX.X, ALU.add))
                link(dve.reciprocal(r0[:, 2:3], r0[:, 1:2]))
                link(dve.tensor_scalar(r1[:, 3], r1[:, 2], r0[:, 2:3], None, ALU.mult))
                dve.wait_ge(s_c, 1)
                for j, seen in ((0, r1[:, 3]), (1, r1[:, 4])):
                    best, least = r0[:, 3 + j:4 + j], r0[:, 5:6]
                    link(dve.tensor_reduce(best, seen, AX.X, ALU.max))
                    link(dve.tensor_scalar(r1[:, 5], seen, best, float(EX), ALU.is_lt, ALU.mult))
                    link(dve.tensor_tensor(r1[:, 5], r1[:, 5], iota8[:, :], ALU.add))
                    link(dve.tensor_reduce(least, r1[:, 5], AX.X, ALU.min))
                    link(dve.tensor_copy(chosen[:, j:j + 1], least))
                    if j == 0:
                        link(dve.tensor_scalar(r1[:, 6], iota8[:, :], least, -2.0, ALU.is_equal, ALU.mult))
                        link(dve.tensor_tensor(r1[:, 4], r1[:, 6], r1[:, 3], ALU.add))
                link(dve.tensor_tensor(r0[:, 6:7], r0[:, 3:4], r0[:, 4:5], ALU.add))
                link(dve.tensor_scalar(r0[:, 6:7], r0[:, 6:7], 1e-9, None, ALU.add))
                link(dve.reciprocal(r0[:, 7:8], r0[:, 6:7]))
                link(dve.tensor_scalar(gn[:, :], r0[:, 3:5], r0[:, 7:8], None, ALU.mult))
                dve.sem_inc(s_gb, 1)
                dve.wait_ge(s_gb, 2)
                dve.tensor_copy(gcol[:, :], banks[:P, 3, 0:TOP])

            @block.scalar
            def _(act):
                act.wait_ge(s_s, 5)
                act.activation(sc[:, 1, :], sc[:, 0, :], ACT.Exp, bias=top[:P, 1:2]).then_inc(s_e, 1)
                act.wait_ge(s_s, 10)
                act.activation(r1[:, 2], r1[:, 1], ACT.Exp).then_inc(s_ge, 1)

            @block.tensor
            def _(pe):
                pe.wait_ge(s_c, 1)
                pe.wait_ge(s_e, 1)
                for c in range(KT):
                    for t in range(NT):
                        pe.matmul(banks[:, 0, c:c + 1], xa[:, t, c * 128:(c + 1) * 128], sc[:, 1, t:t + 1],
                                  start=t == 0, stop=t == NT - 1)
                for t in range(NT):
                    ins = pe.matmul(banks[:, 1, 0:1], ones[:, :], sc[:, 1, t:t + 1], start=t == 0, stop=t == NT - 1)
                ins.then_inc(s_pl, 1)
                pe.wait_ge(s_s, 7)
                for c in range(KT):
                    ins = pe.matmul(banks[0:1, 2, 0:EX], pl[:, c:c + 1], gw[:, c, :], start=c == 0, stop=c == KT - 1)
                ins.then_inc(s_gl, 1)
                pe.wait_ge(s_gb, 1)
                pe.matmul(banks[:P, 3, 0:TOP], ones[0:1, 0:P], gn[:, :], start=True, stop=True).then_inc(s_gb, 1)

        FT = TOP * HT
        v1 = [sb(f"v1{a}", [128, KT, FT * 128], F32R) for a in range(2)]
        v2 = [sb(f"v2{a}", [128, FT, D], F32R) for a in range(2)]
        vb = [sb(f"vb{a}", [1, TOP, D], F32R) for a in range(2)]
        b1 = sb("b1", [128, FT], F32)
        one_r = sb("one_r", [1, P + 1], F32R)

        def source(a, j, form, **sizes):
            return lambda e: a[ds(e[j], 1)].rearrange(form, **sizes)

        pieces = []
        for j in range(TOP):
            c = slice(j * HT * 128, (j + 1) * HT * 128)
            pieces.append((source(w1, j, "a (c p) f -> p (a c) f", p=128), v1[0][:, :, c], v1[1][:, :, c]))
        w = Weights(k, sb, "po", pieces)
        pieces = []
        for j in range(TOP):
            c = slice(j * HT, (j + 1) * HT)
            pieces.append((source(w2, j, "a (c p) f -> p (a c) f", p=128), v2[0][:, c, :], v2[1][:, c, :]))
            pieces.append((source(b2, j, "a f -> a f"), vb[0][:, j, :], vb[1][:, j, :]))
        late = Weights(k, sb, "pol", pieces)
        xt = Normed(k, sb, "pox", x, mean, rstd, ident, 0)
        hf = sb("hf", [128, 2, 2 * P], F32)
        ht = [sb(f"ht{a}", [128, FT, 2, P], F32R) for a in range(2)]
        eo = sb("eo", [P, 2, D], F32)
        s_b1, s_one = sem("b1"), sem("one")
        s_h = sem("h")
        s_f = sem("f")
        s_hh, s_hl = sem("hh"), sem("hl")
        s_o = sem("o")
        s_g = sem("g")
        s_y = sem("y")
        block = ctx.enter_context(nc.Block())

        @block.sync
        def _(sp):
            e = [sp.value_load(chosen[0:1, j:j + 1], min_val=0, max_val=EX - 1) for j in range(TOP)]
            for j in range(TOP):
                sp.dma_start(b1[:, j * HT:(j + 1) * HT], b1_cols[ds(e[j], 1)].rearrange("a p f -> (a p) f"))\
                  .then_inc(s_b1, 16)
            w.load(sp, e)
            late.load(sp, e)

        @block.gpsimd
        def _(pool):
            late.split(pool)

        @block.tensor
        def _(pe):
            pe.sem_inc(xt.s_used, 1)
            xt.transposes(pe, 0)
            w.wait(pe)
            pe.wait_ge(s_one, 1)
            with pe.Fori(0, NP) as i:
                xt.wait(pe, i)
                xt.transposes(pe, i + 1)
                for f in range(FT):
                    pe.wait_ge(s_hl, FT * i + f + 1)
                    product(pe, banks[:, 2 + f % 2, 0:2 * P], v1, xt.parts(), feature_tile(f),
                            range(KT)).then_inc(s_h, 1)
                pe.wait_ge(s_h, FT * (i + 1))
                pe.sem_inc(xt.s_used, 1)
                pe.wait_ge(s_hl, FT * (i + 1) + 2)
                late.wait(pe)
                for n in range(2 * TOP):
                    h, j = divmod(n, TOP)
                    pe.wait_ge(s_g, 2 * TOP * i + n + 1)
                    out = banks[:P, 4 + n % 2, :]
                    product(pe, out, ht, v2, half_of(h), range(j * HT, (j + 1) * HT), last=False)
                    for a in range(2):
                        ins = pe.matmul(out, one_r[:, 0:P], vb[a][:, j, :], start=False, stop=a == 1)
                    ins.then_inc(s_o, 1)

        @block.scalar
        def _(act):
            act.sem_inc(s_g, 2)
            w.high(act)
            xt.high(act, 0)
            act.wait_ge(s_b1, 16 * TOP)
            with act.Fori(0, NP) as i:
                for f in range(FT):
                    act.wait_ge(s_h, FT * i + f + 1)
                    act.wait_ge(s_hl, FT * i + f + 1)
                    act.activation(hf[:, f % 2, :], banks[:, 2 + f % 2, 0:2 * P], ACT.Gelu,
                                   bias=b1[:, f:f + 1]).then_inc(s_f, 1)
                    act.wait_ge(s_f, FT * i + f + 1)
                    act.copy(ht[0][:, f, :, :].rearrange("p h n -> p (h n)"), hf[:, f % 2, :]).then_inc(s_hh, 1)
                xt.high(act, i + 1)
                for n in range(2 * TOP):
                    act.wait_ge(s_o, 2 * TOP * i + n + 1)
                    act.wait_ge(s_y, 2 * TOP * i + n + 1)
                    act.activation(eo[:, n % 2, :], banks[:P, 4 + n % 2, :], ACT.Gelu).then_inc(s_g, 1)

        @block.vector
        def _(dve):
            dve.sem_inc(s_hl, 2)
            dve.sem_inc(s_y, 2)
            dve.memset(one_r[:, :].bitcast(F32), 1.0).then_inc(s_one, 1)
            xt.rows(dve, 0)
            w.low(dve)
            xt.low(dve, 0)
            with dve.Fori(0, NP) as i:
                xt.rows(dve, i + 1)
                for f in range(FT):
                    dve.wait_ge(s_hh, FT * i + f + 1)
                    dve.tensor_tensor(ht[1][:, f, :, :].rearrange("p h n -> p (h n)"), hf[:, f % 2, :],
                                      ht[0][:, f, :, :].bitcast(F32).rearrange("p h n -> p (h n)"),
                                      ALU.subtract).then_inc(s_hl, 1)
                xt.low(dve, i + 1)
                for n in range(2 * TOP):
                    h, j = divmod(n, TOP)
                    t = 2 * i + h
                    dve.wait_ge(s_g, 2 * TOP * i + n + 3)
                    if j:
                        dve.wait_ge(s_y, 2 * TOP * i + n + 2)
                    dve.scalar_tensor_tensor(flat(x, t), eo[:, n % 2, :], gcol[:, j:j + 1], flat(x, t), ALU.mult,
                                             ALU.add).then_inc(s_y, 1)


def graph_transformer(nc, x_in, src, dst, edge_attr, ident_in, mask_in, head_cols, head_rows, sel_in, mean_in,
                      wq, wk, wv, bn_gamma, bn_beta, mix0_wqkv, mix0_wout, mix0_bout,
                      f0_gate, f0_w1, f0_sw1, f0_w2, f0_sw2, f0_b1, f0_b2,
                      gn_wm, gn_wu, gn_bias, gn_gamma, gn_beta,
                      mix1_wqkv, mix1_b, mix1_bq, mix1_wout, mix1_bout, mix1_gamma, mix1_beta,
                      f1_attn_w, f1_attn_b, f1_gate_w, f1_gate_b, f1_w1, f1_b1, f1_w2, f1_b2, out):
    counts_d = nc.dram_tensor("edge_counts", [NT, P, NT, P], U16).ap()
    esum_d = nc.dram_tensor("edge_sums", [NT, P, D], F32).ap()
    with ExitStack() as ctx:
        k = Kernel(nc, ctx)
        ident = k.keep("ident", [128, 128], F32)
        mask = k.keep("mask", [128, 128], F32)
        ones_n = k.keep("ones_n", [128, 128], F32)
        mean = k.keep("mean", [P, NT], F32)
        rstd = k.keep("rstd", [P, NT], F32)
        again = k.keep("again", [P, NT], F32)
        deg = k.keep("deg", [P, NT], F32)
        s_const = k.sem("s_const")
        s_x = k.sem("s_x")
        s_store = k.sem("s_store")

        with ExitStack() as outer:
            counts = outer.enter_context(nc.sbuf_tensor("counts", [P, NT, NT, P], U16))
            with ExitStack() as inner:
                esum = inner.enter_context(nc.sbuf_tensor("esum", [P, NT, D], F32))
                with nc.Block() as block:
                    @block.sync
                    def _(sp):
                        sp.dma_start(ident[:, :], ident_in).then_inc(s_const, 16)
                        sp.dma_start(mask[:, :], mask_in).then_inc(s_const, 16)
                        sp.dma_start(ones_n[:, :], mean_in).then_inc(s_const, 16)
                        sp.wait_ge(s_const, 48)
                edge_phase(k, src, dst, edge_attr, counts, esum, deg, ident)
                with nc.Block() as block:
                    @block.sync
                    def _(sp):
                        for t in range(NT):
                            sp.dma_start(counts_d[t], counts[:, t, :, :]).then_inc(s_store, 16)
                            sp.dma_start(esum_d[t], esum[:, t, :]).then_inc(s_store, 16)
                        sp.wait_ge(s_store, 2 * NT * 16)
        with ExitStack() as rows:
            x = rows.enter_context(nc.sbuf_tensor("rows_x", [P, NT, D], F32))
            y = rows.enter_context(nc.sbuf_tensor("rows_y", [P, NT, D], F32))
            with ExitStack() as inner:
                counts = inner.enter_context(nc.sbuf_tensor("counts_back", [P, NT, NT, P], U16))
                with nc.Block() as block:
                    @block.sync
                    def _(sp):
                        for t in range(NT):
                            sp.dma_start(x[:, t, :], x_in[t * P:(t + 1) * P, :]).then_inc(s_x, 16)
                            sp.dma_start(counts[:, t, :, :], counts_d[t]).then_inc(s_x, 16)
                        sp.wait_ge(s_x, 2 * NT * 16)
                statistics(k, "st0", x, mean, rstd)
                attention_phase(k, x, y, mean, rstd, counts, ident, wq, wk, wv)
            batchnorm_phase(k, x, y, ones_n, bn_gamma, bn_beta)
            k.clear()
            mix_phase(k, "mix0", x, y, mean, rstd, ident, mask, head_cols, head_rows, mix0_wqkv, None, None, mix0_wout, mix0_bout)
            x, y = y, x
            statistics(k, "st1", x, mean, rstd)
            experts_phase(k, x, mean, rstd, ident, sel_in, f0_gate, f0_w1, f0_sw1, f0_w2, f0_sw2, f0_b1, f0_b2)
            k.clear()
            statistics(k, "st2", x, mean, rstd, again)
            mix_phase(k, "mix1", x, y, mean, again, ident, mask, head_cols, head_rows, mix1_wqkv, mix1_b, mix1_bq, mix1_wout, mix1_bout,
                      affine=(mix1_gamma, mix1_beta), base=(mean, rstd))
            graph_phase(k, x, y, mean, rstd, ident, deg, counts_d, esum_d, gn_wm, gn_wu, gn_bias, gn_gamma, gn_beta)
            statistics(k, "st3", y, mean, rstd)
            pooled_phase(k, y, mean, rstd, ident, f1_attn_w, f1_attn_b, f1_gate_w, f1_gate_b, f1_w1, f1_b1, f1_w2, f1_b2)
            s_out = k.sem("s_out")
            with nc.Block() as block:
                @block.sync
                def _(sp):
                    for t in range(NT):
                        sp.dma_start(out[t * P:(t + 1) * P, :], y[:, t, :]).then_inc(s_out, 16)
                    sp.wait_ge(s_out, NT * 16)


def lay_out(i):
    def swap(name, *axes):
        return i[name].transpose(*axes) if axes else i[name].T

    def edges(name, pad):
        a = np.pad(i[name], (0, G * GE - E), constant_values=pad)
        return a.reshape(G * GC, EC).T

    bm, bu = i["L1_gnn_bm"], i["L1_gnn_bu"]
    zero = np.zeros_like(bm)
    return {
        "x": i["x"],
        "src": edges("src", 4095),
        "dst": edges("dst", N - 1),
        "edge_attr": np.pad(i["edge_attr_512"], ((0, G * GE - E), (0, 0))),
        "identity": np.eye(128, dtype=np.float32),
        "head_mask": np.kron(np.eye(2), np.ones((DH, DH))).astype(np.float32),
        "head_cols": np.repeat(np.eye(H, dtype=np.float32), DH, 0).reshape(KT, 128, H).transpose(1, 0, 2),
        "head_rows": np.repeat(np.eye(H, dtype=np.float32), DH, 1).reshape(H, KT, 128),
        "selector": np.repeat(np.eye(8, dtype=np.float32), 128, 1),
        "mean_of_nodes": np.full((128, 128), 1.0 / N, np.float32),
        "wq": i["L0_gnn_Wq"], "wk": i["L0_gnn_Wk"], "wv": i["L0_gnn_Wv"],
        "bn_gamma": i["L0_gnn_bn_gamma"], "bn_beta": i["L0_gnn_bn_beta"],
        "mix0_wqkv": i["L0_mix_w_qkv"], "mix0_wout": i["L0_mix_w_out"], "mix0_bout": i["L0_mix_b_out"],
        "f0_gate": swap("L0_ffn_gate_w"),
        "f0_w1": swap("L0_ffn_w1", 1, 0, 2).reshape(D, -1),
        "f0_sw1": i["L0_ffn_sw1"], "f0_w2": i["L0_ffn_w2"], "f0_sw2": i["L0_ffn_sw2"],
        "f0_b1": np.concatenate([swap("L0_ffn_b1"), i["L0_ffn_sb1"].reshape(4, 128).T], 1),
        "f0_b2": np.concatenate([i["L0_ffn_b2"], i["L0_ffn_sb2"][None]]),
        "gn_wm": swap("L1_gnn_Wm"), "gn_wu": swap("L1_gnn_Wu"),
        "gn_bias": np.stack([np.stack([bm, zero]), np.stack([zero, bu])]),
        "gn_gamma": i["L1_gnn_gamma"], "gn_beta": i["L1_gnn_beta"],
        "mix1_wqkv": swap("L1_mix_qkv_w"), "mix1_b": i["L1_mix_qkv_b"],
        "mix1_bq": i["L1_mix_qkv_b"][:D].reshape(4, 128).T,
        "mix1_wout": swap("L1_mix_out_w"), "mix1_bout": i["L1_mix_out_b"],
        "mix1_gamma": i["L1_mix_ln_gamma"], "mix1_beta": i["L1_mix_ln_beta"],
        "f1_attn_w": i["L1_ffn_attn_w"].reshape(D), "f1_attn_b": i["L1_ffn_attn_b"],
        "f1_gate_w": i["L1_ffn_gate_w"], "f1_gate_b": i["L1_ffn_gate_b"],
        "f1_w1": i["L1_ffn_w1"], "f1_b1": swap("L1_ffn_b1").reshape(2, 128, 8).transpose(2, 1, 0),
        "f1_w2": i["L1_ffn_w2"], "f1_b2": i["L1_ffn_b2"],
    }


def kernel(**inputs):
    import concourse.bacc as _bacc
    from concourse.bass_utils import run_bass_kernel_spmd as _run

    nc = _bacc.Bacc("TRN2", target_bir_lowering=False, num_devices=1)
    arrays, args = {}, []
    for name, a in lay_out({name: np.asarray(a) for name, a in inputs.items()}).items():
        arrays[f"in_{name}_dram"] = np.ascontiguousarray(a)
        args.append(nc.dram_tensor(f"in_{name}_dram", a.shape, mybir.dt.from_np(a.dtype), kind="ExternalInput").ap())
    args.append(nc.dram_tensor("out_dram", (N, D), F32, kind="ExternalOutput").ap())
    graph_transformer(nc, *args)
    return _run(nc, [arrays], core_ids=[0]).results[0]["out_dram"]
```

```python
import concourse.bass as bass
from concourse import mybir
from contextlib import ExitStack

import numpy as np

F32 = mybir.dt.float32
F32R = mybir.dt.float32r
BF16 = mybir.dt.bfloat16
FP16 = mybir.dt.float16
I32 = mybir.dt.int32
U16 = mybir.dt.uint16
ALU = mybir.AluOpType
ACT = mybir.ActivationFunctionType
AX = mybir.AxisListType
ds = bass.ds

N = 1250
D = 512
E = 41250
H = 8
DH = D // H
P = 125
NT = N // P
NP = NT // 2
KT = D // 128
EC = 128
GC = 6
GE = GC * EC
G = -(-E // GE)
STAGE = 2 * D
POOL_LO = (0, 1, 3, 4)
EPS = 1e-5


class Kernel:

    def __init__(self, nc, ctx):
        self.nc, self.ctx = nc, ctx
        self.banks = ctx.enter_context(nc.psum_tensor("banks", [128, 8, 512], F32))
        self.sems = []

    def sem(self, name):
        self.sems.append(self.nc.alloc_semaphore(name=name))
        return self.sems[-1]

    def clear(self):
        self.nc.clear_and_free_semaphores(self.sems)
        self.nc.all_engine_barrier()
        self.sems = []

    def keep(self, name, shape, dt):
        return self.ctx.enter_context(self.nc.sbuf_tensor(name, shape, dt))


def edge_phase(k, src, dst, edge_attr, counts, esum_d, deg, ident, x_in, x, stats):
    nc = k.nc
    ctx = ExitStack()
    with ctx:
        def sb(name, shape, dt):
            return ctx.enter_context(nc.sbuf_tensor(name, shape, dt))

        SW = 418
        idx_i = sb("idx_i", [128, 2, G * GC], I32)
        dst_f = sb("dst_f", [128, G * GC], F32)
        src_f = sb("src_f", [128, G * GC], F32)
        gext = sb("gext", [128, 2, G], F32)
        gall = sb("gall", [128, 2, G], F32)
        tcol = sb("tcol", [1, 2, NT, G], F32)
        gnum = sb("gnum", [1, 2, NT, G], F32)
        tmask = sb("tmask", [1, 3, NT, G], F32)
        tlim = sb("tlim", [1, 6, NT], F32)
        tab = sb("tab", [1, 3, NT], I32)
        iota_s = sb("iota_s", [128, 3 * SW], FP16)
        iota_t = sb("iota_t", [128, NT, P + 1], FP16)
        raw = sb("raw", [128, GC, D], F32)
        e_hi = sb("e_hi", [128, GC, D], F32R)
        e_lo = sb("e_lo", [128, GC, D], F32R)
        oh_s = sb("oh_s", [128, GC, 3 * SW], BF16)
        oh_d = sb("oh_d", [128, GC, P + 1], F32R)
        oh_db = oh_d[:, :, :].bitcast(BF16).rearrange("p c (n two) -> p c n two", two=2)[:, :, :, 1]
        zero_b = sb("zero_b", [128, D], BF16)
        ct = sb("ct", [128, 3 * SW], F32)
        es = sb("es", [P, D], F32)

        s_idx = k.sem("s_idx")
        s_iota = k.sem("s_iota")
        s_big = k.sem("s_big")
        s_prep = k.sem("s_prep")
        s_all = k.sem("s_all")
        s_tab = k.sem("s_tab")
        s_raw = [k.sem(f"s_raw{c}") for c in range(GC)]
        s_hi = [k.sem(f"s_hi{c}") for c in range(GC)]
        s_lo = [k.sem(f"s_lo{c}") for c in range(GC)]
        s_oh = [k.sem(f"s_oh{c}") for c in range(GC)]
        s_use = [k.sem(f"s_use{c}") for c in range(GC)]
        s_fin = k.sem("s_fin")
        s_ct = k.sem("s_ct")
        s_es = k.sem("s_es")
        s_ste = k.sem("s_ste")
        s_x = k.sem("s_x")
        s_xu = k.sem("s_xu")
        s_tr = k.sem("s_tr")
        s_tre = k.sem("s_tre")

        banks = k.banks
        block = ctx.enter_context(nc.Block())
        edge_h = edge_attr.rearrange("(c p) f -> c p f", p=EC)

        def visits(eng, t):
            v0 = eng.value_load(tab[0:1, 0, ds(t, 1)], min_val=0, max_val=NT * G)
            v1 = eng.value_load(tab[0:1, 1, ds(t, 1)], min_val=1, max_val=NT * G)
            return v0, v1

        @block.sync
        def _(sp):
            sp.dma_start(idx_i[:, 0, :], src).then_inc(s_idx, 16)
            sp.dma_start(idx_i[:, 1, :], dst).then_inc(s_idx, 16)
            sp.wait_ge(s_tab, 1)
            with sp.Fori(0, NT) as t:
                v0, v1 = visits(sp, t)
                shift = sp.value_load(tab[0:1, 2, ds(t, 1)], min_val=0, max_val=2 * NT * G)
                with sp.Fori(v0, v1) as v:
                    g = sp.snap(nc.s_assert_within(v + shift - NT * G, 0, G - 1))
                    for c in range(GC):
                        sp.wait_ge(s_lo[c], v + 1)
                        sp.dma_start(raw[:, c, :], edge_h[ds(GC * g + c, 1), :, :].rearrange("a p f -> (a p) f"))\
                          .then_inc(s_raw[c], 16)
            sp.wait_ge(s_ste, NT * 16 + 16)
            sp.wait_ge(s_x, NT * 16 + 16)

        @block.gpsimd
        def _(pool):
            pool.iota(tcol[:, 0, :, :], [[P, NT], [0, G]], base=0, channel_multiplier=0,
                      allow_small_or_imprecise_dtypes=True)
            pool.iota(tcol[:, 1, :, :], [[P, NT], [0, G]], base=P, channel_multiplier=0,
                      allow_small_or_imprecise_dtypes=True)
            pool.iota(gnum[:, 0, :, :], [[0, NT], [1, G]], base=1, channel_multiplier=0,
                      allow_small_or_imprecise_dtypes=True)
            pool.iota(gnum[:, 1, :, :], [[0, NT], [-1, G]], base=G, channel_multiplier=0,
                      allow_small_or_imprecise_dtypes=True).then_inc(s_iota, 1)
            pool.wait_ge(s_prep, 5)
            pool.partition_all_reduce(gall[:, :, :].rearrange("p a g -> p (a g)"),
                                      gext[:, :, :].rearrange("p a g -> p (a g)"), 128,
                                      bass.bass_isa.ReduceOp.max).then_inc(s_all, 1)
            pool.iota(iota_s[:, :], [[1, 3 * SW]], base=0, channel_multiplier=0,
                      allow_small_or_imprecise_dtypes=True)
            pool.iota(iota_t[:, :, :], [[P, NT], [1, P + 1]], base=0, channel_multiplier=0,
                      allow_small_or_imprecise_dtypes=True).then_inc(s_big, 1)
            for c in POOL_LO:
                pool.sem_inc(s_lo[c], 1)
            pool.wait_ge(s_tab, 1)
            with pool.Fori(0, NT) as t:
                v0, v1 = visits(pool, t)
                with pool.Fori(v0, v1) as v:
                    for c in POOL_LO:
                        pool.wait_ge(s_hi[c], v + 1)
                        pool.wait_ge(s_use[c], v + 1)
                        pool.tensor_tensor(e_lo[:, c, :], raw[:, c, :], e_hi[:, c, :].bitcast(F32),
                                           ALU.subtract).then_inc(s_lo[c], 1)

        @block.scalar
        def _(act):
            def rows_of(t):
                act.dma_start(flat(x, t), x_in[ds(t * P, P), :]).then_inc(s_x, 16)

            rows_of(0)
            act.sem_inc(s_es, 1)
            act.sem_inc(s_ste, 16)
            act.sem_inc(s_ct, 1)
            act.wait_ge(s_tab, 1)
            with act.Fori(0, NT) as t:
                v0, v1 = visits(act, t)
                with act.Fori(v0, v1) as v:
                    for c in range(GC):
                        act.wait_ge(s_raw[c], v * 16 + 16)
                        act.wait_ge(s_use[c], v + 1)
                        act.copy(e_hi[:, c, :], raw[:, c, :]).then_inc(s_hi[c], 1)
                act.wait_ge(s_fin, t + 1)
                act.wait_ge(s_tr, t + 1)
                act.copy(ct[:P, :].rearrange("p (b f) -> p b f", b=3), banks[:P, 0:3, 0:SW]).then_inc(s_ct, 1)
                act.wait_ge(s_ste, t * 16 + 16)
                act.copy(es[:, :], banks[:P, 3, :]).then_inc(s_es, 1)
                act.wait_ge(s_ct, t + 2)
                act.copy(deg[:, ds(t, 1)], ct[:P, N:N + 1])
                act.wait_ge(s_xu, t + 1)
                rows_of(act.snap(nc.s_assert_within((t + 1) % NT, 0, NT - 1)))
                act.wait_ge(s_es, t + 2)
                act.dma_start(esum_d[ds(t, 1), :, :].rearrange("t p f -> (t p) f"),
                              es[:, :]).then_inc(s_ste, 16)
            stats.root(act)

        @block.vector
        def _(dve):
            dve.wait_ge(s_idx, 32)
            dve.tensor_copy(src_f[:, :], idx_i[:, 0, :]).then_inc(s_prep, 1)
            dve.tensor_copy(dst_f[:, :], idx_i[:, 1, :]).then_inc(s_prep, 1)
            def counts_out(t):
                dve.tensor_copy(counts[:, ds(t, 1), 0:8, :].rearrange("p t (b a) f -> p (t b) (a f)", b=2),
                                banks[:P, 4:6, 0:4 * P])
                dve.tensor_copy(counts[:, ds(t, 1), 8:NT, :].rearrange("p t a f -> p (t a f)"),
                                banks[:P, 6, 0:2 * P]).then_inc(s_tre, 1)

            dve.memset(banks[:, 4:7, :], 0.0)
            dve.memset(oh_s[:, :, N:], 1.0)
            dve.memset(zero_b[:, :], 0.0).then_inc(s_prep, 1)
            dve.wait_ge(s_prep, 3)
            dg = dst_f[:, :].rearrange("p (g c) -> p g c", c=GC)
            dve.tensor_reduce(gext[:, 0, :], dg, AX.X, ALU.max).then_inc(s_prep, 1)
            dve.tensor_reduce(gext[:, 1, :], dg, AX.X, ALU.min, negate=True).then_inc(s_prep, 1)
            dve.wait_ge(s_all, 1)
            dve.wait_ge(s_iota, 1)
            step = [5]

            def link(ins):
                step[0] += 1
                ins.then_inc(s_prep, 1)
                dve.wait_ge(s_prep, step[0])

            gmax = gall[0:1, 0:1, :].to_broadcast([1, NT, G])
            gmin = gall[0:1, 1:2, :].to_broadcast([1, NT, G])
            link(dve.tensor_tensor(tmask[:, 0], gmax, tcol[:, 0], ALU.is_ge))
            link(dve.scalar_tensor_tensor(tmask[:, 1], gmin, -1.0, tcol[:, 1], ALU.mult, ALU.is_lt))
            link(dve.tensor_tensor(tmask[:, 2], tmask[:, 0], tmask[:, 1], ALU.mult))
            link(dve.tensor_tensor(tmask[:, 0], tmask[:, 2], gnum[:, 0], ALU.mult))
            link(dve.tensor_tensor(tmask[:, 1], tmask[:, 2], gnum[:, 1], ALU.mult))
            hi, lo, cnt, one, v1, v0 = (tlim[:, i, :] for i in range(6))
            link(dve.tensor_reduce(hi, tmask[:, 0], AX.X, ALU.max))
            link(dve.tensor_reduce(lo, tmask[:, 1], AX.X, ALU.max))
            link(dve.tensor_scalar(lo, lo, -1.0, float(G), ALU.mult, ALU.add))
            link(dve.tensor_scalar(lo, lo, float(G - 1), None, ALU.min))
            link(dve.tensor_tensor(cnt, hi, lo, ALU.subtract))
            link(dve.tensor_scalar(cnt, cnt, 1.0, None, ALU.max))
            link(dve.memset(one, 1.0))
            link(dve.tensor_tensor_scan(v1, one, cnt, 0.0, ALU.mult, ALU.add))
            link(dve.tensor_tensor(v0, v1, cnt, ALU.subtract))
            link(dve.tensor_tensor(lo, lo, v0, ALU.subtract))
            link(dve.tensor_copy(tab[:, 0, :], v0))
            link(dve.tensor_copy(tab[:, 1, :], v1))
            link(dve.tensor_scalar(tab[:, 2, :], lo, float(NT * G), None, ALU.add))
            for c in range(GC):
                if c not in POOL_LO:
                    dve.sem_inc(s_lo[c], 1)
            dve.sem_inc(s_tab, 1)
            dve.wait_ge(s_big, 1)
            with dve.Fori(0, NT) as t:
                v0, v1 = visits(dve, t)
                shift = dve.value_load(tab[0:1, 2, ds(t, 1)], min_val=0, max_val=2 * NT * G)
                with dve.Fori(v0, v1) as v:
                    g = dve.snap(nc.s_assert_within(v + shift - NT * G, 0, G - 1))
                    for c in range(GC):
                        chunk = ds(g * GC + c, 1)
                        dve.wait_ge(s_use[c], v + 1)
                        dve.tensor_scalar(oh_s[:, c, 0:N], iota_s[:, 0:N], src_f[:, chunk], None, ALU.is_equal)
                        tile_nodes = iota_t[:, ds(t, 1), :].rearrange("p a f -> p (a f)")
                        dve.tensor_scalar(oh_d[:, c, :], tile_nodes, dst_f[:, chunk], None,
                                          ALU.is_equal).then_inc(s_oh[c], 1)
                        if c not in POOL_LO:
                            dve.wait_ge(s_hi[c], v + 1)
                            dve.tensor_tensor(e_lo[:, c, :], raw[:, c, :], e_hi[:, c, :].bitcast(F32),
                                              ALU.subtract).then_inc(s_lo[c], 1)
                stats.tile(dve, t, s_x)
                dve.wait_ge(stats.s_bn, t + 1)
                dve.sem_inc(s_xu, 1)
                dve.wait_ge(s_tr, t + 1)
                counts_out(dve.snap(nc.s_assert_within((t + NT - 1) % NT, 0, NT - 1)))
            dve.wait_ge(s_tr, NT + 1)
            dve.wait_ge(s_tre, NT)
            counts_out(NT - 1)
            stats.finish(dve)

        @block.tensor
        def _(pe):
            for c in range(GC):
                pe.sem_inc(s_use[c], 1)
            pe.sem_inc(s_tr, 1)
            pe.wait_ge(s_tab, 1)
            with pe.Fori(0, NT) as t:
                v0, v1 = visits(pe, t)
                pe.wait_ge(s_ct, t + 1)
                pe.wait_ge(s_es, t + 1)
                for b in range(3):
                    pe.matmul(banks[:P, b, 0:SW], zero_b[:, 0:P], zero_b[:, 0:SW], start=True, stop=False)
                pe.matmul(banks[:P, 3, :], zero_b[:, 0:P], zero_b[:, :], start=True, stop=False)
                with pe.Fori(v0, v1) as v:
                    for c in range(GC):
                        pe.wait_ge(s_oh[c], v + 1)
                        for b in range(3):
                            pe.matmul(banks[:P, b, 0:SW], oh_db[:, c, 0:P], oh_s[:, c, b * SW:(b + 1) * SW],
                                      start=False, stop=False)
                        pe.wait_ge(s_hi[c], v + 1)
                        pe.matmul(banks[:P, 3, :], oh_d[:, c, 0:P], e_hi[:, c, :], start=False, stop=False)
                        pe.wait_ge(s_lo[c], v + 2)
                        pe.matmul(banks[:P, 3, :], oh_d[:, c, 0:P], e_lo[:, c, :], start=False,
                                  stop=False).then_inc(s_use[c], 1)
                for b in range(3):
                    pe.matmul(banks[:P, b, 0:SW], zero_b[:, 0:P], zero_b[:, 0:SW], start=False, stop=True)
                pe.matmul(banks[:P, 3, :], zero_b[:, 0:P], zero_b[:, :], start=False, stop=True).then_inc(s_fin, 1)
                pe.wait_ge(s_ct, t + 2)
                pe.wait_ge(s_tre, t + 1)
                for a in range(NT):
                    last = pe.transpose(banks[:P, 4 + a // 4, a % 4 * P:(a % 4 + 1) * P], ct[:P, a * P:(a + 1) * P],
                                        ident[:P, :P])
                last.then_inc(s_tr, 1)


class Weights:

    def __init__(self, k, sb, name, pieces, stages=2):
        self.pieces, self.stages = [], stages
        for dram, hi, lo in pieces:
            rows = min(max(1, STAGE // hi.shape[-1]), hi.shape[1])
            self.pieces += [((dram, r, rows), hi[:, r:r + rows], lo[:, r:r + rows])
                            for r in range(0, hi.shape[1], rows)] if len(hi.shape) == 3 else [((dram, 0, 0), hi, lo)]
        self.stage = sb(f"{name}_stage", [128, stages, STAGE], F32)
        self.s_in = [k.sem(f"s_{name}_w_in{b}") for b in range(stages)]
        self.s_hi = k.sem(f"s_{name}_w_hi")
        self.s_lo = k.sem(f"s_{name}_w_lo")

    def view(self, n):
        hi = self.pieces[n][1]
        rows, size = hi.shape[0], hi.free_size()
        flat = self.stage[:rows, n % self.stages, 0:size]
        return flat if len(hi.shape) == 2 else flat.rearrange("p (a b) -> p a b", b=hi.shape[-1])

    def load(self, sp, *chosen, first=0, last=None):
        for n, ((dram, r, rows), _, _) in list(enumerate(self.pieces))[first:last]:
            if n >= self.stages:
                sp.wait_ge(self.s_lo, n - self.stages + 1)
            if callable(dram):
                dram = dram(*chosen)
            if rows:
                dram = dram[:, r:r + rows]
            sp.dma_start(self.view(n), dram).then_inc(self.s_in[n % self.stages], 16)

    def high(self, act):
        for n, (_, hi, _) in enumerate(self.pieces):
            act.wait_ge(self.s_in[n % self.stages], 16 * (n // self.stages + 1))
            act.copy(hi, self.view(n)).then_inc(self.s_hi, 1)

    def low(self, dve):
        for n, (_, hi, lo) in enumerate(self.pieces):
            dve.wait_ge(self.s_hi, n + 1)
            dve.tensor_tensor(lo, self.view(n), hi.bitcast(F32), ALU.subtract).then_inc(self.s_lo, 1)

    def split(self, pool):
        for n, (_, hi, lo) in enumerate(self.pieces):
            pool.wait_ge(self.s_in[n % self.stages], 16 * (n // self.stages + 1))
            pool.tensor_copy(hi, self.view(n)).then_inc(self.s_hi, 1)
            pool.wait_ge(self.s_hi, n + 1)
            pool.tensor_tensor(lo, self.view(n), hi.bitcast(F32), ALU.subtract).then_inc(self.s_lo, 1)

    def wait(self, pe, pieces=None):
        pe.wait_ge(self.s_lo, pieces or len(self.pieces))


def product(pe, out, lhs, rhs, at, terms, first=True, last=True):
    n = 0
    for term in terms:
        for a, b in ((0, 0), (0, 1), (1, 0)):
            l, r = at(lhs[a], rhs[b], term)
            n += 1
            ins = pe.matmul(out, l, r, start=first and n == 1, stop=last and n == 3 * len(terms))
    return ins


class Normed:

    def __init__(self, k, sb, name, x, mean, rstd, ident, bank, affine=None):
        self.k, self.x, self.mean, self.rstd, self.ident, self.bank = k, x, mean, rstd, ident, bank
        self.affine = affine
        self.xn = sb(f"{name}_xn", [P, 2, D], F32)
        self.hi = sb(f"{name}_hi", [128, KT, 2, P], F32R)
        self.lo = sb(f"{name}_lo", [128, KT, 2, P], F32R)
        self.s_xn = k.sem(f"s_{name}_xn")
        self.s_aff = k.sem(f"s_{name}_aff")
        self.s_xt = k.sem(f"s_{name}_xt")
        self.s_hi = k.sem(f"s_{name}_hi")
        self.s_lo = k.sem(f"s_{name}_lo")

    def parts(self):
        return self.hi, self.lo

    def rows(self, dve, i):
        pair = i % NP if isinstance(i, int) else dve.snap(self.k.nc.s_assert_within(i % NP, 0, NP - 1))
        for h in range(2):
            t = ds(2 * pair + h, 1)
            out = self.xn[:, h, :]
            ins = dve.tensor_scalar(out, self.x[:, t, :].rearrange("p a f -> p (a f)"), self.mean[:, t], self.rstd[:, t],
                                    ALU.subtract, ALU.mult)
            if self.affine:
                gamma, beta = self.affine
                ins.then_inc(self.s_aff, 1)
                dve.wait_ge(self.s_aff, 4 * i + 2 * h + 1)
                dve.tensor_tensor(out, out, gamma, ALU.mult).then_inc(self.s_aff, 1)
                dve.wait_ge(self.s_aff, 4 * i + 2 * h + 2)
                ins = dve.tensor_tensor(out, out, beta, ALU.add)
            ins.then_inc(self.s_xn, 1)

    def transposes(self, pe, i):
        for h in range(2):
            pe.wait_ge(self.s_xn, 2 * i + h + 1)
            for c in range(KT):
                ins = pe.transpose(self.k.banks[:, self.bank + h, c * P:(c + 1) * P],
                                   self.xn[:, h, c * 128:(c + 1) * 128], self.ident[:P, :P])
            ins.then_inc(self.s_xt, 1)

    def psum(self, h):
        return self.k.banks[:, self.bank + h, 0:KT * P].rearrange("p (c n) -> p c n", n=P)

    def high(self, act, i, used=None, value=0, step=0, halves=(0, 1)):
        for h in halves:
            act.wait_ge(self.s_xt, 2 * i + h + 1)
            if used is not None:
                act.wait_ge(used, value + step * h)
            act.copy(self.hi[:, :, h, :], self.psum(h)).then_inc(self.s_hi, 1)

    def low(self, dve, i):
        for h in range(2):
            dve.wait_ge(self.s_xt, 2 * i + h + 1)
            dve.wait_ge(self.s_hi, 2 * i + h + 1)
            dve.tensor_tensor(self.lo[:, :, h, :], self.psum(h), self.hi[:, :, h, :].bitcast(F32),
                              ALU.subtract).then_inc(self.s_lo, 1)

    def wait(self, pe, i):
        pe.wait_ge(self.s_lo, 2 * i + 2)


def half_of(h):
    return lambda xt, w, c: (xt[:, c, h, :], w[:, c, :])


def feature_tile(f):
    return lambda w, xt, c: (w[:, c, f * 128:(f + 1) * 128], xt[:, c, :, :].rearrange("p h n -> p (h n)"))


def chain(eng, sem):
    n = [0]

    def link(ins):
        n[0] += 1
        ins.then_inc(sem, 1)
        eng.wait_ge(sem, n[0])

    return link


class Stats:

    def __init__(self, k, sb, name, x, mean, rstd, again=None):
        self.x, self.mean, self.rstd, self.again = x, mean, rstd, again
        self.stats = sb(f"{name}_stats", [P, NT, k.nc.vector.BN_STATS_DIM], F32)
        self.mv = sb(f"{name}_mv", [P, NT, 2], F32)
        self.var = sb(f"{name}_var", [P, 2, NT], F32)
        self.s_bn = k.sem(f"s_{name}_bn")
        self.s_ag = k.sem(f"s_{name}_ag")
        self.s_st = k.sem(f"s_{name}_st")
        self.s_sq = k.sem(f"s_{name}_sq")

    def tile(self, dve, t, landed=None):
        if landed is not None:
            dve.wait_ge(landed, t * 16 + 16)
        dve.bn_stats(flat(self.stats, t), flat(self.x, t)).then_inc(self.s_bn, 1)

    def tiles(self, dve):
        with dve.Fori(0, NT) as t:
            self.tile(dve, t)

    def finish(self, dve):
        mean, rstd, again, mv, var = self.mean, self.rstd, self.again, self.mv, self.var
        dve.wait_ge(self.s_bn, NT)
        for t in range(NT):
            dve.bn_aggr(mv[:, t, :], self.stats[:, t, :]).then_inc(self.s_ag, 1)
        dve.wait_ge(self.s_ag, NT)
        link = chain(dve, self.s_st)
        link(dve.tensor_copy(mean[:, :], mv[:, :, 0]))
        link(dve.tensor_scalar(var[:, 0, :], mv[:, :, 1], EPS, None, ALU.add))
        dve.wait_ge(self.s_sq, 1)
        link(dve.reciprocal(rstd[:, :], var[:, 1, :]))
        if again is not None:
            link(dve.tensor_tensor(var[:, 0, :], rstd[:, :], rstd[:, :], ALU.mult))
            link(dve.tensor_tensor(var[:, 0, :], var[:, 0, :], mv[:, :, 1], ALU.mult))
            link(dve.tensor_scalar(var[:, 0, :], var[:, 0, :], EPS, None, ALU.add))
            dve.wait_ge(self.s_sq, 2)
            link(dve.reciprocal(again[:, :], var[:, 1, :]))
            link(dve.tensor_tensor(again[:, :], again[:, :], rstd[:, :], ALU.mult))

    def root(self, act):
        act.wait_ge(self.s_st, 2)
        act.activation(self.var[:, 1, :], self.var[:, 0, :], ACT.Sqrt).then_inc(self.s_sq, 1)
        if self.again is not None:
            act.wait_ge(self.s_st, 6)
            act.activation(self.var[:, 1, :], self.var[:, 0, :], ACT.Sqrt).then_inc(self.s_sq, 1)


def attention_phase(k, x, y, mean, rstd, counts, counts_d, ident, Wq, Wk, Wv):
    nc = k.nc
    banks = k.banks
    with ExitStack() as ctx:
        def sb(name, shape, dt):
            return ctx.enter_context(nc.sbuf_tensor(name, shape, dt))

        kst = sb("kst", [128, H, N], F32R)
        vs = sb("vs", [P, NT, H, DH + 1], F32)
        wq = [sb(f"wq_s{a}", [128, KT, D], F32R) for a in range(2)]

        with ExitStack() as inner:
            def sbi(name, shape, dt):
                return inner.enter_context(nc.sbuf_tensor(name, shape, dt))

            wk = [sbi(f"wk_s{a}", [128, KT, D], F32R) for a in range(2)]
            wv = [sbi(f"wv_s{a}", [128, KT, D], F32R) for a in range(2)]
            w = Weights(k, sbi, "akv", [(src.rearrange("(c p) f -> p c f", p=128), t[0][:], t[1][:])
                                        for src, t in ((Wk, wk), (Wv, wv))], stages=3)
            late = Weights(k, sbi, "aq", [(Wq.rearrange("(c p) f -> p c f", p=128), wq[0][:], wq[1][:])])
            xt = Normed(k, sbi, "akv", x, mean, rstd, ident, 0)
            s_stc = k.sem("s_akv_stc")
            s_one = k.sem("s_akv_one")
            s_kp = k.sem("s_akv_kp")
            s_kh = k.sem("s_akv_kh")
            s_kl = k.sem("s_akv_kl")
            s_vp = k.sem("s_akv_vp")
            s_vc = k.sem("s_akv_vc")
            block = inner.enter_context(nc.Block())
            rows = ((0, 64), (64, 128))

            def kcols(i):
                return ds(i * 2 * P, 2 * P)

            @block.sync
            def _(sp):
                w.load(sp)
                late.load(sp)
                sp.dma_start(counts_d.rearrange("t p a d -> p t a d"), counts[:, :, :, :]).then_inc(s_stc, 16)
                sp.wait_ge(s_stc, 16)

            @block.gpsimd
            def _(pool):
                pool.memset(vs[:, :, :, DH:DH + 1], 1.0).then_inc(s_one, 1)
                late.split(pool)

            @block.tensor
            def _(pe):
                xt.transposes(pe, 0)
                w.wait(pe, len(w.pieces) // 2)
                with pe.Fori(0, NP) as i:
                    xt.wait(pe, i)
                    xt.transposes(pe, i + 1)
                    for a in range(4):
                        pe.wait_ge(s_kl, 4 * i + a + 1)
                        product(pe, banks[:, 2 + a % 2, 0:2 * P], wk, xt.parts(), feature_tile(a),
                                range(KT)).then_inc(s_kp, 1)
                    w.wait(pe)
                    for h in range(2):
                        pe.wait_ge(s_vc, 2 * i + h + 1)
                        ins = product(pe, banks[:P, 4 + h, :], xt.parts(), wv, half_of(h), range(KT))
                        ins.then_inc(s_vp, 1)

            @block.scalar
            def _(act):
                act.sem_inc(s_vc, 2)
                xt.high(act, 0)
                w.high(act)
                act.wait_ge(s_one, 1)
                with act.Fori(0, NP) as i:
                    for a in range(4):
                        act.wait_ge(s_kp, 4 * i + a + 1)
                        for e, (r0, r1) in enumerate(rows):
                            ins = act.copy(kst[r0:r1, 2 * a + e, kcols(i)], banks[r0:r1, 2 + a % 2, 0:2 * P])
                        ins.then_inc(s_kh, 1)
                    for h in range(2):
                        act.wait_ge(s_vp, 2 * i + h + 1)
                        act.copy(vs[:, ds(2 * i + h, 1), :, 0:DH].rearrange("p a h d -> p (a h) d"),
                                 banks[:P, 4 + h, :].rearrange("p (h d) -> p h d", d=DH)).then_inc(s_vc, 1)
                        xt.high(act, i + 1, s_vp, 2 * i + 1, 1, (h,))

            @block.vector
            def _(dve):
                dve.sem_inc(s_kl, 2)
                xt.rows(dve, 0)
                xt.low(dve, 0)
                w.low(dve)
                with dve.Fori(0, NP) as i:
                    xt.rows(dve, i + 1)
                    for a in range(4):
                        dve.wait_ge(s_kh, 4 * i + a + 1)
                        for e, (r0, r1) in enumerate(rows):
                            q0, q1 = rows[1 - e]
                            ins = dve.tensor_tensor(kst[q0:q1, 2 * a + e, kcols(i)], banks[r0:r1, 2 + a % 2, 0:2 * P],
                                                    kst[r0:r1, 2 * a + e, kcols(i)].bitcast(F32), ALU.subtract)
                        ins.then_inc(s_kl, 1)
                    xt.low(dve, i + 1)

        UNITS = NT // 2
        SR, ER, PR, AHEAD = 4, 4, 4, 4
        NU = H * UNITS
        QU = 2 * UNITS
        HG = H // 2
        qh = sb("qh", [128, H, 2 * P], F32R)
        ql = sb("ql", [128, H, 2 * P], F32R)
        er = sb("er", [P, ER, 2, 2 * P], F32)
        pr = sb("pr", [P, PR, 2, 2 * P], F32)
        so = sb("so", [DH + 1, 2, 2 * P], F32)
        zr = sb("zr", [P, 2, 2, HG], F32)
        on = sb("on", [P, 2, D // 2], F32)
        xt = Normed(k, sb, "att", x, mean, rstd, ident, 0)
        s_qp = k.sem("s_qp")
        s_qh = k.sem("s_qh")
        s_ql = k.sem("s_ql")
        s_s = k.sem("s_s")
        s_e = k.sem("s_e")
        s_c = k.sem("s_c")
        s_p = k.sem("s_p")
        s_av = k.sem("s_av")
        s_so = k.sem("s_so")
        s_ot = k.sem("s_ot")
        s_on = k.sem("s_on")
        s_n = k.sem("s_n")
        s_y = k.sem("s_y")
        block = ctx.enter_context(nc.Block())
        rows = ((0, 64), (64, 128))
        LO, HI = float(np.exp(np.float32(-5.0))), float(np.exp(np.float32(5.0)))

        @block.tensor
        def _(pe):
            def q_product(i, a):
                pe.wait_ge(s_ql, 4 * i + a + 1)
                product(pe, banks[:, 2, 0:2 * P], wq, xt.parts(), feature_tile(a), range(KT)).then_inc(s_qp, 1)

            def scores(i, n):
                h, u = divmod(n, UNITS)
                if n % QU == 0:
                    pe.wait_ge(s_ql, 4 * i + n // QU + 2)
                pe.wait_ge(s_e, NU * i + n + 1)
                for j in range(2):
                    cols = slice((2 * u + j) * P, (2 * u + j + 1) * P)
                    out = banks[:P, 4 + n % SR, j * 2 * P:(j + 1) * 2 * P]
                    pe.matmul(out, kst[:, h, cols], qh[:, h, :], start=True, stop=False)
                    ins = pe.matmul(out, kst[:, h, cols], ql[:, h, :], start=False, stop=True)
                ins.then_inc(s_s, 1)

            def back(i, h):
                if h == 0:
                    xt.wait(pe, i + 1)
                if h == HG:
                    pe.wait_ge(s_on, 2 * i + 2)
                pe.wait_ge(s_so, H * i + h + 3)
                for g in range(2):
                    ins = pe.transpose(banks[:P, g, h % HG * (DH + 1):(h % HG + 1) * (DH + 1)],
                                       so[:, h % 2, g * P:(g + 1) * P], ident[:DH + 1, :DH + 1])
                ins.then_inc(s_ot, 1)

            pe.sem_inc(s_av, PR)
            xt.transposes(pe, 0)
            xt.wait(pe, 0)
            for a in range(4):
                q_product(0, a)
            for n in range(AHEAD):
                scores(0, n)
            with pe.Fori(0, NP) as i:
                for n in range(NU):
                    h, u = divmod(n, UNITS)
                    if n + AHEAD < NU:
                        scores(i, n + AHEAD)
                    else:
                        scores(i + 1, n + AHEAD - NU)
                    if n == 3:
                        pe.wait_ge(s_on, 2 * i + 1)
                        xt.transposes(pe, i + 1)
                    pe.wait_ge(s_p, NU * i + n + 1 + ER)
                    if u == 0:
                        pe.wait_ge(s_so, H * i + h + 1)
                        if h % 2 == 0:
                            pe.wait_ge(s_ql, 4 * i + h // 2 + 5)
                    for j in range(2):
                        ins = pe.matmul(banks[:DH + 1, 2 + h % 2, 0:2 * P], vs[:, 2 * u + j, h, :], pr[:, n % PR, j, :],
                                        start=u == 0 and j == 0, stop=u == UNITS - 1 and j == 1)
                    ins.then_inc(s_av, 1)
                    if n % QU == 7:
                        if n < QU:
                            xt.wait(pe, i + 1)
                        pe.wait_ge(s_so, H * i + h + 2)
                        q_product(i + 1, n // QU)
                    if h and u == 2:
                        back(i, h - 1)
                back(i, H - 1)

        @block.scalar
        def _(act):
            def q_high(i, a):
                act.wait_ge(s_qp, 4 * i + a + 1)
                for e, (r0, r1) in enumerate(rows):
                    for q0, q1 in rows:
                        ins = act.copy(qh[q0:q1, 2 * a + e, :], banks[r0:r1, 2, 0:2 * P])
                ins.then_inc(s_qh, 1)

            def out(i, h):
                act.wait_ge(s_av, NU * i + UNITS * (h + 1) + PR)
                if h >= 2:
                    act.wait_ge(s_ot, H * i + h - 1)
                act.copy(so[:, h % 2, :], banks[:DH + 1, 2 + h % 2, 0:2 * P]).then_inc(s_so, 1)

            act.sem_inc(s_e, SR)
            act.sem_inc(s_so, 2)
            xt.high(act, 0)
            for a in range(4):
                q_high(0, a)
            with act.Fori(0, NP) as i:
                for n in range(NU):
                    h, u = divmod(n, UNITS)
                    act.wait_ge(s_s, NU * i + n + 1)
                    act.wait_ge(s_p, NU * i + n + 1)
                    act.activation(er[:, n % ER, :, :].rearrange("p j n -> p (j n)"),
                                   banks[:P, 4 + n % SR, 0:4 * P], ACT.Exp, scale=1.0 / 8.0).then_inc(s_e, 1)
                    if n == 5:
                        xt.high(act, i + 1, s_qp, 4 * i + 4)
                    if n % QU == 9:
                        q_high(i + 1, n // QU)
                    if h and u == 1:
                        out(i, h - 1)
                out(i, H - 1)

        @block.vector
        def _(dve):
            def q_low(i, a):
                dve.wait_ge(s_qh, 4 * i + a + 1)
                for e, (r0, r1) in enumerate(rows):
                    for q0, q1 in rows:
                        ins = dve.tensor_tensor(ql[q0:q1, 2 * a + e, :], banks[r0:r1, 2, 0:2 * P],
                                                qh[r0:r1, 2 * a + e, :].bitcast(F32), ALU.subtract)
                ins.then_inc(s_ql, 1)

            def clip(i, n):
                dve.wait_ge(s_e, NU * i + n + 1 + SR)
                dve.tensor_scalar(er[:, n % ER, :, :], er[:, n % ER, :, :], HI, LO, ALU.min, ALU.max).then_inc(s_c, 1)

            def divide(i, q):
                dve.wait_ge(s_ot, H * i + HG * (q + 1))
                out = banks[:P, 0:2, 0:HG * (DH + 1)].rearrange("p g (h d) -> p g h d", d=DH + 1)
                first = 6 * (2 * i + q)
                dve.tensor_scalar(zr[:, 0], out[:, :, :, DH:DH + 1].rearrange("p g h d -> p g (h d)"), 1e-6, None,
                                  ALU.add).then_inc(s_n, 1)
                dve.wait_ge(s_n, first + 1)
                dve.reciprocal(zr[:, 1], zr[:, 0]).then_inc(s_n, 1)
                dve.wait_ge(s_n, first + 2)
                for g in range(2):
                    ins = dve.tensor_tensor(on[:, g, :].rearrange("p (h d) -> p h d", d=DH), out[:, g, :, 0:DH],
                                            zr[:, 1, g, :].unsqueeze(2).to_broadcast([P, HG, DH]), ALU.mult)
                    ins.then_inc(s_n, 1)
                dve.wait_ge(s_n, first + 4)
                dve.sem_inc(s_on, 1)
                dve.wait_ge(s_y, 2 * i + 2)
                for g in range(2):
                    ys = y[:, ds(2 * i + g, 1), q * (D // 2):(q + 1) * (D // 2)].rearrange("p a f -> p (a f)")
                    dve.tensor_tensor(ys, ys, on[:, g, :], ALU.add).then_inc(s_n, 1)

            dve.sem_inc(s_ql, 1)
            dve.sem_inc(s_on, 1)
            dve.sem_inc(s_p, ER)
            xt.rows(dve, 0)
            xt.low(dve, 0)
            for a in range(4):
                q_low(0, a)
            with dve.Fori(0, NP) as i:
                clip(i, 0)
                for n in range(NU):
                    h, u = divmod(n, UNITS)
                    if n + 1 < NU:
                        clip(i, n + 1)
                    dve.wait_ge(s_c, NU * i + n + 1)
                    dve.wait_ge(s_av, NU * i + n + 1)
                    cnt = counts[:, ds(2 * i, 2), 2 * u:2 * u + 2, :].rearrange("p g j d -> p j g d")
                    dve.tensor_tensor(pr[:, n % PR, :, :].rearrange("p j (g d) -> p j g d", g=2),
                                      er[:, n % ER, :, :].rearrange("p j (g d) -> p j g d", g=2), cnt,
                                      ALU.mult).then_inc(s_p, 1)
                    if n == 0:
                        xt.rows(dve, i + 1)
                    if n in (1, 2):
                        t = ds(2 * i + n - 1, 1)
                        dve.tensor_scalar(y[:, t, :].rearrange("p a f -> p (a f)"),
                                          x[:, t, :].rearrange("p a f -> p (a f)"), mean[:, t], rstd[:, t],
                                          ALU.subtract, ALU.mult).then_inc(s_y, 1)
                    if n == 5:
                        xt.low(dve, i + 1)
                    if n % QU == 9:
                        q_low(i + 1, n // QU)
                    if n == UNITS * HG + 2:
                        divide(i, 0)
                divide(i, 1)
                dve.wait_ge(s_n, 6 * (2 * i + 2))


def mix_phase(k, name, x, y, mean, rstd, ident, mask_in, head_cols, head_rows, wqkv, qkv_b, q_cols, wout, out_b,
              affine=None, base=None, norm=None):
    nc, banks = k.nc, k.banks
    with ExitStack() as ctx:
        def sb(nm, shape, dt):
            return ctx.enter_context(nc.sbuf_tensor(f"{name}_{nm}", shape, dt))

        def sem(nm):
            return k.sem(f"s_{name}_{nm}")

        kvw = [sb(f"kvw{a}", [128, KT, D], F32R) for a in range(2)]
        ks8 = [sb(f"ks8{a}", [128, KT, H], F32R) for a in range(2)]
        sel = sb("sel", [H, KT, 128], F32R)
        wq = [sb(f"wq{a}", [128, KT, D], F32R) for a in range(2)]
        bq = sb("bq", [128, KT], F32)
        rows = sb("rows", [P, 5, D], F32)
        s_row = sem("row")
        gb = (rows[:, 3, :], rows[:, 4, :]) if affine else None
        bias = qkv_b is not None

        var = sb("var", [P, D], F32) if norm else None

        with ExitStack() as inner:
            def sbi(nm, shape, dt):
                return inner.enter_context(nc.sbuf_tensor(nm, shape, dt))

            wk = [sbi(f"{name}_wk{a}", [128, KT, D], F32R) for a in range(2)]
            wv = [sbi(f"{name}_wv{a}", [128, KT, D], F32R) for a in range(2)]
            wo = sbi(f"{name}_wo", [128, KT, D], F32)
            wsrc = wqkv.rearrange("(c p) f -> p c f", p=128)
            w = Weights(k, sbi, f"{name}k", [
                (wsrc[:, :, D:2 * D], wk[0][:], wk[1][:]), (wsrc[:, :, 2 * D:3 * D], wv[0][:], wv[1][:])], stages=3)
            late = Weights(k, sbi, f"{name}l", [
                (wsrc[:, :, 0:D], wq[0][:], wq[1][:])], stages=1)
            xt = Normed(k, sbi, f"{name}k", x, mean, rstd, ident, 0, gb)
            kx = sbi(f"{name}_kx", [P, 2, 2, D], F32)
            stats = Stats(k, sbi, f"{name}s", x, base[0], base[1], again=rstd) if base else None
            kf = sbi(f"{name}_kf", [P, 2, D], F32)
            kh, kl, vh, vl = (sbi(f"{name}_{nm}", [P, 2, D], F32R) for nm in ("kh", "kl", "vh", "vl"))
            vf = sbi(f"{name}_vf", [P, 2, D], F32) if bias else None
            kb = sbi(f"{name}_kb", [P, 2, D], F32) if bias else None
            ones = sbi(f"{name}_ones", [P, 2], F32)
            kvm = sbi(f"{name}_kvm", [128, KT, 128], F32)
            ksm = sbi(f"{name}_ksm", [128, KT], F32)
            mask = sbi(f"{name}_mask", [128, 128], F32)
            ones_n = sbi(f"{name}_ones_n", [128, 128], F32) if norm else None
            ks8f = sbi(f"{name}_ks8f", [128, KT, H], F32)
            hcol = sbi(f"{name}_hcol", [128, KT, H], F32)
            hrow = sbi(f"{name}_hrow", [H, KT, 128], F32)
            s_kp, s_vp = sem("kp"), sem("vp")
            s_kb, s_vb = sem("kb"), sem("vb")
            s_ke, s_kf = sem("ke"), sem("kf")
            s_kh, s_kl, s_vh, s_vl = sem("kh"), sem("kl"), sem("vh"), sem("vl")
            s_kv = sem("kv")
            s_one, s_f, s_w, s_wh = sem("one"), sem("f"), sem("w"), sem("wh")
            s_wo = sem("wo")
            if norm:
                centre = sbi(f"{name}_centre", [P, D], F32)
                sq = sbi(f"{name}_sq", [P, 2, D], F32)
                sums_sq = sbi(f"{name}_sums_sq", [P, D], F32)
                s_ba = sem("ba")
                s_bm, s_bc = sem("bm"), sem("bc")
                s_bd, s_bs = sem("bd"), sem("bs")
                s_bv = sem("bv")
            block = inner.enter_context(nc.Block())

            @block.sync
            def _(sp):
                w.load(sp, last=2)
                sp.dma_start(rows[:, 2, :], out_b.partition_broadcast(P)).then_inc(s_row, 16)
                sp.dma_start(hcol[:, :, :], head_cols).then_inc(s_row, 16)
                sp.dma_start(mask[:, :], mask_in).then_inc(s_row, 16)
                if norm:
                    sp.dma_start(ones_n[:, :], norm[0]).then_inc(s_row, 16)
                sp.dma_start(hrow[:, :, :], head_rows).then_inc(s_row, 16)
                if norm:
                    sp.dma_start(rows[:, 0, :], norm[1].partition_broadcast(P)).then_inc(s_row, 16)
                    sp.dma_start(rows[:, 1, :], norm[2].partition_broadcast(P)).then_inc(s_row, 16)
                if affine:
                    sp.dma_start(rows[:, 3, :], affine[0].partition_broadcast(P)).then_inc(s_row, 16)
                    sp.dma_start(rows[:, 4, :], affine[1].partition_broadcast(P)).then_inc(s_row, 16)
                if bias:
                    sp.dma_start(rows[:, 0, :], qkv_b[D:2 * D].partition_broadcast(P)).then_inc(s_row, 16)
                    sp.dma_start(rows[:, 1, :], qkv_b[2 * D:3 * D].partition_broadcast(P)).then_inc(s_row, 16)
                    sp.dma_start(bq[:, :], q_cols).then_inc(s_row, 16)
                w.load(sp, first=2)
                late.load(sp)
                sp.dma_start(wo[:, :, :], wout.rearrange("(c p) f -> p c f", p=128)).then_inc(s_wo, 16)

            nrow = 64 + (48 if norm else 0) + (32 if affine else 0) + (48 if bias else 0)

            @block.gpsimd
            def _(pool):
                pool.memset(ones[:, :], 1.0).then_inc(s_one, 1)
                late.split(pool)
                if norm:
                    pool.sem_inc(s_ba, 1)
                    pool.memset(sums_sq[:, :], 0.0).then_inc(s_ba, 1)
                    with pool.Fori(0, NP) as i:
                        for h in range(2):
                            pool.wait_ge(s_ba, 2 * i + h + 2)
                            pool.wait_ge(s_bs, 2 * i + h + 1)
                            pool.tensor_tensor(sums_sq[:, :], sums_sq[:, :], sq[:, h, :], ALU.add).then_inc(s_ba, 1)

            @block.tensor
            def _(pe):
                pe.sem_inc(s_kv, 2)
                xt.transposes(pe, 0)
                if norm:
                    pe.wait_ge(s_row, nrow)
                    for t in range(NT):
                        ins = pe.matmul(banks[:P, 2, :], ones_n[:P, :P], y[:, t, :], start=t == 0, stop=t == NT - 1)
                    ins.then_inc(s_bm, 1)
                    pe.wait_ge(s_bc, 1)
                w.wait(pe, len(w.pieces) // 2)
                pe.wait_ge(s_one, 2)

                def keys_values(i):
                    xt.wait(pe, i)
                    for h in range(2):
                        if not isinstance(i, int):
                            pe.wait_ge(s_ke, 2 * i + h + 1)
                        product(pe, banks[:P, 2 + h, :], xt.parts(), wk, half_of(h), range(KT)).then_inc(s_kp, 1)
                    w.wait(pe)
                    for h in range(2):
                        if not isinstance(i, int):
                            pe.wait_ge(s_vl, 2 * i + h + 1)
                        ins = product(pe, banks[:P, 4 + h, :], xt.parts(), wv, half_of(h), range(KT))
                        ins.then_inc(s_vp, 1)
                    xt.transposes(pe, i + 1)

                def sums(i):
                    for h in range(2):
                        pe.wait_ge(s_kl, 2 * i + h + 1)
                        pe.wait_ge(s_vl, 2 * i + h + 3)
                        for j in range(KT):
                            c = slice(128 * j, 128 * (j + 1))
                            for a, b in ((vh, kh), (vh, kl), (vl, kh)):
                                pe.matmul(banks[:, 6, c], a[:, h, c], b[:, h, c], start=False, stop=False,
                                          skip_group_check=True)
                            ins = pe.matmul(banks[:, 7, 2 * j:2 * j + 2], kf[:, h, c], ones[:, :], start=False,
                                            stop=False, skip_group_check=True)
                        ins.then_inc(s_kv, 1)

                keys_values(0)
                with pe.Fori(0, NP - 1) as i:
                    keys_values(i + 1)
                    sums(i)
                sums(NP - 1)
                if norm:
                    xt.wait(pe, NP)
                    pe.wait_ge(s_ba, NT + 2)
                    pe.matmul(banks[:P, 1, :], ones_n[:P, :P], sums_sq[:, :], start=True, stop=True).then_inc(s_bv, 1)
                for j in range(KT):
                    if j == 0:
                        pe.wait_ge(s_f, 2)
                        pe.wait_ge(s_wo, 16)
                        late.wait(pe)
                    pe.matmul(banks[:, 2 + j, :], kvm[:, j, :], wo[:, j, :], start=True, stop=True).then_inc(s_w, 1)

            @block.scalar
            def _(act):
                if stats:
                    stats.root(act)
                xt.high(act, 0)
                w.high(act)
                with act.Fori(0, NP) as i:
                    for h in range(2):
                        if bias:
                            act.wait_ge(s_kb, 2 * i + h + 1)
                            src = kb[:, h, :]
                        else:
                            act.wait_ge(s_kp, 2 * i + h + 1)
                            src = banks[:P, 2 + h, :]
                        act.activation(kx[:, h, 0, :], src, ACT.Exp)
                        act.activation(kx[:, h, 1, :], src, ACT.Relu).then_inc(s_ke, 1)
                    xt.high(act, i + 1, s_vp, 2 * i + 1, 1)
                    for h in range(2):
                        act.wait_ge(s_kf, 2 * i + h + 1)
                        act.copy(kh[:, h, :], kf[:, h, :]).then_inc(s_kh, 1)
                    for h in range(2):
                        if bias:
                            act.wait_ge(s_vb, 2 * i + h + 1)
                        act.wait_ge(s_vp, 2 * i + h + 1)
                        act.wait_ge(s_kv, 2 * i + h + 1)
                        act.copy(vh[:, h, :], vf[:, h, :] if bias else banks[:P, 4 + h, :]).then_inc(s_vh, 1)
                    if norm:
                        for h in range(2):
                            act.wait_ge(s_bd, 2 * i + h + 1)
                            act.wait_ge(s_ba, 2 * i + h + 1)
                            act.activation(sq[:, h, :], flat(y, 2 * i + h), ACT.Square).then_inc(s_bs, 1)
                for j in range(KT):
                    act.wait_ge(s_w, j + 1)
                    act.copy(kvw[0][:, j, :], banks[:, 2 + j, :]).then_inc(s_wh, 1)

            @block.vector
            def _(dve):
                dve.sem_inc(s_ke, 2)
                dve.sem_inc(s_vl, 2)
                if stats:
                    stats.tiles(dve)
                    stats.finish(dve)
                dve.wait_ge(s_row, nrow)
                dve.memset(banks[:, 6:8, :], 0.0).then_inc(s_one, 1)
                xt.rows(dve, 0)
                xt.low(dve, 0)
                w.low(dve)
                if norm:
                    dve.wait_ge(s_bm, 1)
                    dve.tensor_copy(centre[:, :], banks[:P, 2, :]).then_inc(s_bc, 1)
                    dve.wait_ge(s_bc, 1)
                with dve.Fori(0, NP) as i:
                    xt.rows(dve, i + 1)
                    if bias:
                        for h in range(2):
                            dve.wait_ge(s_kp, 2 * i + h + 1)
                            dve.wait_ge(s_ke, 2 * i + h + 1)
                            dve.tensor_tensor(kb[:, h, :], banks[:P, 2 + h, :], rows[:, 0, :], ALU.add).then_inc(s_kb, 1)
                        for h in range(2):
                            dve.wait_ge(s_vp, 2 * i + h + 1)
                            dve.wait_ge(s_vl, 2 * i + h + 1)
                            dve.tensor_tensor(vf[:, h, :], banks[:P, 4 + h, :], rows[:, 1, :], ALU.add).then_inc(s_vb, 1)
                    xt.low(dve, i + 1)
                    for h in range(2):
                        dve.wait_ge(s_ke, 2 * i + h + 3)
                        dve.wait_ge(s_kv, 2 * i + h + 1)
                        dve.scalar_tensor_tensor(kf[:, h, :], kx[:, h, 0, :], 1.0, kx[:, h, 1, :], ALU.min,
                                                 ALU.add).then_inc(s_kf, 1)
                    for h in range(2):
                        dve.wait_ge(s_kh, 2 * i + h + 1)
                        dve.tensor_tensor(kl[:, h, :], kf[:, h, :], kh[:, h, :].bitcast(F32),
                                          ALU.subtract).then_inc(s_kl, 1)
                    for h in range(2):
                        dve.wait_ge(s_vh, 2 * i + h + 1)
                        dve.tensor_tensor(vl[:, h, :], vf[:, h, :] if bias else banks[:P, 4 + h, :],
                                          vh[:, h, :].bitcast(F32), ALU.subtract).then_inc(s_vl, 1)
                    if norm:
                        for h in range(2):
                            dve.tensor_tensor(flat(y, 2 * i + h), flat(y, 2 * i + h), centre[:, :],
                                              ALU.subtract).then_inc(s_bd, 1)
                dve.wait_ge(s_kv, 2 * NP + 2)
                kvb = banks[:, 6, :].rearrange("p (j d) -> p j d", d=128)
                many = mask[:, :].unsqueeze(1).to_broadcast([128, KT, 128])
                dve.tensor_tensor(kvm[:, :, :], kvb, many, ALU.mult).then_inc(s_f, 1)
                dve.tensor_copy(ksm[:, :], banks[:, 7, 0:2 * KT].rearrange("p (j a) -> p j a", a=2)[:, :, 0]).then_inc(s_f, 1)
                dve.wait_ge(s_f, 2)
                dve.tensor_tensor(ks8f[:, :, :], hcol[:, :, :], ksm[:, :].unsqueeze(2).to_broadcast([128, KT, H]),
                                  ALU.mult).then_inc(s_f, 1)
                dve.tensor_copy(sel[:, :, :], hrow[:, :, :])
                dve.wait_ge(s_f, 3)
                dve.tensor_copy(ks8[0][:, :, :], ks8f[:, :, :]).then_inc(s_f, 1)
                dve.wait_ge(s_f, 4)
                dve.tensor_tensor(ks8[1][:, :, :], ks8f[:, :, :], ks8[0][:, :, :].bitcast(F32), ALU.subtract)
                if norm:
                    dve.wait_ge(s_bv, 1)
                    dve.tensor_scalar(var[:, :], banks[:P, 1, :], EPS, None, ALU.add)
                dve.wait_ge(s_wh, KT)
                for j in range(KT):
                    dve.tensor_tensor(kvw[1][:, j, :], banks[:, 2 + j, :], kvw[0][:, j, :].bitcast(F32), ALU.subtract)

        qx = sb("qx", [128, 2, KT, 2 * P], F32)
        qf = sb("qf", [128, KT, 2 * P], F32)
        qp = [sb(f"qp{a}", [128, KT, 2 * P], F32R) for a in range(2)]
        rz = sb("rz", [H, 2, 2 * P], F32)
        zs = [sb(f"zs{a}", [H, 2 * P], F32R) for a in range(2)]
        qz = sb("qz", [128, KT, 2 * P], F32)
        qs = [sb(f"qs{a}", [128, KT, 2, P], F32R) for a in range(2)]
        tmp = sb("tmp", [P, 2, D], F32)
        ab = sb("ab", [P, 2, NT], F32)
        xt = Normed(k, sb, f"{name}q", x, mean, rstd, ident, 0, gb)
        inv = sb("inv", [P, 2, D], F32) if norm else None
        xb = sb("xb", [P, 2, D], F32) if norm else None
        once = base
        s_qp, s_qe, s_qf, s_qh, s_ql = sem("qp"), sem("qe"), sem("qf"), sem("qh"), sem("ql")
        s_z = sem("z")
        s_ze, s_zr, s_zh, s_zl = sem("ze"), sem("zr"), sem("zh"), sem("zl")
        s_zb = sem("zb")
        s_qz, s_sh, s_sl = sem("qz"), sem("sh"), sem("sl")
        s_br, s_bi, s_bt, s_xb = sem("br"), sem("bi"), sem("bt"), sem("xb")
        s_o, s_t, s_y, s_b, s_ab = sem("o"), sem("t"), sem("y"), sem("b"), sem("ab")
        block = ctx.enter_context(nc.Block())

        def tile(a, t):
            return a[:, ds(t, 1), :].rearrange("p a f -> p (a f)")

        def qbank(f):
            return banks[:, 2 + f // 2, f % 2 * 2 * P:(f % 2 + 1) * 2 * P]

        def zbank(f):
            return banks[:, 4 + f // 2, f % 2 * 2 * P:(f % 2 + 1) * 2 * P]

        @block.tensor
        def _(pe):
            def q_products(i, tiles):
                for f in tiles:
                    product(pe, qbank(f), wq, xt.parts(), feature_tile(f), range(KT)).then_inc(s_qp, 1)

            xt.transposes(pe, 0)
            xt.wait(pe, 0)
            q_products(0, range(KT))
            xt.transposes(pe, 1)
            with pe.Fori(0, NP) as i:
                for f in range(KT):
                    pe.wait_ge(s_ql, KT * i + f + 1)
                    if f == 0:
                        pe.wait_ge(s_qz, i + 1)
                    ins = product(pe, banks[0:H, 4, 0:2 * P], ks8, qp, plain, [f], first=f == 0, last=f == KT - 1)
                ins.then_inc(s_z, 1)
                xt.wait(pe, i + 1)
                q_products(i + 1, range(2))
                pe.wait_ge(s_zl, i + 1)
                for f in range(KT):
                    for a in range(2):
                        ins = pe.matmul(zbank(f), sel[:, f, :], zs[a][:, :], start=a == 0, stop=a == 1)
                ins.then_inc(s_zb, 1)
                q_products(i + 1, range(2, KT))
                xt.transposes(pe, i + 2)
                for h in range(2):
                    if h == 0:
                        pe.wait_ge(s_sl, i + 1)
                    pe.wait_ge(s_t, 2 * i + h + 1)
                    product(pe, banks[:P, 6 + h, :], qs, kvw, half_of(h), range(KT)).then_inc(s_o, 1)

        @block.scalar
        def _(act):
            def elu(i):
                for f in range(KT):
                    act.wait_ge(s_qp, KT * i + f // 2 * 2 + 2)
                    b = bq[:, f:f + 1] if bias else 0.0
                    act.activation(qx[:, 0, f, :], qbank(f), ACT.Exp, bias=b)
                    act.activation(qx[:, 1, f, :], qbank(f), ACT.Relu, bias=b).then_inc(s_qe, 1)
                for f in range(KT):
                    act.wait_ge(s_qf, KT * i + f + 1)
                    act.copy(qp[0][:, f, :], qf[:, f, :]).then_inc(s_qh, 1)

            xt.high(act, 0)
            elu(0)
            xt.high(act, 1, s_qp, KT)
            if norm:
                act.activation(inv[:, 0, :], var[:, :], ACT.Sqrt).then_inc(s_br, 1)
            with act.Fori(0, NP) as i:
                act.wait_ge(s_zr, i + 1)
                act.copy(zs[0][:, :], rz[:, 1, :]).then_inc(s_zh, 1)
                act.wait_ge(s_qz, i + 2)
                act.wait_ge(s_o, 2 * i + 1)
                act.copy(qs[0][:, :, :, :].rearrange("p c h n -> p c (h n)"), qz[:, :, :]).then_inc(s_sh, 1)
                elu(i + 1)
                xt.high(act, i + 2, s_qp, KT * i + 2 * KT)

        @block.vector
        def _(dve):
            def elu(i):
                for f in range(KT):
                    dve.wait_ge(s_qe, KT * i + f + 1)
                    dve.scalar_tensor_tensor(qf[:, f, :], qx[:, 0, f, :], 1.0, qx[:, 1, f, :], ALU.min,
                                             ALU.add).then_inc(s_qf, 1)
                for f in range(KT):
                    dve.wait_ge(s_qh, KT * i + f + 1)
                    dve.tensor_tensor(qp[1][:, f, :], qf[:, f, :], qp[0][:, f, :].bitcast(F32),
                                      ALU.subtract).then_inc(s_ql, 1)

            dve.sem_inc(s_t, 2)
            dve.sem_inc(s_qz, 1)
            dve.sem_inc(s_o, 1)
            if once is not None:
                dve.tensor_scalar(ab[:, 0, :], once[1][:, :], 1.0, None, ALU.add).then_inc(s_ab, 1)
                dve.tensor_tensor(ab[:, 1, :], once[0][:, :], once[1][:, :], ALU.mult).then_inc(s_ab, 1)
                dve.wait_ge(s_ab, 2)
            xt.rows(dve, 0)
            xt.low(dve, 0)
            xt.rows(dve, 1)
            if norm:
                dve.tensor_tensor(rows[:, 2, :], rows[:, 2, :], rows[:, 1, :], ALU.add).then_inc(s_bi, 1)
            elu(0)
            xt.low(dve, 1)
            if norm:
                dve.wait_ge(s_br, 1)
                dve.reciprocal(inv[:, 1, :], inv[:, 0, :]).then_inc(s_bi, 1)
                dve.wait_ge(s_bi, 2)
                dve.tensor_tensor(inv[:, 1, :], inv[:, 1, :], rows[:, 0, :], ALU.mult).then_inc(s_bi, 1)
                dve.wait_ge(s_bi, 3)
            with dve.Fori(0, NP) as i:
                dve.wait_ge(s_z, i + 1)
                dve.tensor_scalar(rz[:, 0, :], banks[0:H, 4, 0:2 * P], eps_of(name), None, ALU.add).then_inc(s_ze, 1)
                dve.wait_ge(s_ze, i + 1)
                dve.reciprocal(rz[:, 1, :], rz[:, 0, :]).then_inc(s_zr, 1)
                dve.wait_ge(s_zh, i + 1)
                dve.tensor_tensor(zs[1][:, :], rz[:, 1, :], zs[0][:, :].bitcast(F32), ALU.subtract).then_inc(s_zl, 1)
                xt.rows(dve, i + 2)
                dve.wait_ge(s_zb, i + 1)
                for g in range(2):
                    ins = dve.tensor_tensor(qz[:, 2 * g:2 * g + 2, :], qf[:, 2 * g:2 * g + 2, :],
                                            banks[:, 4 + g, 0:4 * P].rearrange("p (f n) -> p f n", f=2), ALU.mult)
                ins.then_inc(s_qz, 1)
                dve.wait_ge(s_sh, i + 1)
                dve.tensor_tensor(qs[1][:, :, :, :].rearrange("p c h n -> p c (h n)"), qz[:, :, :],
                                  qs[0][:, :, :, :].bitcast(F32).rearrange("p c h n -> p c (h n)"),
                                  ALU.subtract).then_inc(s_sl, 1)
                elu(i + 1)
                xt.low(dve, i + 2)
                for h in range(2):
                    t = 2 * i + h
                    if once is not None:
                        dve.tensor_scalar(tile(y, t), tile(x, t), ab[:, 0, ds(t, 1)], ab[:, 1, ds(t, 1)],
                                          ALU.mult, ALU.subtract).then_inc(s_b, 1)
                    if norm:
                        dve.tensor_tensor(tile(y, t), tile(y, t), inv[:, 1, :], ALU.mult).then_inc(s_bt, 1)
                        dve.wait_ge(s_xb, t + 1)
                    dve.wait_ge(s_o, t + 2)
                    dve.wait_ge(s_y, t + 1)
                    dve.tensor_tensor(tmp[:, h, :], banks[:P, 6 + h, :], xb[:, h, :] if norm else rows[:, 2, :],
                                      ALU.add).then_inc(s_t, 1)

        @block.gpsimd
        def _(pool):
            pool.sem_inc(s_y, 2)
            if norm:
                pool.wait_ge(s_bi, 1)
            with pool.Fori(0, NP) as i:
                if norm:
                    for h in range(2):
                        t = 2 * i + h
                        pool.wait_ge(s_t, t + 1)
                        pool.tensor_tensor(xb[:, h, :], tile(x, t), rows[:, 2, :], ALU.add).then_inc(s_xb, 1)
                for h in range(2):
                    t = 2 * i + h
                    if once is not None:
                        pool.wait_ge(s_b, t + 1)
                    if norm:
                        pool.wait_ge(s_bt, t + 1)
                    pool.wait_ge(s_t, t + 3)
                    pool.tensor_tensor(tile(y, t), tile(y, t), tmp[:, h, :], ALU.add).then_inc(s_y, 1)


def eps_of(name):
    return {"mix0": 1e-6, "mix1": 1e-8}[name]


def flat(a, t):
    return a[:, ds(t, 1), :].rearrange("p a f -> p (a f)")


def plain(a, b, c):
    return a[:, c, :], b[:, c, :]


def experts_phase(k, x, mean, rstd, ident, sel, gate_w, w1, sw1, w2, sw2, b1_cols, b2_rows):
    nc, banks = k.nc, k.banks
    EX, FT = 8, 12
    with ExitStack() as ctx:
        def sb(nm, shape, dt):
            return ctx.enter_context(nc.sbuf_tensor(f"moe_{nm}", shape, dt))

        def sem(nm):
            return k.sem(f"s_moe_{nm}")

        v1 = [sb(f"v1{a}", [128, KT, 1024], F32R) for a in range(2)]
        vs1 = [sb(f"vs1{a}", [128, KT, D], F32R) for a in range(2)]
        v2 = [sb(f"v2{a}", [128, FT, D], F32R) for a in range(2)]
        vg = [sb(f"vg{a}", [128, KT, EX], F32R) for a in range(2)]
        vb = [sb(f"vb{a}", [EX + 1, D], F32R) for a in range(2)]
        sel_r = sb("sel", [EX, EX, 128], F32R)
        b1 = sb("b1", [128, FT], F32)
        w = Weights(k, sb, "moe", [
            (gate_w.rearrange("(c p) e -> p c e", p=128), vg[0][:], vg[1][:]),
            (b2_rows, vb[0][:, :], vb[1][:, :]),
            (sw1.rearrange("(c p) f -> p c f", p=128), vs1[0][:], vs1[1][:]),
            (w1.rearrange("(c p) f -> p c f", p=128), v1[0][:], v1[1][:])], stages=3)
        late = Weights(k, sb, "moel", [
            (w2.rearrange("e p f -> p e f"), v2[0][:, 0:EX], v2[1][:, 0:EX]),
            (sw2.rearrange("(c p) f -> p c f", p=128), v2[0][:, EX:], v2[1][:, EX:])])
        xt = Normed(k, sb, "moex", x, mean, rstd, ident, 0)
        stats = Stats(k, sb, "st1", x, mean, rstd)
        ht = [sb(f"ht{a}", [128, FT, 2, P], F32R) for a in range(2)]
        hr = sb("hr", [128, 2, 2 * P], F32)
        hp = sb("hp", [128, 2, 2 * P], F32)
        iota8 = sb("iota8", [P, EX], F32)
        g1 = sb("g1", [P, 8, 2, EX], F32)
        g0 = sb("g0", [P, 8, 2], F32)
        cth = sb("cth", [EX + 1, 2, P], F32R)
        ctl = sb("ctl", [EX + 1, 2, P], F32R)
        s_c0 = sem("c0")
        s_bl = sem("bl")
        s_g = sem("g")
        s_gs = sem("gs")
        s_ge = sem("ge")
        s_ct = sem("ct")
        s_c1, s_cc = sem("c1"), sem("cc")
        s_h = sem("h")
        s_r = sem("r")
        s_p = sem("p")
        s_hh = sem("hh")
        s_hl = sem("hl")
        s_o = sem("o")
        s_y = sem("y")
        block = ctx.enter_context(nc.Block())
        LINKS = 22
        order = list(range(EX, FT)) + list(range(EX))

        @block.sync
        def _(sp):
            sp.dma_start(b1[:, :], b1_cols).then_inc(s_bl, 16)
            sp.dma_start(hp[0:EX, :, :].rearrange("p a b -> p (a b)"), sel[:, 0:4 * P]).then_inc(s_bl, 16)
            sp.dma_start(hr[0:EX, :, :].rearrange("p a b -> p (a b)"), sel[:, 4 * P:8 * P]).then_inc(s_bl, 16)
            sp.dma_start(g1[0:EX, 0:2, :, :].rearrange("p a b c -> p (a b c)")[:, 0:EX * 128 - 8 * P],
                         sel[:, 8 * P:EX * 128]).then_inc(s_bl, 16)
            w.load(sp)
            late.load(sp)

        @block.gpsimd
        def _(pool):
            pool.iota(iota8[:, :], [[1, EX]], base=0, channel_multiplier=0,
                      allow_small_or_imprecise_dtypes=True).then_inc(s_c0, 1)
            late.split(pool)

        @block.tensor
        def _(pe):
            pe.sem_inc(s_o, 1)
            xt.transposes(pe, 0)
            w.wait(pe, 4)
            pe.wait_ge(s_c0, 4)
            with pe.Fori(0, NP) as i:
                xt.wait(pe, i)
                xt.transposes(pe, i + 1)
                pe.wait_ge(s_cc, i + 1)
                for h in range(2):
                    ins = product(pe, banks[:P, 5, EX * h:EX * (h + 1)], xt.parts(), vg, half_of(h), range(KT))
                ins.then_inc(s_g, 1)
                for q, f in enumerate(order):
                    if q == 3:
                        pe.wait_ge(s_gs, LINKS * (i + 1))
                        for h in range(2):
                            ins = pe.transpose(banks[0:EX, 5, 128 + h * P:128 + (h + 1) * P], g1[:, 7, h, :],
                                               ident[:P, :P])
                        ins.then_inc(s_ct, 1)
                    if q == FT - EX:
                        pe.wait_ge(s_cc, i + 2)
                        w.wait(pe)
                    pe.wait_ge(s_hl, FT * i + q + 1)
                    bank = banks[:, 2 + q % 3, :]
                    ws, col = (v1, f) if f < EX else (vs1, f - EX)
                    ins = product(pe, bank[:, 0:2 * P], ws, xt.parts(), feature_tile(col), range(KT))
                    if f < EX:
                        for n, part in enumerate((cth, ctl)):
                            ins = pe.matmul(bank[:, 2 * P:4 * P], sel_r[:, f, :],
                                            part[0:EX, :, :].rearrange("p h n -> p (h n)"), start=n == 0, stop=n == 1)
                    ins.then_inc(s_h, 1)
                late.wait(pe)
                for h in range(2):
                    pe.wait_ge(s_y, 2 * i + h + 1)
                    out = banks[:P, 6 + h, :]
                    for n, (a, b) in enumerate(((cth, vb[0]), (cth, vb[1]), (ctl, vb[0]))):
                        pe.matmul(out, a[:, h, :], b[:, :], start=n == 0, stop=False)
                    for q, f in enumerate(order):
                        pe.wait_ge(s_hl, FT * i + q + 1 + 3)
                        ins = product(pe, out, ht, v2, half_of(h), [f], first=False, last=q == FT - 1)
                    ins.then_inc(s_o, 1)

        @block.scalar
        def _(act):
            stats.root(act)
            xt.high(act, 0)
            w.high(act)
            act.wait_ge(s_bl, 64)
            with act.Fori(0, NP) as i:
                act.wait_ge(s_gs, LINKS * i + 2)
                act.activation(g1[:, 1], g1[:, 0], ACT.Exp).then_inc(s_ge, 1)
                for q in range(FT + 1):
                    if q < FT:
                        f = order[q]
                        act.wait_ge(s_h, FT * i + q + 1)
                        act.wait_ge(s_hl, FT * i + q + 2)
                        act.activation(hr[:, q % 2, :], banks[:, 2 + q % 3, 0:2 * P], ACT.Relu,
                                       bias=b1[:, f:f + 1]).then_inc(s_r, 1)
                    if q:
                        m, f = q - 1, order[q - 1]
                        if f < EX:
                            act.wait_ge(s_p, EX * i + f + 1)
                        else:
                            act.wait_ge(s_r, FT * i + m + 1)
                        act.copy(ht[0][:, f, :, :].rearrange("p h n -> p (h n)"),
                                 (hp if f < EX else hr)[:, m % 2, :]).then_inc(s_hh, 1)
                xt.high(act, i + 1, s_h, FT * i + FT)

        @block.vector
        def _(dve):
            dve.sem_inc(s_hl, 3)
            dve.sem_inc(s_y, 2)
            stats.tiles(dve)
            stats.finish(dve)
            dve.wait_ge(s_bl, 64)
            flat_sel = sel_r[:, :, :].rearrange("p e m -> p (e m)")
            dve.tensor_copy(flat_sel[:, 0:4 * P], hp[0:EX, :, :].rearrange("p a b -> p (a b)"))
            dve.tensor_copy(flat_sel[:, 4 * P:8 * P], hr[0:EX, :, :].rearrange("p a b -> p (a b)")).then_inc(s_c0, 1)
            dve.tensor_copy(flat_sel[:, 8 * P:], g1[0:EX, 0:2, :, :].rearrange("p a b c -> p (a b c)")[:, 0:EX * 128 - 8 * P])\
               .then_inc(s_c0, 1)
            dve.memset(cth[:, :, :].bitcast(F32), 1.0).then_inc(s_cc, 1)
            dve.memset(ctl[:, :, :].bitcast(F32), 0.0).then_inc(s_c0, 1)
            dve.wait_ge(s_c0, 4)
            xt.rows(dve, 0)
            xt.low(dve, 0)
            w.low(dve)
            with dve.Fori(0, NP) as i:
                xt.rows(dve, i + 1)
                n = [0]

                def link(ins):
                    n[0] += 1
                    ins.then_inc(s_gs, 1)
                    dve.wait_ge(s_gs, LINKS * i + n[0])

                def wide(a):
                    return a.unsqueeze(2).to_broadcast([P, 2, EX])

                gate = banks[:P, 5, 0:2 * EX].rearrange("p (h e) -> p h e", e=EX)
                many = iota8[:, :].unsqueeze(1).to_broadcast([P, 2, EX])
                dve.wait_ge(s_g, i + 1)
                link(dve.tensor_reduce(g0[:, 0], gate, AX.X, ALU.max))
                link(dve.tensor_tensor(g1[:, 0], gate, wide(g0[:, 0]), ALU.subtract))
                dve.wait_ge(s_ge, i + 1)
                link(dve.tensor_reduce(g0[:, 1], g1[:, 1], AX.X, ALU.add))
                link(dve.reciprocal(g0[:, 2], g0[:, 1]))
                link(dve.tensor_tensor(g1[:, 2], g1[:, 1], wide(g0[:, 2]), ALU.mult))
                for c, seen in ((4, g1[:, 2]), (5, g1[:, 3])):
                    link(dve.tensor_reduce(g0[:, 3], seen, AX.X, ALU.max))
                    link(dve.tensor_tensor(g1[:, 6], seen, wide(g0[:, 3]), ALU.is_lt))
                    link(dve.scalar_tensor_tensor(g1[:, 6], g1[:, 6], float(EX), many, ALU.mult, ALU.add))
                    link(dve.tensor_reduce(g0[:, 4], g1[:, 6], AX.X, ALU.min))
                    link(dve.tensor_tensor(g1[:, c], many, wide(g0[:, 4]), ALU.is_equal))
                    if c == 4:
                        link(dve.scalar_tensor_tensor(g1[:, 3], g1[:, 4], -2.0, g1[:, 2], ALU.mult, ALU.add))
                link(dve.tensor_tensor(g1[:, 4], g1[:, 4], g1[:, 5], ALU.add))
                link(dve.tensor_tensor(g1[:, 6], g1[:, 2], g1[:, 4], ALU.mult))
                link(dve.tensor_reduce(g0[:, 3], g1[:, 6], AX.X, ALU.add))
                link(dve.tensor_scalar(g0[:, 4], g0[:, 3], 1e-20, None, ALU.add))
                link(dve.reciprocal(g0[:, 5], g0[:, 4]))
                link(dve.tensor_tensor(g1[:, 7], g1[:, 6], wide(g0[:, 5]), ALU.mult))
                assert n[0] == LINKS
                dve.wait_ge(s_ct, i + 1)
                tr = banks[0:EX, 5, 128:128 + 2 * P].rearrange("p (h n) -> p h n", n=P)
                dve.wait_ge(s_o, 2 * i + 1)
                dve.tensor_copy(cth[0:EX, :, :], tr).then_inc(s_c1, 1)
                dve.wait_ge(s_c1, i + 1)
                dve.tensor_tensor(ctl[0:EX, :, :], tr, cth[0:EX, :, :].bitcast(F32), ALU.subtract).then_inc(s_cc, 1)
                for q in range(FT + 1):
                    if q < FT and order[q] < EX:
                        f = order[q]
                        dve.wait_ge(s_r, FT * i + q + 1)
                        dve.tensor_tensor(hp[:, q % 2, :], hr[:, q % 2, :], banks[:, 2 + q % 3, 2 * P:4 * P],
                                          ALU.mult).then_inc(s_p, 1)
                    if q:
                        m, f = q - 1, order[q - 1]
                        dve.wait_ge(s_hh, FT * i + m + 1)
                        dve.tensor_tensor(ht[1][:, f, :, :].rearrange("p h n -> p (h n)"),
                                          (hp if f < EX else hr)[:, m % 2, :],
                                          ht[0][:, f, :, :].bitcast(F32).rearrange("p h n -> p (h n)"),
                                          ALU.subtract).then_inc(s_hl, 1)
                xt.low(dve, i + 1)
                for h in range(2):
                    dve.wait_ge(s_o, 2 * i + h + 2)
                    dve.tensor_tensor(flat(x, 2 * i + h), flat(x, 2 * i + h), banks[:P, 6 + h, :],
                                      ALU.add).then_inc(s_y, 1)


def graph_phase(k, x, y, mean, rstd, ident, deg, counts_d, esum_d, wm, wu, bias_rows, gamma, beta):
    nc, banks = k.nc, k.banks
    with ExitStack() as ctx:
        def sb(nm, shape, dt):
            return ctx.enter_context(nc.sbuf_tensor(f"gn_{nm}", shape, dt))

        def sem(nm):
            return k.sem(f"s_gn_{nm}")

        wms = [sb(f"wm{a}", [128, KT, D], F32R) for a in range(2)]
        wus = [sb(f"wu{a}", [128, 2 * KT, D], F32R) for a in range(2)]
        wbs = [sb(f"wb{a}", [2, 2, D], F32R) for a in range(2)]
        w = Weights(k, sb, "gn", [(wm.rearrange("(c p) f -> p c f", p=128), wms[0][:], wms[1][:]),
                                  (bias_rows, wbs[0][:], wbs[1][:])])
        late = Weights(k, sb, "gnl", [(wu.rearrange("(c p) f -> p c f", p=128), wus[0][:], wus[1][:])], stages=1)
        xa = [sb(f"xa{a}", [P, NT, D], F32R) for a in range(2)]
        xf = sb("xf", [P, 2, D], F32)
        row = late.stage[:P, 0, :].rearrange("p (a f) -> p a f", a=2)
        cin = sb("cin", [P, NT, P], U16)
        ein = sb("ein", [P, D], F32)
        cs = [sb(f"cs{a}", [P, NT, P], F32R) for a in range(2)]
        rd = sb("rd", [P, 3, NT], F32)
        ag = sb("ag", [P, 2, D + 2], F32)
        at = [sb(f"at{a}", [128, KT, 2, P], F32R) for a in range(2)]
        gt = sb("gt", [2, 2, P], F32R)
        mt = [sb(f"mt{a}", [128, KT, 2, P], F32R) for a in range(2)]
        xt = Normed(k, sb, "gnx", x, mean, rstd, ident, 0)
        og = sb("og", [P, 2, D], F32)
        stats = sb("stats", [P, NT, nc.vector.BN_STATS_DIM], F32)
        mv = sb("mv", [P, NT, 2], F32)
        lr = sb("lr", [P, 3, NT], F32)
        s_row = sem("row")
        s_xf, s_xh, s_x1 = sem("xf"), sem("xh"), sem("x1")
        s_rd = sem("rd")
        s_in = [sem(f"in{a}") for a in range(2)]
        s_ch, s_cl = sem("ch"), sem("cl")
        s_ag = sem("ag")
        s_e1 = sem("e1")
        s_e2 = sem("e2")
        s_at = sem("at")
        s_ah, s_al = sem("ah"), sem("al")
        s_mp = sem("mp")
        s_mh, s_ml = sem("mh"), sem("ml")
        s_u = sem("u")
        s_ge = sem("ge")
        s_gx, s_go = sem("gx"), sem("go")
        s_bs, s_yb = sem("bs"), sem("yb")
        s_ln, s_sq, s_f1, s_f2 = sem("ln"), sem("sq"), sem("f1"), sem("f2")
        block = ctx.enter_context(nc.Block())

        def tile_of(eng, n):
            return n % NT if isinstance(n, int) else eng.snap(nc.s_assert_within(n % NT, 0, NT - 1))

        @block.sync
        def _(sp):
            def load(n):
                t = tile_of(sp, n)
                sp.wait_ge(s_cl, n + 1)
                sp.dma_start(cin[:, :, :], counts_d[ds(t, 1), :, :, :].rearrange("t p a d -> (t p) a d")).then_inc(s_in[0], 16)
                sp.wait_ge(s_e1, n + 1)
                sp.dma_start(ein[:, :], esum_d[ds(t, 1), :, :].rearrange("t p f -> (t p) f")).then_inc(s_in[1], 16)

            load(0)
            w.load(sp)
            late.load(sp, last=2)
            load(1)
            late.load(sp, first=2, last=4)
            load(2)
            late.load(sp, first=4)
            late.wait(sp)
            sp.dma_start(row[:, 0, :], gamma.partition_broadcast(P)).then_inc(s_row, 16)
            sp.dma_start(row[:, 1, :], beta.partition_broadcast(P)).then_inc(s_row, 16)
            with sp.Fori(0, NP) as i:
                load(2 * i + 3)
                load(2 * i + 4)
            for landed in s_in:
                sp.wait_ge(landed, (NT + 3) * 16)

        @block.gpsimd
        def _(pool):
            late.split(pool)
            pool.wait_ge(s_row, 32)
            with pool.Fori(0, NT) as t:
                pool.tensor_tensor(flat(y, t), flat(y, t), row[:, 1, :], ALU.add).then_inc(s_yb, 1)

        @block.tensor
        def _(pe):
            def sums(n, h):
                pe.wait_ge(s_cl, n + 2)
                pe.wait_ge(s_e1, n + 1)
                for c in range(NT):
                    for m, (a, b) in enumerate(((0, 0), (0, 1), (1, 0))):
                        ins = pe.matmul(banks[:P, 2 + h, :], cs[a][:, c, :], xa[b][:, c, :], start=c == 0 and m == 0,
                                        stop=c == NT - 1 and m == 2)
                ins.then_inc(s_ag, 1)

            pe.sem_inc(s_ag, 1)
            pe.sem_inc(s_at, 2)
            pe.sem_inc(s_mp, 1)
            pe.sem_inc(s_u, 1)
            pe.wait_ge(s_x1, NT)
            for n in range(2):
                sums(n, n)
            xt.transposes(pe, 0)
            w.wait(pe)
            with pe.Fori(0, NP) as i:
                pe.wait_ge(s_ge, 2 * i + 1)
                for h in range(2):
                    pe.wait_ge(s_e2, 2 * i + h + 1)
                    for c in range(KT):
                        pe.transpose(banks[:, 4 + h, c * P:(c + 1) * P], ag[:, h, c * 128:(c + 1) * 128], ident[:P, :P])
                    if h == 0:
                        pe.wait_ge(s_ml, i * KT + 2)
                    pe.transpose(banks[0:2, 6 + h, 0:P], ag[:, h, D:D + 2], ident[:P, :P]).then_inc(s_at, 1)
                sums(2 * i + 2, 0)
                pe.wait_ge(s_al, 2 * i + 2)
                for f in range(KT):
                    pe.wait_ge(s_ml, i * KT + f + 1)
                    out = banks[:, 6 + f % 2, 0:2 * P]
                    product(pe, out, wms, at, feature_tile(f), range(KT), last=False)
                    g = gt[:, :, :].rearrange("p h n -> p (h n)")
                    for a in range(2):
                        ins = pe.matmul(out, wbs[a][:, 0, f * 128:(f + 1) * 128], g, start=False, stop=a == 1)
                    ins.then_inc(s_mp, 1)
                sums(2 * i + 3, 1)
                xt.wait(pe, i)
                xt.transposes(pe, i + 1)
                late.wait(pe)
                pe.wait_ge(s_ml, (i + 1) * KT + 2)
                for h in range(2):
                    out = banks[:P, 4 + h, :]
                    product(pe, out, xt.parts(), wus, half_of(h), range(KT), last=False)
                    product(pe, out, mt, wus, lambda a, b, c: (a[:, c, h, :], b[:, KT + c, :]), range(KT), first=False,
                            last=False)
                    for a in range(2):
                        ins = pe.matmul(out, gt[:, h, :], wbs[a][:, 1, :], start=False, stop=a == 1)
                    ins.then_inc(s_u, 1)

        @block.scalar
        def _(act):
            def counts_high(n):
                act.wait_ge(s_in[0], n * 16 + 16)
                act.wait_ge(s_ag, n + 1)
                act.copy(cs[0][:, :, :], cin[:, :, :]).then_inc(s_ch, 1)

            act.sem_inc(s_ge, 1)
            for t in range(NT):
                act.wait_ge(s_xf, t + 1)
                act.copy(xa[0][:, t, :], xf[:, t % 2, :]).then_inc(s_xh, 1)
            counts_high(0)
            w.high(act)
            for n in (1, 2):
                counts_high(n)
            xt.high(act, 0)
            with act.Fori(0, NP) as i:
                act.wait_ge(s_mp, KT * i + 1)
                act.wait_ge(s_u, 2 * i + 1)
                for h in range(2):
                    act.wait_ge(s_at, 2 * i + h + 3)
                    act.copy(at[0][:, :, h, :], banks[:, 4 + h, 0:KT * P].rearrange("p (c n) -> p c n", n=P))
                    act.copy(gt[:, h, :], banks[0:2, 6 + h, 0:P]).then_inc(s_ah, 1)
                counts_high(2 * i + 3)
                for f in range(KT):
                    act.wait_ge(s_mp, KT * i + f + 2)
                    act.copy(mt[0][:, f, :, :].rearrange("p h n -> p (h n)"), banks[:, 6 + f % 2, 0:2 * P]).then_inc(s_mh, 1)
                counts_high(2 * i + 4)
                for h in range(2):
                    act.wait_ge(s_u, 2 * i + h + 2)
                    act.wait_ge(s_go, 2 * i + h + 1)
                    act.activation(og[:, h, :], banks[:P, 4 + h, :], ACT.Gelu).then_inc(s_ge, 1)
                xt.high(act, i + 1, s_u, 2 * i + 2, 1)
            act.wait_ge(s_ln, 1)
            act.activation(lr[:, 1, :], lr[:, 0, :], ACT.Sqrt).then_inc(s_sq, 1)

        @block.vector
        def _(dve):
            def counts_low(n):
                dve.wait_ge(s_ch, n + 1)
                dve.tensor_tensor(cs[1][:, :, :], cin[:, :, :], cs[0][:, :, :].bitcast(F32),
                                  ALU.subtract).then_inc(s_cl, 1)

            def average(n, h):
                t = tile_of(dve, n)
                dve.wait_ge(s_in[1], n * 16 + 16)
                dve.wait_ge(s_ag, n + 2)
                dve.wait_ge(s_at, n + 1)
                dve.tensor_tensor(ag[:, h, 0:D], banks[:P, 2 + h, :], ein[:, :], ALU.add).then_inc(s_e1, 1)
                dve.tensor_copy(ag[:, h, D:D + 1], rd[:, 2, ds(t, 1)])
                dve.wait_ge(s_e1, n + 2)
                dve.tensor_scalar(ag[:, h, 0:D], ag[:, h, 0:D], rd[:, 1, ds(t, 1)], None, ALU.mult).then_inc(s_e2, 1)

            dve.sem_inc(s_cl, 1)
            dve.sem_inc(s_e1, 1)
            dve.sem_inc(s_ml, 2)
            dve.sem_inc(s_go, 2)
            for t in range(NT + 1):
                if t < NT:
                    if t >= 2:
                        dve.wait_ge(s_x1, t - 1)
                    dve.tensor_scalar(xf[:, t % 2, :], x[:, t, :], mean[:, t:t + 1], rstd[:, t:t + 1], ALU.subtract,
                                      ALU.mult).then_inc(s_xf, 1)
                if 1 <= t <= NT:
                    dve.wait_ge(s_xh, t)
                    dve.wait_ge(s_xf, t)
                    dve.tensor_tensor(xa[1][:, t - 1, :], xf[:, (t - 1) % 2, :], xa[0][:, t - 1, :].bitcast(F32),
                                      ALU.subtract).then_inc(s_x1, 1)
            counts_low(0)
            link = chain(dve, s_rd)
            link(dve.tensor_scalar(rd[:, 0, :], deg[:, :], 1.0, None, ALU.max))
            link(dve.reciprocal(rd[:, 1, :], rd[:, 0, :]))
            link(dve.tensor_tensor(rd[:, 2, :], deg[:, :], rd[:, 1, :], ALU.mult))
            dve.memset(ag[:, :, D + 1:D + 2], 1.0)
            dve.wait_ge(s_x1, NT)
            w.low(dve)
            counts_low(1)
            average(0, 0)
            xt.rows(dve, 0)
            counts_low(2)
            average(1, 1)
            xt.low(dve, 0)
            with dve.Fori(0, NP) as i:
                for h in range(2):
                    dve.wait_ge(s_ah, 2 * i + h + 1)
                    dve.tensor_tensor(at[1][:, :, h, :], banks[:, 4 + h, 0:KT * P].rearrange("p (c n) -> p c n", n=P),
                                      at[0][:, :, h, :].bitcast(F32), ALU.subtract).then_inc(s_al, 1)
                for h in range(2):
                    t = 2 * i + h
                    dve.wait_ge(s_go, t + 1)
                    dve.tensor_scalar(xf[:, h, :], flat(x, t), mean[:, ds(t, 1)], rstd[:, ds(t, 1)], ALU.subtract,
                                      ALU.mult).then_inc(s_gx, 1)
                xt.rows(dve, i + 1)
                counts_low(2 * i + 3)
                average(2 * i + 2, 0)
                for f in range(KT):
                    dve.wait_ge(s_mh, KT * i + f + 1)
                    dve.tensor_tensor(mt[1][:, f, :, :].rearrange("p h n -> p (h n)"), banks[:, 6 + f % 2, 0:2 * P],
                                      mt[0][:, f, :, :].bitcast(F32).rearrange("p h n -> p (h n)"),
                                      ALU.subtract).then_inc(s_ml, 1)
                counts_low(2 * i + 4)
                average(2 * i + 3, 1)
                for h in range(2):
                    t = 2 * i + h
                    dve.wait_ge(s_gx, t + 1)
                    dve.wait_ge(s_ge, t + 2)
                    dve.tensor_tensor(flat(x, t), xf[:, h, :], og[:, h, :], ALU.add).then_inc(s_go, 1)
                xt.low(dve, i + 1)
                for h in range(2):
                    t = 2 * i + h
                    dve.wait_ge(s_go, t + 3)
                    dve.bn_stats(flat(stats, t), flat(x, t)).then_inc(s_bs, 1)
            dve.wait_ge(s_bs, NT)
            for t in range(NT):
                dve.bn_aggr(mv[:, t, :], stats[:, t, :]).then_inc(s_bs, 1)
            dve.wait_ge(s_bs, 2 * NT)
            dve.tensor_scalar(lr[:, 0, :], mv[:, :, 1], EPS, None, ALU.add).then_inc(s_ln, 1)
            dve.wait_ge(s_sq, 1)
            dve.reciprocal(lr[:, 2, :], lr[:, 1, :]).then_inc(s_ln, 1)
            dve.wait_ge(s_ln, 2)
            dve.wait_ge(s_row, 32)
            dve.wait_ge(s_yb, NT)
            with dve.Fori(0, NP) as i:
                for h in range(2):
                    t = 2 * i + h
                    dve.scalar_tensor_tensor(flat(x, t), flat(x, t), mv[:, ds(t, 1), 0], row[:, 0, :], ALU.subtract,
                                             ALU.mult).then_inc(s_f1, 1)
                for h in range(2):
                    t = 2 * i + h
                    dve.wait_ge(s_f1, t + 1)
                    dve.scalar_tensor_tensor(flat(y, t), flat(x, t), lr[:, 2, ds(t, 1)], flat(y, t), ALU.mult,
                                             ALU.add).then_inc(s_f2, 1)


def pooled_phase(k, x, mean, rstd, ident, attn_w, attn_b, gate_w, gate_b, w1, b1_cols, w2, b2, out):
    nc, banks = k.nc, k.banks
    EX, HT, TOP = 8, 2, 2
    with ExitStack() as ctx:
        def sb(nm, shape, dt):
            return ctx.enter_context(nc.sbuf_tensor(f"po_{nm}", shape, dt))

        def sem(nm):
            return k.sem(f"s_po_{nm}")

        chosen = sb("chosen", [1, TOP], I32)
        gcol = sb("gcol", [P, TOP], F32)
        ones = sb("ones", [P, 128], F32)

        with ExitStack() as inner:
            def sbi(nm, shape, dt):
                return inner.enter_context(nc.sbuf_tensor(f"po_{nm}", shape, dt))

            aw = sbi("aw", [P, D], F32)
            ab = sbi("ab", [P, 1], F32)
            gw = sbi("gw", [128, KT, EX], F32)
            gb = sbi("gb", [1, EX], F32)
            xa = sbi("xa", [P, NT, D], F32)
            xw = sbi("xw", [P, 2, D], F32)
            sc = sbi("sc", [P, 2, NT], F32)
            top = sbi("top", [128, 2], F32)
            glob = sbi("glob", [128, 1], F32)
            acc = sbi("acc", [P, D], F32)
            esum = sbi("esum", [P, 1], F32)
            tot = sbi("tot", [128, 1], F32)
            pl = sbi("pl", [128, KT], F32)
            r1 = sbi("r1", [1, 8, EX], F32)
            r0 = sbi("r0", [1, 8], F32)
            gn = sbi("gn", [1, TOP], F32)
            iota8 = sbi("iota8", [1, EX], F32)
            stats = Stats(k, sbi, "st3", x, mean, rstd)
            s_in, s_c, s_x, s_m, s_w, s_s = sem("in"), sem("c"), sem("x"), sem("m"), sem("w"), sem("s")
            s_pa, s_se = sem("pa"), sem("se")
            s_all, s_e, s_pl, s_gl, s_ge, s_gb = sem("all"), sem("e"), sem("pl"), sem("gl"), sem("ge"), sem("gb")
            block = inner.enter_context(nc.Block())

            @block.sync
            def _(sp):
                sp.dma_start(aw[:, :], attn_w.partition_broadcast(P)).then_inc(s_in, 16)
                sp.dma_start(ab[:, :], attn_b.partition_broadcast(P)).then_inc(s_in, 16)
                sp.dma_start(gw[:, :, :], gate_w.rearrange("(c p) e -> p c e", p=128)).then_inc(s_in, 16)
                sp.dma_start(gb[:, :], gate_b.partition_broadcast(1)).then_inc(s_in, 16)

            @block.gpsimd
            def _(pool):
                pool.memset(ones[:, :], 1.0)
                pool.iota(iota8[:, :], [[1, EX]], base=0, channel_multiplier=0,
                          allow_small_or_imprecise_dtypes=True).then_inc(s_c, 1)
                pool.wait_ge(s_in, 64)
                for t in range(NT):
                    pool.wait_ge(s_x, t + 1)
                    if t >= 2:
                        pool.wait_ge(s_w, t - 1)
                    pool.tensor_tensor(xw[:, t % 2, :], xa[:, t, :], aw[:, :], ALU.mult).then_inc(s_m, 1)
                pool.wait_ge(s_s, 4)
                pool.partition_all_reduce(glob[:, :], top[:, 0:1], 128, bass.bass_isa.ReduceOp.max).then_inc(s_all, 1)

            @block.vector
            def _(dve):
                stats.tiles(dve)
                stats.finish(dve)
                dve.wait_ge(s_in, 64)
                for t in range(NT + 2):
                    if t < NT:
                        dve.tensor_scalar(xa[:, t, :], x[:, t, :], mean[:, t:t + 1], rstd[:, t:t + 1], ALU.subtract,
                                          ALU.mult).then_inc(s_x, 1)
                    if t >= 2:
                        dve.wait_ge(s_m, t - 1)
                        dve.tensor_reduce(sc[:, 0, t - 2:t - 1], xw[:, t % 2, :], AX.X, ALU.add).then_inc(s_w, 1)
                dve.memset(top[:, :], -3e38).then_inc(s_w, 1)
                dve.wait_ge(s_w, NT + 1)
                link = chain(dve, s_s)
                link(dve.tensor_scalar(sc[:, 0, :], sc[:, 0, :], ab[:, :], None, ALU.add))
                link(dve.tensor_reduce(top[:P, 0:1], sc[:, 0, :], AX.X, ALU.max))
                link(dve.tensor_copy(r0[:, 0:1], gb[:, 0:1]))
                link(dve.tensor_copy(r0[:, 1:2], gb[:, 0:1]))
                dve.wait_ge(s_all, 1)
                link(dve.tensor_scalar(top[:, 1:2], glob[:, :], -1.0, None, ALU.mult))
                dve.wait_ge(s_e, 1)
                dve.tensor_reduce(esum[:, :], sc[:, 1, :], AX.X, ALU.add).then_inc(s_se, 1)
                dve.tensor_scalar(acc[:, :], xa[:, 0, :], sc[:, 1, 0:1], None, ALU.mult).then_inc(s_pa, 1)
                for t in range(1, NT):
                    dve.wait_ge(s_pa, t)
                    dve.scalar_tensor_tensor(acc[:, :], xa[:, t, :], sc[:, 1, t:t + 1], acc[:, :], ALU.mult,
                                             ALU.add).then_inc(s_pa, 1)
                dve.wait_ge(s_pl, 1)
                link(dve.reciprocal(tot[:, :], banks[:, 1, 0:1]))
                link(dve.tensor_scalar(pl[:, :], banks[:, 0, 0:KT], tot[:, :], None, ALU.mult))
                dve.wait_ge(s_gl, 1)
                link(dve.tensor_tensor(r1[:, 0], banks[0:1, 2, 0:EX], gb[:, :], ALU.add))
                link(dve.tensor_reduce(r0[:, 0:1], r1[:, 0], AX.X, ALU.max))
                link(dve.tensor_scalar(r1[:, 1], r1[:, 0], r0[:, 0:1], None, ALU.subtract))
                dve.wait_ge(s_ge, 1)
                link(dve.tensor_reduce(r0[:, 1:2], r1[:, 2], AX.X, ALU.add))
                link(dve.reciprocal(r0[:, 2:3], r0[:, 1:2]))
                link(dve.tensor_scalar(r1[:, 3], r1[:, 2], r0[:, 2:3], None, ALU.mult))
                dve.wait_ge(s_c, 1)
                for j, seen in ((0, r1[:, 3]), (1, r1[:, 4])):
                    best, least = r0[:, 3 + j:4 + j], r0[:, 5:6]
                    link(dve.tensor_reduce(best, seen, AX.X, ALU.max))
                    link(dve.tensor_scalar(r1[:, 5], seen, best, float(EX), ALU.is_lt, ALU.mult))
                    link(dve.tensor_tensor(r1[:, 5], r1[:, 5], iota8[:, :], ALU.add))
                    link(dve.tensor_reduce(least, r1[:, 5], AX.X, ALU.min))
                    link(dve.tensor_copy(chosen[:, j:j + 1], least))
                    if j == 0:
                        link(dve.tensor_scalar(r1[:, 6], iota8[:, :], least, -2.0, ALU.is_equal, ALU.mult))
                        link(dve.tensor_tensor(r1[:, 4], r1[:, 6], r1[:, 3], ALU.add))
                link(dve.tensor_tensor(r0[:, 6:7], r0[:, 3:4], r0[:, 4:5], ALU.add))
                link(dve.tensor_scalar(r0[:, 6:7], r0[:, 6:7], 1e-9, None, ALU.add))
                link(dve.reciprocal(r0[:, 7:8], r0[:, 6:7]))
                link(dve.tensor_scalar(gn[:, :], r0[:, 3:5], r0[:, 7:8], None, ALU.mult))
                dve.sem_inc(s_gb, 1)
                dve.wait_ge(s_gb, 2)
                dve.tensor_copy(gcol[:, :], banks[:P, 3, 0:TOP])

            @block.scalar
            def _(act):
                stats.root(act)
                act.wait_ge(s_s, 5)
                act.activation(sc[:, 1, :], sc[:, 0, :], ACT.Exp, bias=top[:P, 1:2]).then_inc(s_e, 1)
                act.wait_ge(s_s, 10)
                act.activation(r1[:, 2], r1[:, 1], ACT.Exp).then_inc(s_ge, 1)

            @block.tensor
            def _(pe):
                pe.wait_ge(s_c, 1)
                pe.wait_ge(s_e, 1)
                pe.wait_ge(s_pa, NT)
                for c in range(KT):
                    pe.matmul(banks[:, 0, c:c + 1], acc[:, c * 128:(c + 1) * 128], ones[:, 0:1], start=True, stop=True)
                pe.wait_ge(s_se, 1)
                pe.matmul(banks[:, 1, 0:1], ones[:, :], esum[:, :], start=True, stop=True).then_inc(s_pl, 1)
                pe.wait_ge(s_s, 7)
                for c in range(KT):
                    ins = pe.matmul(banks[0:1, 2, 0:EX], pl[:, c:c + 1], gw[:, c, :], start=c == 0, stop=c == KT - 1)
                ins.then_inc(s_gl, 1)
                pe.wait_ge(s_gb, 1)
                pe.matmul(banks[:P, 3, 0:TOP], ones[0:1, 0:P], gn[:, :], start=True, stop=True).then_inc(s_gb, 1)

        FT = TOP * HT
        v1 = [sb(f"v1{a}", [128, KT, FT * 128], F32R) for a in range(2)]
        v2 = [sb(f"v2{a}", [128, FT, D], F32R) for a in range(2)]
        vb = [sb(f"vb{a}", [1, TOP, D], F32R) for a in range(2)]
        b1 = sb("b1", [128, FT], F32)
        one_r = sb("one_r", [1, P + 1], F32R)

        def source(a, j, form, **sizes):
            return lambda e: a[ds(e[j], 1)].rearrange(form, **sizes)

        pieces = []
        for j in range(TOP):
            c = slice(j * HT * 128, (j + 1) * HT * 128)
            pieces.append((source(w1, j, "a (c p) f -> p (a c) f", p=128), v1[0][:, :, c], v1[1][:, :, c]))
        for j in range(TOP):
            c = slice(j * HT, (j + 1) * HT)
            pieces.append((source(w2, j, "a (c p) f -> p (a c) f", p=128), v2[0][:, c, :], v2[1][:, c, :]))
            pieces.append((source(b2, j, "a f -> a f"), vb[0][:, j, :], vb[1][:, j, :]))
        w = Weights(k, sb, "po", pieces, stages=4)
        xt = Normed(k, sb, "pox", x, mean, rstd, ident, 0)
        hf = sb("hf", [128, 2, 2 * P], F32)
        ht = [sb(f"ht{a}", [128, FT, 2, P], F32R) for a in range(2)]
        eo = sb("eo", [P, 2, D], F32)
        s_b1, s_one = sem("b1"), sem("one")
        s_out = sem("out")
        s_h = sem("h")
        s_f = sem("f")
        s_hh, s_hl = sem("hh"), sem("hl")
        s_o = sem("o")
        s_g = sem("g")
        s_y = sem("y")
        block = ctx.enter_context(nc.Block())

        @block.sync
        def _(sp):
            e = [sp.value_load(chosen[0:1, j:j + 1], min_val=0, max_val=EX - 1) for j in range(TOP)]
            for j in range(TOP):
                sp.dma_start(b1[:, j * HT:(j + 1) * HT], b1_cols[ds(e[j], 1)].rearrange("a p f -> (a p) f"))\
                  .then_inc(s_b1, 16)
            w.load(sp, e)
            with sp.Fori(0, NT) as t:
                sp.wait_ge(s_y, TOP * t + TOP + 2)
                sp.dma_start(out[ds(t * P, P), :], flat(x, t)).then_inc(s_out, 16)
            sp.wait_ge(s_out, NT * 16)

        @block.tensor
        def _(pe):
            xt.transposes(pe, 0)
            w.wait(pe, TOP)
            pe.wait_ge(s_one, 1)
            with pe.Fori(0, NP) as i:
                xt.wait(pe, i)
                xt.transposes(pe, i + 1)
                for f in range(FT):
                    pe.wait_ge(s_hl, FT * i + f + 1)
                    product(pe, banks[:, 2 + f % 2, 0:2 * P], v1, xt.parts(), feature_tile(f),
                            range(KT)).then_inc(s_h, 1)
                pe.wait_ge(s_hl, FT * (i + 1) + 2)
                w.wait(pe)
                for n in range(2 * TOP):
                    h, j = divmod(n, TOP)
                    pe.wait_ge(s_g, 2 * TOP * i + n + 1)
                    out = banks[:P, 4 + n % 2, :]
                    product(pe, out, ht, v2, half_of(h), range(j * HT, (j + 1) * HT), last=False)
                    for a in range(2):
                        ins = pe.matmul(out, one_r[:, 0:P], vb[a][:, j, :], start=False, stop=a == 1)
                    ins.then_inc(s_o, 1)

        @block.scalar
        def _(act):
            act.sem_inc(s_g, 2)
            xt.high(act, 0)
            w.high(act)
            act.wait_ge(s_b1, 16 * TOP)
            with act.Fori(0, NP) as i:
                for f in range(FT):
                    act.wait_ge(s_h, FT * i + f + 1)
                    act.wait_ge(s_hl, FT * i + f + 1)
                    act.activation(hf[:, f % 2, :], banks[:, 2 + f % 2, 0:2 * P], ACT.Gelu,
                                   bias=b1[:, f:f + 1]).then_inc(s_f, 1)
                    act.wait_ge(s_f, FT * i + f + 1)
                    act.copy(ht[0][:, f, :, :].rearrange("p h n -> p (h n)"), hf[:, f % 2, :]).then_inc(s_hh, 1)
                xt.high(act, i + 1, s_h, FT * i + FT)
                for n in range(2 * TOP):
                    act.wait_ge(s_o, 2 * TOP * i + n + 1)
                    act.wait_ge(s_y, 2 * TOP * i + n + 1)
                    act.activation(eo[:, n % 2, :], banks[:P, 4 + n % 2, :], ACT.Gelu).then_inc(s_g, 1)

        @block.vector
        def _(dve):
            dve.sem_inc(s_hl, 2)
            dve.sem_inc(s_y, 2)
            dve.memset(one_r[:, :].bitcast(F32), 1.0).then_inc(s_one, 1)
            xt.rows(dve, 0)
            xt.low(dve, 0)
            w.low(dve)
            with dve.Fori(0, NP) as i:
                xt.rows(dve, i + 1)
                for f in range(FT):
                    dve.wait_ge(s_hh, FT * i + f + 1)
                    dve.tensor_tensor(ht[1][:, f, :, :].rearrange("p h n -> p (h n)"), hf[:, f % 2, :],
                                      ht[0][:, f, :, :].bitcast(F32).rearrange("p h n -> p (h n)"),
                                      ALU.subtract).then_inc(s_hl, 1)
                xt.low(dve, i + 1)
                for n in range(2 * TOP):
                    h, j = divmod(n, TOP)
                    t = 2 * i + h
                    dve.wait_ge(s_g, 2 * TOP * i + n + 3)
                    if j:
                        dve.wait_ge(s_y, 2 * TOP * i + n + 2)
                    dve.scalar_tensor_tensor(flat(x, t), eo[:, n % 2, :], gcol[:, j:j + 1], flat(x, t), ALU.mult,
                                             ALU.add).then_inc(s_y, 1)


def graph_transformer(nc, x_in, src, dst, edge_attr, ident_in, mask_in, head_cols, head_rows, sel_in, mean_in,
                      wq, wk, wv, bn_gamma, bn_beta, mix0_wqkv, mix0_wout, mix0_bout,
                      f0_gate, f0_w1, f0_sw1, f0_w2, f0_sw2, f0_b1, f0_b2,
                      gn_wm, gn_wu, gn_bias, gn_gamma, gn_beta,
                      mix1_wqkv, mix1_b, mix1_bq, mix1_wout, mix1_bout, mix1_gamma, mix1_beta,
                      f1_attn_w, f1_attn_b, f1_gate_w, f1_gate_b, f1_w1, f1_b1, f1_w2, f1_b2, out):
    counts_d = nc.dram_tensor("edge_counts", [NT, P, NT, P], U16).ap()
    esum_d = nc.dram_tensor("edge_sums", [NT, P, D], F32).ap()
    with ExitStack() as ctx:
        k = Kernel(nc, ctx)
        ident = k.keep("ident", [128, 128], F32)
        mean = k.keep("mean", [P, NT], F32)
        rstd = k.keep("rstd", [P, NT], F32)
        again = k.keep("again", [P, NT], F32)
        deg = k.keep("deg", [P, NT], F32)
        s_const = k.sem("s_const")

        with ExitStack() as rows:
            x = rows.enter_context(nc.sbuf_tensor("rows_x", [P, NT, D], F32))
            y = rows.enter_context(nc.sbuf_tensor("rows_y", [P, NT, D], F32))
            with ExitStack() as inner:
                def sb(name, shape, dt):
                    return inner.enter_context(nc.sbuf_tensor(name, shape, dt))

                counts = sb("counts", [P, NT, NT, P], U16)
                stats = Stats(k, sb, "st0", x, mean, rstd)
                with nc.Block() as block:
                    @block.sync
                    def _(sp):
                        sp.dma_start(ident[:, :], ident_in).then_inc(s_const, 16)
                        sp.wait_ge(s_const, 16)
                edge_phase(k, src, dst, edge_attr, counts, esum_d, deg, ident, x_in, x, stats)
                attention_phase(k, x, y, mean, rstd, counts, counts_d, ident, wq, wk, wv)
            k.clear()
            mix_phase(k, "mix0", x, y, mean, rstd, ident, mask_in, head_cols, head_rows,
                      mix0_wqkv, None, None, mix0_wout, mix0_bout,
                      norm=(mean_in, bn_gamma, bn_beta))
            x, y = y, x
            experts_phase(k, x, mean, rstd, ident, sel_in, f0_gate, f0_w1, f0_sw1, f0_w2, f0_sw2, f0_b1, f0_b2)
            k.clear()
            mix_phase(k, "mix1", x, y, mean, again, ident, mask_in, head_cols, head_rows,
                      mix1_wqkv, mix1_b, mix1_bq, mix1_wout, mix1_bout,
                      affine=(mix1_gamma, mix1_beta), base=(mean, rstd))
            graph_phase(k, x, y, mean, rstd, ident, deg, counts_d, esum_d, gn_wm, gn_wu, gn_bias, gn_gamma, gn_beta)
            pooled_phase(k, y, mean, rstd, ident, f1_attn_w, f1_attn_b, f1_gate_w, f1_gate_b, f1_w1, f1_b1, f1_w2, f1_b2, out)


def lay_out(i):
    def swap(name, *axes):
        return i[name].transpose(*axes) if axes else i[name].T

    def edges(name, pad):
        a = np.pad(i[name], (0, G * GE - E), constant_values=pad)
        return a.reshape(G * GC, EC).T

    bm, bu = i["L1_gnn_bm"], i["L1_gnn_bu"]
    zero = np.zeros_like(bm)
    return {
        "x": i["x"],
        "src": edges("src", 4095),
        "dst": edges("dst", N),
        "edge_attr": np.pad(i["edge_attr_512"], ((0, G * GE - E), (0, 0))),
        "identity": np.eye(128, dtype=np.float32),
        "head_mask": np.kron(np.eye(2), np.ones((DH, DH))).astype(np.float32),
        "head_cols": np.repeat(np.eye(H, dtype=np.float32), DH, 0).reshape(KT, 128, H).transpose(1, 0, 2),
        "head_rows": np.repeat(np.eye(H, dtype=np.float32), DH, 1).reshape(H, KT, 128),
        "selector": np.repeat(np.eye(8, dtype=np.float32), 128, 1),
        "mean_of_nodes": np.full((128, 128), 1.0 / N, np.float32),
        "wq": i["L0_gnn_Wq"], "wk": i["L0_gnn_Wk"], "wv": i["L0_gnn_Wv"],
        "bn_gamma": i["L0_gnn_bn_gamma"], "bn_beta": i["L0_gnn_bn_beta"],
        "mix0_wqkv": i["L0_mix_w_qkv"], "mix0_wout": i["L0_mix_w_out"], "mix0_bout": i["L0_mix_b_out"],
        "f0_gate": swap("L0_ffn_gate_w"),
        "f0_w1": swap("L0_ffn_w1", 1, 0, 2).reshape(D, -1),
        "f0_sw1": i["L0_ffn_sw1"], "f0_w2": i["L0_ffn_w2"], "f0_sw2": i["L0_ffn_sw2"],
        "f0_b1": np.concatenate([swap("L0_ffn_b1"), i["L0_ffn_sb1"].reshape(4, 128).T], 1),
        "f0_b2": np.concatenate([i["L0_ffn_b2"], i["L0_ffn_sb2"][None]]),
        "gn_wm": swap("L1_gnn_Wm"), "gn_wu": swap("L1_gnn_Wu"),
        "gn_bias": np.stack([np.stack([bm, zero]), np.stack([zero, bu])]),
        "gn_gamma": i["L1_gnn_gamma"], "gn_beta": i["L1_gnn_beta"],
        "mix1_wqkv": swap("L1_mix_qkv_w"), "mix1_b": i["L1_mix_qkv_b"],
        "mix1_bq": i["L1_mix_qkv_b"][:D].reshape(4, 128).T,
        "mix1_wout": swap("L1_mix_out_w"), "mix1_bout": i["L1_mix_out_b"],
        "mix1_gamma": i["L1_mix_ln_gamma"], "mix1_beta": i["L1_mix_ln_beta"],
        "f1_attn_w": i["L1_ffn_attn_w"].reshape(D), "f1_attn_b": i["L1_ffn_attn_b"],
        "f1_gate_w": i["L1_ffn_gate_w"], "f1_gate_b": i["L1_ffn_gate_b"],
        "f1_w1": i["L1_ffn_w1"], "f1_b1": swap("L1_ffn_b1").reshape(2, 128, 8).transpose(2, 1, 0),
        "f1_w2": i["L1_ffn_w2"], "f1_b2": i["L1_ffn_b2"],
    }


def kernel(**inputs):
    import concourse.bacc as _bacc
    from concourse.bass_utils import run_bass_kernel_spmd as _run

    nc = _bacc.Bacc("TRN2", target_bir_lowering=False, num_devices=1)
    arrays, args = {}, []
    for name, a in lay_out({name: np.asarray(a) for name, a in inputs.items()}).items():
        arrays[f"in_{name}_dram"] = np.ascontiguousarray(a)
        args.append(nc.dram_tensor(f"in_{name}_dram", a.shape, mybir.dt.from_np(a.dtype), kind="ExternalInput").ap())
    args.append(nc.dram_tensor("out_dram", (N, D), F32, kind="ExternalOutput").ap())
    graph_transformer(nc, *args)
    return _run(nc, [arrays], core_ids=[0]).results[0]["out_dram"]
```
